# Optimizing a Trainium2 kernel written in Bass

```python
import numpy as np
import jax
import jax.numpy as jnp

def _softmax(x, axis=-1):
    return jax.nn.softmax(x, axis=axis)

def _gelu(x):
    return jax.nn.gelu(x, approximate=True)

def _silu(x):
    return jax.nn.silu(x)

def _sigmoid(x):
    return jax.nn.sigmoid(x)

def _layernorm(x, axis=-1, eps=1e-05):
    m = jnp.mean(x, axis=axis, keepdims=True)
    v = jnp.var(x, axis=axis, keepdims=True)
    return (x - m) / jnp.sqrt(v + eps)

def _scatter_add(tgt, idx, src, axis=0):
    return tgt.at[idx].add(src)

def _segment_sum(src, seg, n):
    return jax.ops.segment_sum(src, seg, n)
kernel_name = 'mk_conv_seq_d4_conv_nchw256_r4_002b4e'

def setup_inputs(seed: int=0):
    np.random.seed(seed)
    _w = jnp.asarray

    def _rec_inputs():
        import jax
        import jax.numpy as jnp
        _gk = jax.random.key(seed)
        x = -0.0003482 + 1 * jax.random.normal(jax.random.fold_in(_gk, 1), (8, 64, 24, 24), jnp.float32)
        return x
    x = _rec_inputs()

    def _L0_conv_setup():
        import jax, jax.numpy as jnp
        import numpy as np
        KK = 9
        PAD = 1
        EPS = 1e-05

        def _conv2d(x, w, b):
            y = jax.lax.conv_general_dilated(x, w, window_strides=(1, 1), padding=((PAD, PAD), (PAD, PAD)), dimension_numbers=('NCHW', 'OIHW', 'NCHW'))
            return y + b[None, :, None, None]

        def _bilinear_sample_one(img, py, px):
            C, H, W = img.shape
            y0 = jnp.floor(py).astype(jnp.int32)
            x0 = jnp.floor(px).astype(jnp.int32)
            wy = py - y0
            wx = px - x0

            def g(yi, xi):
                ok = ((yi >= 0) & (yi < H) & (xi >= 0) & (xi < W)).astype(img.dtype)
                v = img[:, jnp.clip(yi, 0, H - 1), jnp.clip(xi, 0, W - 1)]
                return v * ok[None]
            v00 = g(y0, x0)
            v01 = g(y0, x0 + 1)
            v10 = g(y0 + 1, x0)
            v11 = g(y0 + 1, x0 + 1)
            return v00 * (1 - wy) * (1 - wx) + v01 * (1 - wy) * wx + v10 * wy * (1 - wx) + v11 * wy * wx
        key = jax.random.key(seed)
        ks = jax.random.split(key, 8)
        B, C, H, W = (8, 64, 24, 24)
        O = 64
        x = jax.random.normal(ks[0], (B, C, H, W), dtype=jnp.float32)
        w_off = jax.random.normal(ks[1], (3 * KK, C, 3, 3), dtype=jnp.float32) * 0.01
        b_off = jnp.zeros((3 * KK,), dtype=jnp.float32)
        w_dcn = jax.random.normal(ks[2], (O, C, 3, 3), dtype=jnp.float32) * (1.0 / np.sqrt(C * KK))
        b_dcn = jnp.zeros((O,), dtype=jnp.float32)
        gamma = jnp.ones((O,), dtype=jnp.float32)
        beta = jnp.zeros((O,), dtype=jnp.float32)
        running_mean = jax.random.normal(ks[3], (O,), dtype=jnp.float32) * 0.1
        running_var = jax.random.uniform(ks[4], (O,), dtype=jnp.float32, minval=0.5, maxval=1.5)
        return {'x': x, 'w_off': w_off, 'b_off': b_off, 'w_dcn': w_dcn, 'b_dcn': b_dcn, 'gamma': gamma, 'beta': beta, 'running_mean': running_mean, 'running_var': running_var}
    _L0_conv_all = _L0_conv_setup()
    _L0_conv_in = {k: v for k, v in _L0_conv_all.items() if k in ('w_off', 'b_off', 'w_dcn', 'b_dcn', 'gamma', 'beta', 'running_mean', 'running_var')}
    del _L0_conv_all

    def _L1_conv_setup():
        import jax, jax.numpy as jnp
        import numpy as np
        EPS = 1e-05

        def _conv3x3(x, w, b):
            y = jax.lax.conv_general_dilated(x, w, window_strides=(1, 1), padding=((1, 1), (1, 1)), dimension_numbers=('NCHW', 'OIHW', 'NCHW'))
            return y + b[None, :, None, None]

        def _bilinear_gather(x, py, px):
            B, C, H, W = x.shape
            Kk = py.shape[1]
            y0 = jnp.floor(py)
            x0 = jnp.floor(px)
            ly = py - y0
            lx = px - x0
            y0i = y0.astype(jnp.int32)
            x0i = x0.astype(jnp.int32)
            xf = x.reshape(B, C, H * W)

            def gather(yi, xi):
                valid = (yi >= 0) & (yi < H) & (xi >= 0) & (xi < W)
                idx = (jnp.clip(yi, 0, H - 1) * W + jnp.clip(xi, 0, W - 1)).reshape(B, -1)
                g = jax.vmap(lambda xb, ib: xb[:, ib])(xf, idx).reshape(B, C, Kk, H, W)
                return g * valid[:, None].astype(x.dtype)
            v00 = gather(y0i, x0i)
            v01 = gather(y0i, x0i + 1)
            v10 = gather(y0i + 1, x0i)
            v11 = gather(y0i + 1, x0i + 1)
            ly = ly[:, None]
            lx = lx[:, None]
            return v00 * (1 - ly) * (1 - lx) + v01 * (1 - ly) * lx + v10 * ly * (1 - lx) + v11 * ly * lx

        def _shift_forward(x, w_off, b_off, w_conv, b_conv, gamma, beta, run_mean, run_var):
            B, C, H, W = x.shape
            om = _conv3x3(x, w_off, b_off)
            dy = om[:, 0:18:2]
            dx = om[:, 1:18:2]
            mask = jax.nn.sigmoid(om[:, 18:27])
            kk = jnp.arange(3, dtype=x.dtype) - 1.0
            ky = jnp.repeat(kk, 3)
            kx = jnp.tile(kk, 3)
            hh = jnp.arange(H, dtype=x.dtype)
            ww = jnp.arange(W, dtype=x.dtype)
            py = hh[None, None, :, None] + ky[None, :, None, None] + dy
            px = ww[None, None, None, :] + kx[None, :, None, None] + dx
            s = _bilinear_gather(x, py, px) * mask[:, None]
            Co = w_conv.shape[0]
            y = jnp.einsum('bckhw,ock->bohw', s, w_conv.reshape(Co, C, 9))
            y = y + b_conv[None, :, None, None]
            inv = jax.lax.rsqrt(run_var + EPS)
            y = (y - run_mean[None, :, None, None]) * (inv * gamma)[None, :, None, None] + beta[None, :, None, None]
            y = jax.nn.relu(y)
            return x + y
        key = jax.random.key(seed)
        ks = jax.random.split(key, 3)
        B, C, H, W = (2, 64, 24, 24)
        x = jax.random.normal(ks[0], (B, C, H, W), dtype=jnp.float32)
        w_off = jax.random.normal(ks[1], (27, C, 3, 3), dtype=jnp.float32) * 0.01
        b_off = jnp.zeros((27,), dtype=jnp.float32)
        w_conv = jax.random.normal(ks[2], (C, C, 3, 3), dtype=jnp.float32) * 0.02
        b_conv = jnp.zeros((C,), dtype=jnp.float32)
        gamma = jnp.ones((C,), dtype=jnp.float32)
        beta = jnp.zeros((C,), dtype=jnp.float32)
        run_mean = jnp.zeros((C,), dtype=jnp.float32)
        run_var = jnp.ones((C,), dtype=jnp.float32)
        return {'x': x, 'w_off': w_off, 'b_off': b_off, 'w_conv': w_conv, 'b_conv': b_conv, 'gamma': gamma, 'beta': beta, 'run_mean': run_mean, 'run_var': run_var}
    _L1_conv_all = _L1_conv_setup()
    _L1_conv_in = {k: v for k, v in _L1_conv_all.items() if k in ('w_off', 'b_off', 'w_conv', 'b_conv', 'gamma', 'beta', 'run_mean', 'run_var')}
    del _L1_conv_all

    def _L2_conv_setup():
        import jax, jax.numpy as jnp
        import numpy as np

        def _conv3x3(x, w):
            return jax.lax.conv_general_dilated(x, w, window_strides=(1, 1), padding=((1, 1), (1, 1)), dimension_numbers=('NCHW', 'OIHW', 'NCHW'))

        def _conv1x1(x, w):
            return jax.lax.conv_general_dilated(x, w, window_strides=(1, 1), padding=((0, 0), (0, 0)), dimension_numbers=('NCHW', 'OIHW', 'NCHW'))
        key = jax.random.key(seed)
        k_x, k_w1, k_w2, k_wm = jax.random.split(key, 4)
        N, C, H, W = (16, 64, 16, 16)
        fan = C * 9
        x = jax.random.normal(k_x, (N, C, H, W), dtype=jnp.float32)
        w1 = jax.random.normal(k_w1, (C, C, 3, 3), dtype=jnp.float32) * (2.0 / fan) ** 0.5
        w2 = jax.random.normal(k_w2, (C, C, 3, 3), dtype=jnp.float32) * (2.0 / fan) ** 0.5
        w_mask = jax.random.normal(k_wm, (1, C, 1, 1), dtype=jnp.float32) * (1.0 / C) ** 0.5
        b_mask = jnp.zeros((1,), dtype=jnp.float32)
        return {'x': x, 'w1': w1, 'w2': w2, 'w_mask': w_mask, 'b_mask': b_mask}
    _L2_conv_all = _L2_conv_setup()
    _L2_conv_in = {k: v for k, v in _L2_conv_all.items() if k in ('w1', 'w2', 'w_mask', 'b_mask')}
    del _L2_conv_all

    def _L3_conv_setup():
        import jax, jax.numpy as jnp
        import numpy as np
        B, C, H, W = (16, 64, 24, 24)
        CQ = C // 8
        CM = C // 2

        def conv1x1(x, w, b=None):
            y = jnp.einsum('bchw,oc->bohw', x, w)
            if b is not None:
                y = y + b[None, :, None, None]
            return y

        def cross_attention(x, wq, bq, wk, bk, wv, bv, gamma):
            b_, c_, h_, w_ = x.shape
            q = conv1x1(x, wq, bq)
            k = conv1x1(x, wk, bk)
            v = conv1x1(x, wv, bv)
            e_h = jnp.einsum('bchw,bckw->bhwk', q, k)
            diag = jnp.eye(h_, dtype=bool)[None, :, None, :]
            e_h = jnp.where(diag, -jnp.inf, e_h)
            e_w = jnp.einsum('bchw,bchv->bhwv', q, k)
            att = jax.nn.softmax(jnp.concatenate([e_h, e_w], axis=3), axis=3)
            a_h, a_w = (att[..., :h_], att[..., h_:])
            out_h = jnp.einsum('bckw,bhwk->bchw', v, a_h)
            out_w = jnp.einsum('bchv,bhwv->bchw', v, a_w)
            return gamma * (out_h + out_w) + x

        def spatial_weighted(x, w_q_right, w_v_right, w_up, b_up):
            b_, _, h_, w_ = x.shape
            inp = conv1x1(x, w_v_right).reshape(b_, CM, h_ * w_)
            mask = conv1x1(x, w_q_right).reshape(b_, 1, h_ * w_)
            mask = jax.nn.softmax(mask, axis=2)
            ctx = jnp.einsum('bcn,bon->bco', inp, mask)
            ctx = jnp.einsum('bci,oc->boi', ctx, w_up) + b_up[None, :, None]
            mask_ch = jax.nn.sigmoid(ctx)[..., None]
            return x * mask_ch

        def channel_weighted(x, w_q_left, w_v_left):
            b_, _, h_, w_ = x.shape
            g = conv1x1(x, w_q_left)
            avg = jnp.mean(g, axis=(2, 3))
            theta = conv1x1(x, w_v_left).reshape(b_, CM, h_ * w_)
            ctx = jnp.einsum('bc,bcn->bn', avg, theta)
            ctx = jax.nn.softmax(ctx, axis=1).reshape(b_, 1, h_, w_)
            return x * jax.nn.sigmoid(ctx)
        key = jax.random.key(seed)
        ks = jax.random.split(key, 16)
        s = lambda fan_in: (2.0 / fan_in) ** 0.5
        inp = {'x': jax.random.normal(ks[0], (B, C, H, W), jnp.float32), 'w_q_right': jax.random.normal(ks[1], (1, C), jnp.float32) * s(C), 'w_v_right': jax.random.normal(ks[2], (CM, C), jnp.float32) * s(C), 'w_up': jax.random.normal(ks[3], (C, CM), jnp.float32) * s(CM), 'b_up': jnp.zeros((C,), jnp.float32), 'w_q_left': jax.random.normal(ks[4], (CM, C), jnp.float32) * s(C), 'w_v_left': jax.random.normal(ks[5], (CM, C), jnp.float32) * s(C), 'cr_wq': jax.random.normal(ks[6], (CQ, C), jnp.float32) * s(C), 'cr_bq': jnp.zeros((CQ,), jnp.float32), 'cr_wk': jax.random.normal(ks[7], (CQ, C), jnp.float32) * s(C), 'cr_bk': jnp.zeros((CQ,), jnp.float32), 'cr_wv': jax.random.normal(ks[8], (C, C), jnp.float32) * s(C), 'cr_bv': jnp.zeros((C,), jnp.float32), 'gamma': jax.random.normal(ks[9], (1,), jnp.float32) * 0.1}
        return inp
    _L3_conv_all = _L3_conv_setup()
    _L3_conv_in = {k: v for k, v in _L3_conv_all.items() if k in ('w_q_right', 'w_v_right', 'w_up', 'b_up', 'w_q_left', 'w_v_left', 'cr_wq', 'cr_bq', 'cr_wk', 'cr_bk', 'cr_wv', 'cr_bv', 'gamma')}
    del _L3_conv_all
    return {'x': x, 'L0_conv_w_off': _L0_conv_in['w_off'], 'L0_conv_b_off': _L0_conv_in['b_off'], 'L0_conv_w_dcn': _L0_conv_in['w_dcn'], 'L0_conv_b_dcn': _L0_conv_in['b_dcn'], 'L0_conv_gamma': _L0_conv_in['gamma'], 'L0_conv_beta': _L0_conv_in['beta'], 'L0_conv_running_mean': _L0_conv_in['running_mean'], 'L0_conv_running_var': _L0_conv_in['running_var'], 'L1_conv_w_off': _L1_conv_in['w_off'], 'L1_conv_b_off': _L1_conv_in['b_off'], 'L1_conv_w_conv': _L1_conv_in['w_conv'], 'L1_conv_b_conv': _L1_conv_in['b_conv'], 'L1_conv_gamma': _L1_conv_in['gamma'], 'L1_conv_beta': _L1_conv_in['beta'], 'L1_conv_run_mean': _L1_conv_in['run_mean'], 'L1_conv_run_var': _L1_conv_in['run_var'], 'L2_conv_w1': _L2_conv_in['w1'], 'L2_conv_w2': _L2_conv_in['w2'], 'L2_conv_w_mask': _L2_conv_in['w_mask'], 'L2_conv_b_mask': _L2_conv_in['b_mask'], 'L3_conv_w_q_right': _L3_conv_in['w_q_right'], 'L3_conv_w_v_right': _L3_conv_in['w_v_right'], 'L3_conv_w_up': _L3_conv_in['w_up'], 'L3_conv_b_up': _L3_conv_in['b_up'], 'L3_conv_w_q_left': _L3_conv_in['w_q_left'], 'L3_conv_w_v_left': _L3_conv_in['w_v_left'], 'L3_conv_cr_wq': _L3_conv_in['cr_wq'], 'L3_conv_cr_bq': _L3_conv_in['cr_bq'], 'L3_conv_cr_wk': _L3_conv_in['cr_wk'], 'L3_conv_cr_bk': _L3_conv_in['cr_bk'], 'L3_conv_cr_wv': _L3_conv_in['cr_wv'], 'L3_conv_cr_bv': _L3_conv_in['cr_bv'], 'L3_conv_gamma': _L3_conv_in['gamma']}

def reference(x, L0_conv_w_off, L0_conv_b_off, L0_conv_w_dcn, L0_conv_b_dcn, L0_conv_gamma, L0_conv_beta, L0_conv_running_mean, L0_conv_running_var, L1_conv_w_off, L1_conv_b_off, L1_conv_w_conv, L1_conv_b_conv, L1_conv_gamma, L1_conv_beta, L1_conv_run_mean, L1_conv_run_var, L2_conv_w1, L2_conv_w2, L2_conv_w_mask, L2_conv_b_mask, L3_conv_w_q_right, L3_conv_w_v_right, L3_conv_w_up, L3_conv_b_up, L3_conv_w_q_left, L3_conv_w_v_left, L3_conv_cr_wq, L3_conv_cr_bq, L3_conv_cr_wk, L3_conv_cr_bk, L3_conv_cr_wv, L3_conv_cr_bv, L3_conv_gamma):
    import jax
    import jax.numpy as jnp

    def _L0_conv_ref(x, w_off, b_off, w_dcn, b_dcn, gamma, beta, running_mean, running_var):
        import jax, jax.numpy as jnp
        import numpy as np
        KK = 9
        PAD = 1
        EPS = 1e-05

        def _conv2d(x, w, b):
            y = jax.lax.conv_general_dilated(x, w, window_strides=(1, 1), padding=((PAD, PAD), (PAD, PAD)), dimension_numbers=('NCHW', 'OIHW', 'NCHW'))
            return y + b[None, :, None, None]

        def _bilinear_sample_one(img, py, px):
            C, H, W = img.shape
            y0 = jnp.floor(py).astype(jnp.int32)
            x0 = jnp.floor(px).astype(jnp.int32)
            wy = py - y0
            wx = px - x0

            def g(yi, xi):
                ok = ((yi >= 0) & (yi < H) & (xi >= 0) & (xi < W)).astype(img.dtype)
                v = img[:, jnp.clip(yi, 0, H - 1), jnp.clip(xi, 0, W - 1)]
                return v * ok[None]
            v00 = g(y0, x0)
            v01 = g(y0, x0 + 1)
            v10 = g(y0 + 1, x0)
            v11 = g(y0 + 1, x0 + 1)
            return v00 * (1 - wy) * (1 - wx) + v01 * (1 - wy) * wx + v10 * wy * (1 - wx) + v11 * wy * wx
        B, C, H, W = x.shape
        O = w_dcn.shape[0]
        om = _conv2d(x, w_off, b_off)
        offset = om[:, :2 * KK]
        mask = jax.nn.sigmoid(om[:, 2 * KK:])
        off_y = offset[:, 0::2]
        off_x = offset[:, 1::2]
        ky, kx = jnp.meshgrid(jnp.arange(3), jnp.arange(3), indexing='ij')
        ky = ky.reshape(KK).astype(x.dtype)
        kx = kx.reshape(KK).astype(x.dtype)
        hh = jnp.arange(H, dtype=x.dtype)
        ww = jnp.arange(W, dtype=x.dtype)
        py = off_y + hh[None, None, :, None] + ky[None, :, None, None] - PAD
        px = off_x + ww[None, None, None, :] + kx[None, :, None, None] - PAD
        sampled = jax.vmap(_bilinear_sample_one)(x, py, px)
        sampled = sampled * mask[:, None]
        out = jnp.einsum('bckhw,ock->bohw', sampled, w_dcn.reshape(O, C, KK))
        out = out + b_dcn[None, :, None, None]
        inv = jax.lax.rsqrt(running_var + EPS)
        out = (out - running_mean[None, :, None, None]) * (gamma * inv)[None, :, None, None]
        out = out + beta[None, :, None, None]
        return jax.nn.relu(out)

    def _L1_conv_ref(x, w_off, b_off, w_conv, b_conv, gamma, beta, run_mean, run_var):
        import jax, jax.numpy as jnp
        import numpy as np
        EPS = 1e-05

        def _conv3x3(x, w, b):
            y = jax.lax.conv_general_dilated(x, w, window_strides=(1, 1), padding=((1, 1), (1, 1)), dimension_numbers=('NCHW', 'OIHW', 'NCHW'))
            return y + b[None, :, None, None]

        def _bilinear_gather(x, py, px):
            B, C, H, W = x.shape
            Kk = py.shape[1]
            y0 = jnp.floor(py)
            x0 = jnp.floor(px)
            ly = py - y0
            lx = px - x0
            y0i = y0.astype(jnp.int32)
            x0i = x0.astype(jnp.int32)
            xf = x.reshape(B, C, H * W)

            def gather(yi, xi):
                valid = (yi >= 0) & (yi < H) & (xi >= 0) & (xi < W)
                idx = (jnp.clip(yi, 0, H - 1) * W + jnp.clip(xi, 0, W - 1)).reshape(B, -1)
                g = jax.vmap(lambda xb, ib: xb[:, ib])(xf, idx).reshape(B, C, Kk, H, W)
                return g * valid[:, None].astype(x.dtype)
            v00 = gather(y0i, x0i)
            v01 = gather(y0i, x0i + 1)
            v10 = gather(y0i + 1, x0i)
            v11 = gather(y0i + 1, x0i + 1)
            ly = ly[:, None]
            lx = lx[:, None]
            return v00 * (1 - ly) * (1 - lx) + v01 * (1 - ly) * lx + v10 * ly * (1 - lx) + v11 * ly * lx

        def _shift_forward(x, w_off, b_off, w_conv, b_conv, gamma, beta, run_mean, run_var):
            B, C, H, W = x.shape
            om = _conv3x3(x, w_off, b_off)
            dy = om[:, 0:18:2]
            dx = om[:, 1:18:2]
            mask = jax.nn.sigmoid(om[:, 18:27])
            kk = jnp.arange(3, dtype=x.dtype) - 1.0
            ky = jnp.repeat(kk, 3)
            kx = jnp.tile(kk, 3)
            hh = jnp.arange(H, dtype=x.dtype)
            ww = jnp.arange(W, dtype=x.dtype)
            py = hh[None, None, :, None] + ky[None, :, None, None] + dy
            px = ww[None, None, None, :] + kx[None, :, None, None] + dx
            s = _bilinear_gather(x, py, px) * mask[:, None]
            Co = w_conv.shape[0]
            y = jnp.einsum('bckhw,ock->bohw', s, w_conv.reshape(Co, C, 9))
            y = y + b_conv[None, :, None, None]
            inv = jax.lax.rsqrt(run_var + EPS)
            y = (y - run_mean[None, :, None, None]) * (inv * gamma)[None, :, None, None] + beta[None, :, None, None]
            y = jax.nn.relu(y)
            return x + y
        return _shift_forward(x, w_off, b_off, w_conv, b_conv, gamma, beta, run_mean, run_var)

    def _L2_conv_ref(x, w1, w2, w_mask, b_mask):
        import jax, jax.numpy as jnp
        import numpy as np

        def _conv3x3(x, w):
            return jax.lax.conv_general_dilated(x, w, window_strides=(1, 1), padding=((1, 1), (1, 1)), dimension_numbers=('NCHW', 'OIHW', 'NCHW'))

        def _conv1x1(x, w):
            return jax.lax.conv_general_dilated(x, w, window_strides=(1, 1), padding=((0, 0), (0, 0)), dimension_numbers=('NCHW', 'OIHW', 'NCHW'))
        logits = _conv1x1(x, w_mask) + b_mask[None, :, None, None]
        hard = (logits > 0).astype(x.dtype)
        mask = logits + jax.lax.stop_gradient(hard - logits)
        mask_dilate = jax.lax.reduce_window(mask, -jnp.inf, jax.lax.max, (1, 1, 3, 3), (1, 1, 1, 1), 'SAME')
        h = jax.nn.relu(_conv3x3(x, w1) * mask_dilate)
        h = jax.nn.relu(_conv3x3(h, w2) * mask)
        out = x + h * mask
        return out

    def _L3_conv_ref(x, w_q_right, w_v_right, w_up, b_up, w_q_left, w_v_left, cr_wq, cr_bq, cr_wk, cr_bk, cr_wv, cr_bv, gamma):
        import jax, jax.numpy as jnp
        import numpy as np
        B, C, H, W = (16, 64, 24, 24)
        CQ = C // 8
        CM = C // 2

        def conv1x1(x, w, b=None):
            y = jnp.einsum('bchw,oc->bohw', x, w)
            if b is not None:
                y = y + b[None, :, None, None]
            return y

        def cross_attention(x, wq, bq, wk, bk, wv, bv, gamma):
            b_, c_, h_, w_ = x.shape
            q = conv1x1(x, wq, bq)
            k = conv1x1(x, wk, bk)
            v = conv1x1(x, wv, bv)
            e_h = jnp.einsum('bchw,bckw->bhwk', q, k)
            diag = jnp.eye(h_, dtype=bool)[None, :, None, :]
            e_h = jnp.where(diag, -jnp.inf, e_h)
            e_w = jnp.einsum('bchw,bchv->bhwv', q, k)
            att = jax.nn.softmax(jnp.concatenate([e_h, e_w], axis=3), axis=3)
            a_h, a_w = (att[..., :h_], att[..., h_:])
            out_h = jnp.einsum('bckw,bhwk->bchw', v, a_h)
            out_w = jnp.einsum('bchv,bhwv->bchw', v, a_w)
            return gamma * (out_h + out_w) + x

        def spatial_weighted(x, w_q_right, w_v_right, w_up, b_up):
            b_, _, h_, w_ = x.shape
            inp = conv1x1(x, w_v_right).reshape(b_, CM, h_ * w_)
            mask = conv1x1(x, w_q_right).reshape(b_, 1, h_ * w_)
            mask = jax.nn.softmax(mask, axis=2)
            ctx = jnp.einsum('bcn,bon->bco', inp, mask)
            ctx = jnp.einsum('bci,oc->boi', ctx, w_up) + b_up[None, :, None]
            mask_ch = jax.nn.sigmoid(ctx)[..., None]
            return x * mask_ch

        def channel_weighted(x, w_q_left, w_v_left):
            b_, _, h_, w_ = x.shape
            g = conv1x1(x, w_q_left)
            avg = jnp.mean(g, axis=(2, 3))
            theta = conv1x1(x, w_v_left).reshape(b_, CM, h_ * w_)
            ctx = jnp.einsum('bc,bcn->bn', avg, theta)
            ctx = jax.nn.softmax(ctx, axis=1).reshape(b_, 1, h_, w_)
            return x * jax.nn.sigmoid(ctx)
        cross = lambda t: cross_attention(t, cr_wq, cr_bq, cr_wk, cr_bk, cr_wv, cr_bv, gamma)
        ctx_channel = cross(spatial_weighted(x, w_q_right, w_v_right, w_up, b_up))
        ctx_spatial = cross(channel_weighted(x, w_q_left, w_v_left))
        return cross(ctx_spatial + ctx_channel)

    def _gn(v, G=32, eps=1e-05):
        B_, C_, H_, W_ = v.shape
        g = v.reshape(B_, G, C_ // G, H_, W_)
        m = jnp.mean(g, axis=(2, 3, 4), keepdims=True)
        s = jnp.var(g, axis=(2, 3, 4), keepdims=True)
        return ((g - m) / jnp.sqrt(s + eps)).reshape(v.shape)

    def _ln_c(v, eps=1e-06):
        m = jnp.mean(v, axis=1, keepdims=True)
        s = jnp.var(v, axis=1, keepdims=True)
        return (v - m) / jnp.sqrt(s + eps)

    def _ln_t(v, eps=1e-05):
        m = jnp.mean(v, axis=-1, keepdims=True)
        s = jnp.var(v, axis=-1, keepdims=True)
        return (v - m) / jnp.sqrt(s + eps)

    def _to_tokens(v):
        B_, C_, H_, W_ = v.shape
        return v.reshape(B_, C_, H_ * W_).transpose(0, 2, 1)

    def _from_tokens(t, like):
        B_, C_, H_, W_ = like.shape
        return t.transpose(0, 2, 1).reshape(B_, C_, H_, W_)
    x = _L0_conv_ref(x, L0_conv_w_off, L0_conv_b_off, L0_conv_w_dcn, L0_conv_b_dcn, L0_conv_gamma, L0_conv_beta, L0_conv_running_mean, L0_conv_running_var)
    x = _L1_conv_ref(x, L1_conv_w_off, L1_conv_b_off, L1_conv_w_conv, L1_conv_b_conv, L1_conv_gamma, L1_conv_beta, L1_conv_run_mean, L1_conv_run_var)
    x = _L2_conv_ref(x, L2_conv_w1, L2_conv_w2, L2_conv_w_mask, L2_conv_b_mask)
    x = _L3_conv_ref(x, L3_conv_w_q_right, L3_conv_w_v_right, L3_conv_w_up, L3_conv_b_up, L3_conv_w_q_left, L3_conv_w_v_left, L3_conv_cr_wq, L3_conv_cr_bq, L3_conv_cr_wk, L3_conv_cr_bk, L3_conv_cr_wv, L3_conv_cr_bv, L3_conv_gamma)
    return x

_drawn_inputs = setup_inputs


def setup_inputs(seed=0):
    import zlib

    import numpy as np

    out = dict(_drawn_inputs(seed))
    spreads = {'L0_conv_b_off': (0.0, 0.1),
     'L0_conv_b_dcn': (0.0, 0.1),
     'L0_conv_gamma': (1.0, 0.2),
     'L0_conv_beta': (0.0, 0.1),
     'L1_conv_b_off': (0.0, 0.1),
     'L1_conv_b_conv': (0.0, 0.1),
     'L1_conv_gamma': (1.0, 0.2),
     'L1_conv_beta': (0.0, 0.1),
     'L1_conv_run_mean': (0.0, 0.1),
     'L1_conv_run_var': (1.0, 0.538),
     'L3_conv_b_up': (0.0, 0.319),
     'L3_conv_cr_bq': (0.0, 2.0),
     'L3_conv_cr_bk': (0.0, 2.0),
     'L3_conv_cr_bv': (0.0, 0.8)}
    factors = {'L3_conv_w_q_right': 8.0,
     'L3_conv_w_q_left': 40.675,
     'L3_conv_w_v_left': 34.419,
     'L3_conv_cr_wq': 8.0,
     'L3_conv_cr_wk': 8.0,
     'L3_conv_cr_wv': 3.479}
    for name, (base, spread) in spreads.items():
        noise = np.random.default_rng([zlib.crc32(name.encode()), seed]).standard_normal(out[name].shape)
        drawn = base * np.exp(spread * noise) if base else spread * noise
        out[name] = jnp.asarray(drawn.astype(out[name].dtype))
    for name, factor in factors.items():
        out[name] = (out[name] * factor).astype(out[name].dtype)
    return out
```

```python
from contextlib import ExitStack

import numpy as np

import concourse.bass as bass
from concourse import mybir

ALU = mybir.AluOpType
ACT = mybir.ActivationFunctionType
AX = mybir.AxisListType.X
F32 = mybir.dt.float32
F16 = mybir.dt.float16

B, C, H, W = 8, 64, 24, 24
HW = H * W
PAIRS = B // 2
HP, WP = H + 2, W + 2
HALF = HW // 2
HR = H // 2
TAPS = 9
EPS = 1e-5
T0 = 5
TILE_ROWS = (T0 * H, (TAPS - T0) * H)
CR = 5
CHUNKS = -(-H // CR)
Y_ROWS = 21
SCALE16 = 1024.0
REACH = 2
SEG = 256
BLOCK_ROWS = 9
G = 4
NG = H // G
GP = G * W
CQ = 8
CM = 32
MASKED = -1e30


def chunk_rows(c):
    return min(CR, H - c * CR)


def blocks_of(c, ky, narrow):
    first, last = 0, H - 1
    if narrow:
        shift = ky - 1
        first = max(0, c * CR - REACH - shift)
        last = min(H - 1, c * CR + chunk_rows(c) - 1 + REACH - shift)
    return [(r, min(r + BLOCK_ROWS, last + 1)) for r in range(first, last + 1, BLOCK_ROWS)]


class Signal:

    def __init__(self, nc, ctx, name, per_pair, primed=False):
        self.sem = ctx.enter_context(nc.semaphore(name))
        self.per_pair = per_pair
        self.primed = int(primed)

    def __call__(self, i, k):
        assert 1 - self.primed <= k <= self.per_pair, k
        return self.sem, i * self.per_pair + (k + self.primed)


class Ring:

    def __init__(self, nc, ctx, name, tiles, items):
        n = len(tiles)
        self.tiles = tiles
        self.read = {item: (signal, k) for item, signal, k in items}
        self.place = {item: (u % n, u // n + 1) for u, (item, _, _) in enumerate(items)}
        self.before = {item: items[u - n][0] if u >= n else None for u, (item, _, _) in enumerate(items)}
        self.last = {u % n: item for u, (item, _, _) in enumerate(items)}
        assert len(self.place) == len(items)
        self.full = [Signal(nc, ctx, f"{name}{t}_full", len(range(t, len(items), n))) for t in range(n)]

    def tile(self, item):
        return self.tiles[self.place[item][0]]

    def filled(self, i, item):
        slot, n = self.place[item]
        return self.full[slot](i, n)

    def emptied(self, i, item):
        signal, k = self.read[item]
        return signal(i, k)

    def may_fill(self, i, item):
        if self.before[item] is None:
            return self.read[self.last[self.place[item][0]]][0](i, 0)
        return self.emptied(i, self.before[item])

    def full_sem(self, item):
        return self.full[self.place[item][0]].sem


def groups():
    return [(c, ky, b) for ky in range(3) for c in range(CHUNKS) for b in range(len(blocks_of(c, ky, NARROW)))]


NARROW = False


def build(nc, a, out):
    ctx = ExitStack()
    with ctx:
        def sb(name, shape, dt=F32):
            return ctx.enter_context(nc.sbuf_tensor(name, shape, dt))

        primed = []

        def sig(name, per_pair, reused=False):
            signal = Signal(nc, ctx, name, per_pair, primed=reused)
            if reused:
                primed.append(signal)
            return signal

        work_t = [ctx.enter_context(nc.psum_tensor(f"work{s}_ps", [128, 2, 512], F32)) for s in range(2)]
        att_t = [ctx.enter_context(nc.psum_tensor(f"att{s}_ps", [128, 512], F32)) for s in range(2)]
        ysum = ctx.enter_context(nc.psum_tensor("ysum", [128, 2, 512], F32))

        const = {n: sb(f"{n}_sb", list(v.shape), v.dtype) for n, v in a.items() if n != "x"}
        woff, boff, wdcn, bn = const["woff"], const["boff"], const["wdcn"], const["bn"]
        grid, negq, selp, sele, selx = (const[n] for n in ("grid", "negq", "selp", "sele", "selx"))
        bnw = sb("bnw", [128, 2, 4])
        zero16 = sb("zero16", [128, 512], F16)

        xin = sb("xin", [128, HW])
        xpad = [sb(f"xpad{n}", [128, HP, WP]) for n in range(3)]
        hpad = sb("hpad", [128, HP, WP])
        mpad = sb("mpad", [128, HP, WP])
        coords = sb("coords", [96, HW])
        hatf = [[sb(f"hatf{d}{t}", [120, HW]) for t in range(2)] for d in range(2)]
        haty = [[[sb(f"haty{s}{t}{p}", [120, HW], F16) for p in range(2)] for t in range(2)] for s in range(2)]
        hatx = [[[sb(f"hatx{s}{t}{p}", [120, HW], F16) for p in range(2)] for t in range(2)] for s in range(2)]
        hxe = [[sb(f"hxe{s}{b}", [120, 3, HW]) for b in range(2)] for s in range(2)]
        zt = [sb(f"zt{s}", [120, CHUNKS, TAPS * C]) for s in range(2)]
        prod = [[sb(f"prod{s}{b}", [120, 3, BLOCK_ROWS * W]) for b in range(2)] for s in range(2)]
        shared = sb("shared", [128, HP * W + 3 * HW])
        hmax = shared[:, 0:HP * W].rearrange("p (h w) -> p h w", w=W)
        dil, lgt, lgd = (shared[:, HP * W + n * HW:HP * W + (n + 1) * HW] for n in range(3))
        relu1 = dil
        c2 = lgd
        x3 = sb("x3", [128, HW])
        pl = [sb(f"pl{n}", [128, HW]) for n in range(2)]
        small = sb("small", [128, 24])
        ublk = sb("ublk", [128, 128])
        xt = [sb(f"xt{n}", [128, HW]) for n in range(2)]
        xt.append(xt[0])
        xcol = x3[:]
        qs = sb("qs", [64, 2, NG, GP])
        ks = sb("ks", [64, 2, NG, W])
        vs = sb("vs", [GP, 2, NG, 128])
        es = sb("es", [GP, 2, 2 * NG, W])
        pr = sb("pr", [GP, 2, 2 * NG, W])
        st = sb("st", [GP, 5, 4 * NG])
        lset = sb("lset", [4 * NG, GP])
        pb = sb("pb", [GP, 2, 2 * NG, G, W])
        pt = shared[0:GP, 0:4 * NG * GP].rearrange("p (s j n) -> p s j n", s=2, j=2 * NG)
        dw = sb("dw", [128, HW])
        gw = dw
        ow = pl
        mix = ow[0]
        ares = [xt[0], xt[1], sb("ares", [128, HW])]

        loaded = ctx.enter_context(nc.semaphore("consts_loaded"))
        s_border = ctx.enter_context(nc.semaphore("borders_set"))
        s_bn = ctx.enter_context(nc.semaphore("bn_step"))
        x_loaded = sig("x_loaded", 16)
        x_padded = sig("x_padded", 1)
        x1_padded = sig("x1_padded", 1)
        coords_raw = sig("coords_raw", 2)
        sig_exp = sig("sigmoid_exp", 2)
        sig_add = sig("sigmoid_add", 2)
        coords_ready = sig("coords_ready", 2)
        dist_y = sig("dist_y", 8)
        dist_x = sig("dist_x", 8)
        haty_f = sig("haty_f", 8)
        hatx_f = sig("hatx_f", 8)
        haty_hi = sig("haty_hi", 8)
        haty_lo = sig("haty_lo", 8, reused=True)
        hatx_m = sig("hatx_masked", 8)
        hatx_hi = sig("hatx_hi", 8)
        hatx_lo = sig("hatx_lo", 8, reused=True)
        n_groups = len(groups())
        per_row = n_groups // 3
        prod_ready = [sig(f"prod{s}_ready", 2 * n_groups, reused=True) for s in range(2)]
        prod_used = sig("prod_used", 2 * (n_groups - 1))
        y_summed = sig("y_summed", 2, reused=True)
        y_read = sig("y_read", 4, reused=True)
        z_ready = sig("z_ready", 4 * CHUNKS)
        hx_ready = sig("hx_ready", 4 * TAPS)
        x2_ready = sig("x2_ready", 1, reused=True)
        lgt_ready = sig("lgt_ready", 1)
        lgd_ready = sig("lgd_ready", 1)
        gate_ready = sig("gate_ready", 1)
        hmax_a = sig("hmax_a", 1)
        hmax_ready = sig("hmax_ready", 1)
        dil_a = sig("dil_a", 1)
        dil_ready = sig("dil_ready", 1)
        h_ready = sig("h_ready", 2, reused=True)
        c2_relu = sig("c2_relu", 2, reused=True)
        c2_gated = sig("c2_gated", 1)
        x3_ready = sig("x3_ready", 1)

        pl_ready = [sig(f"pool_logits{n}", 2) for n in range(2)]
        pl_max = [sig(f"pool_max{n}", 2) for n in range(2)]
        pl_exp = [sig(f"pool_exp{n}", 1) for n in range(2)]
        pl_rcp = [sig(f"pool_rcp{n}", 1) for n in range(2)]
        xs_sum = sig("pooled_sum", 1)
        xs_ready = sig("pooled_ready", 1)
        ctx_ready = sig("ctx_ready", 1)
        sc_exp = sig("scale_exp", 1)
        sc_add = sig("scale_add", 1)
        sc_ready = sig("scale_ready", 1)
        xm_sum = sig("mean_sum", 1)
        xm_ready = sig("mean_ready", 1)
        avg_ready = sig("avg_ready", 1)
        u_ready = sig("theta_ready", 1)
        ublk_ready = sig("theta_spread", 1)
        pp_ready = sig("pixel_softmax", 1)
        pp_exp = sig("pixel_sigmoid_exp", 1)
        pp_add = sig("pixel_sigmoid_add", 1)
        pp_rcp = sig("pixel_sigmoid", 1)
        xt_ready = sig("att_input", 3)
        xcol_ready = sig("att_input_by_columns", 3)
        q_ready = sig("q_ready", 12)
        k_ready = sig("k_ready", 3)
        v_ready = sig("v_ready", 12)
        e_ready = sig("energy_ready", 6)
        e_max = sig("energy_max", 3)
        e_sub = sig("energy_shifted", 3)
        p_exp = sig("p_exp", 3)
        p_sum = sig("p_sum", 3)
        s_log = sig("sum_log", 3)
        s_rcp = sig("sum_rcp", 3)
        lse_ready = sig("lse_ready", 3)
        lset_ready = sig("lse_rows_ready", 3)
        p_norm = sig("p_normed", 3)
        pb_ready = [sig(f"p{s}_blocks", 3) for s in range(2)]
        pt_ready = [sig(f"p{s}_turned", 9) for s in range(2)]
        d_ready = sig("gap_ready", 6)
        g_exp = sig("gap_exp", 3)
        g_add = sig("gap_add", 3)
        g_ready = sig("share_ready", 3)
        o_ready = sig("out_read", 12, reused=True)
        m_diff = sig("mix_diff", 3)
        m_mul = sig("mix_scaled", 3)
        m_add = sig("mix_added", 3)
        a_ready = sig("att_output", 3, reused=True)
        stored = sig("stored", 16, reused=True)

        items = []
        for l in range(2):
            items.append((("offsets", l), coords_raw, l + 1))
            for s in range(2):
                ls = l * 2 + s
                items += [(("z", l, s, c), z_ready, ls * CHUNKS + c + 1) for c in range(CHUNKS)]
                for t in range(2):
                    items += [(("y", l, s, t), dist_y, ls * 2 + t + 1), (("x", l, s, t), dist_x, ls * 2 + t + 1),
                              (("m", l, s, t), hatx_m, ls * 2 + t + 1)]
            for g in range(n_groups):
                if g % per_row == 0:
                    items += [(("hx", l, s, q), hx_ready, ((l * 3 + g // per_row) * 2 + s) * 3 + q % 3 + 1)
                              for s in range(2) for q in range(g // per_row * 3, g // per_row * 3 + 3)]
                items += [(("hy", l, s, g), prod_ready[s], l * n_groups + g + 1) for s in range(2)]
        items += [(("gate",), lgt_ready, 1), (("conv1",), h_ready, 2), (("conv2",), c2_relu, 2)]
        work = Ring(nc, ctx, "work", work_t, items)
        items = [(("pool_logits", h), pl_ready[0], h + 1) for h in range(2)]
        items += [(("avg",), avg_ready, 1), (("theta",), u_ready, 1)]
        items += [(("pixel_logits", h), pl_ready[1], h + 1) for h in range(2)]
        items += [(("ctx",), ctx_ready, 1), (("scale",), sc_exp, 1)]
        dh = [(d, h) for d in range(2) for h in range(2)]
        for x in range(3):
            items += [(("q", x, d, h), q_ready, x * 4 + d * 2 + h + 1) for d, h in dh] + [(("k", x), k_ready, x + 1)]
            items += [(("v", x, d, h), v_ready, x * 4 + d * 2 + h + 1) for d, h in dh]
            items += [(("e", x, s), e_ready, x * 2 + s + 1) for s in range(2)] + [(("lse", x), lset_ready, x + 1)]
            items += [(("d", x, h), d_ready, x * 2 + h + 1) for h in range(2)]
            items += [(("p", x, s, j), pt_ready[s], x * 3 + j + 1) for s in range(2) for j in range(3)]
            items += [(("o", x, d, h), o_ready, x * 4 + d * 2 + h + 1) for d, h in dh]
        att = Ring(nc, ctx, "att", att_t, items)

        n_const = len(const)
        block = ctx.enter_context(nc.Block())

        NMX, SUM, RCP, XS, XR, CTX, SE, SA, SR, XM, XA, AVG, U, BUPN = 0, 2, 4, 6, 7, 8, 9, 10, 11, 12, 13, 14, 15, 16

        def rows(buf, r0, r1):
            return buf[:, r0 + 1:r1 + 1, 1:W + 1]

        def halves(buf):
            return buf.rearrange("p (b n) -> p b n", b=2)

        def grid3(buf):
            return buf.rearrange("p (h w) -> p h w", w=W)

        def y_pieces(r0, r1):
            if r0 < Y_ROWS:
                yield 0, r0 * W, r0, min(r1, Y_ROWS)
            if r1 > Y_ROWS:
                yield 1, (max(r0, Y_ROWS) - Y_ROWS) * W, max(r0, Y_ROWS), r1

        @block.sync
        def _(sp):
            for signal in primed:
                sp.sem_inc(signal.sem, 1)
            for n, t in const.items():
                sp.dma_start(t[:], a[n]).then_inc(loaded, 16)
            with sp.Fori(0, PAIRS) as i:
                sp.wait_ge(*x2_ready(i, 0))
                sp.dma_start(xin[:], a["x"][i]).then_inc(x_loaded.sem, 16)

        @block.gpsimd
        def _(pool):
            nc.gpsimd.memset(zero16[:], 0.0).then_inc(s_border, 1)
            for buf in (*xpad, hpad):
                nc.gpsimd.memset(buf[:], 0.0).then_inc(s_border, 1)
            nc.gpsimd.memset(mpad[:], MASKED).then_inc(s_border, 1)
            pool.wait_ge(s_border, 6)
            pool.wait_ge(loaded, 16 * n_const)
            with pool.Fori(0, PAIRS) as i:
                pool.wait_ge(*x_loaded(i, 16))
                pool.wait_ge(*y_summed(i, 0))
                nc.gpsimd.nop(nofuse=True)
                nc.gpsimd.tensor_copy(rows(xpad[0], 0, H), grid3(xin[:])).then_inc(x_padded.sem, 1)

                for l in range(2):
                    if l == 1:
                        pool.wait_ge(*y_read(i, 2))
                        nc.gpsimd.nop(nofuse=True)
                        nc.gpsimd.tensor_copy(rows(xpad[1], 0, H), grid3(xin[:])).then_inc(x1_padded.sem, 1)
                    for s in range(2):
                        for t in range(2):
                            n = TILE_ROWS[t]
                            k = (l * 2 + s) * 2 + t + 1
                            hi, lo = haty[s][t]
                            pool.wait_ge(*haty_f(i, k))
                            pool.wait_ge(*y_summed(i, l))
                            nc.gpsimd.nop(nofuse=True)
                            nc.gpsimd.tensor_copy(hi[0:n, :], hatf[0][t][0:n, :]).then_inc(haty_hi.sem, 1)
                            pool.wait_ge(*haty_hi(i, k))
                            nc.gpsimd.tensor_tensor(lo[0:n, :], hatf[0][t][0:n, :], hi[0:n, :],
                                                    ALU.subtract).then_inc(haty_lo.sem, 1)
                            hi, lo = hatx[s][t]
                            pool.wait_ge(*hatx_m(i, k))
                            nc.gpsimd.nop(nofuse=True)
                            nc.gpsimd.tensor_copy(hi[0:n, :], hatf[1][t][0:n, :]).then_inc(hatx_hi.sem, 1)
                            pool.wait_ge(*hatx_hi(i, k))
                            nc.gpsimd.tensor_tensor(lo[0:n, :], hatf[1][t][0:n, :], hi[0:n, :],
                                                    ALU.subtract).then_inc(hatx_lo.sem, 1)
                for x in range(3):
                    pool.wait_ge(*xt_ready(i, max(2, x + 1)))
                    if x:
                        pool.wait_ge(*v_ready(i, 4 * x))
                    nc.gpsimd.nop(nofuse=True)
                    nc.gpsimd.tensor_copy(xcol.rearrange("p (w h) -> p h w", h=H), grid3(xt[x][:])).then_inc(xcol_ready.sem, 1)
                    pool.wait_ge(*p_norm(i, x + 1))
                    if x:
                        pool.wait_ge(*att.filled(i, ("p", x - 1, 1, 2)))
                    else:
                        pool.wait_ge(*a_ready(i, 0))
                    p_b = pr[:, 1, :, :].unsqueeze(2).broadcast_to([GP, 2 * NG, G, W])
                    k_b = const["blk"][:].unsqueeze(1).broadcast_to([GP, 2 * NG, G, W])
                    nc.gpsimd.tensor_tensor(pb[:, 1], p_b, k_b, ALU.mult).then_inc(pb_ready[1].sem, 1)

        @block.scalar
        def _(act):
            act.wait_ge(loaded, 16 * n_const)
            act.wait_ge(s_bn, 1)
            nc.scalar.activation(bnw[:, :, 1], bnw[:, :, 0], ACT.Sqrt).then_inc(s_bn, 1)
            act.wait_ge(s_bn, 8)
            nc.scalar.preload_act_table(ACT.Ln)
            with act.Fori(0, PAIRS) as i:
                for l in range(2):
                    for s in range(2):
                        for c in range(CHUNKS):
                            n = chunk_rows(c) * W
                            item = ("z", l, s, c)
                            act.wait_ge(*work.filled(i, item))
                            act.wait_ge(*y_summed(i, l))
                            nc.scalar.copy(zt[s][0:n, c, :].rearrange("p (b n) -> p b n", b=2),
                                           work.tile(item)[0:n, :, 0:HALF]).then_inc(z_ready.sem, 1)
                        if s == 0:
                            act.wait_ge(*coords_raw(i, l + 1))
                            nc.scalar.activation(coords[64:96, :], coords[64:96, :], ACT.Exp,
                                                 scale=-1.0).then_inc(sig_exp.sem, 1)
                        for t in range(2):
                            n = TILE_ROWS[t]
                            k = (l * 2 + s) * 2 + t + 1
                            for kind, d, done, d_done in (("y", 0, haty_f, dist_y),
                                                               ("x", 1, hatx_f, dist_x)):
                                item = (kind, l, s, t)
                                act.wait_ge(*work.filled(i, item))
                                act.wait_ge(*(haty_lo if kind == "y" else hatx_lo)(i, max(0, k - 2)))
                                nc.scalar.activation(hatf[d][t][0:n, :].rearrange("p (b n) -> p b n", b=2),
                                                     work.tile(item)[0:n, :, 0:HALF], ACT.Abs,
                                                     bias=negq[0:n, 0:1]).then_inc(d_done.sem, 1)
                                act.wait_ge(*d_done(i, k))
                                nc.scalar.activation(hatf[d][t][0:n, :], hatf[d][t][0:n, :], ACT.Relu,
                                                     bias=negq[0:n, 1:2], scale=-SCALE16).then_inc(done.sem, 1)
                    for ky in range(3):
                        for s in range(2):
                            for k in range(3 * ky, 3 * ky + 3):
                                item = ("hx", l, s, k)
                                act.wait_ge(*work.filled(i, item))
                                if ky == 2:
                                    act.wait_ge(*prod_ready[s](i, l * n_groups + per_row))
                                else:
                                    act.wait_ge(*prod_ready[s](i, l * n_groups))
                                nc.scalar.copy(halves(hxe[s][ky % 2][:, k % 3, :]),
                                               work.tile(item)[0:120, :, 0:HALF]).then_inc(hx_ready.sem, 1)
                    act.wait_ge(*y_summed(i, l + 1))
                    for bank, c0, r0, r1 in y_pieces(0, H):
                        nc.scalar.activation((xin, relu1)[l][:, r0 * W:r1 * W], ysum[:, bank, c0:c0 + (r1 - r0) * W],
                                             ACT.Relu, bias=bnw[:, l, 3:4], scale=bnw[:, l, 2:3]).then_inc(y_read.sem, 1)

                for n, name in enumerate(("pool_logits", "pixel_logits")):
                    for h in range(2):
                        item = (name, h)
                        act.wait_ge(*att.filled(i, item))
                        nc.scalar.copy(pl[n][:, h * HALF:(h + 1) * HALF], att.tile(item)[:, 0:HALF]).then_inc(pl_ready[n].sem, 1)
                    act.wait_ge(*pl_max[n](i, 2))
                    nc.scalar.activation(pl[n][:], pl[n][:], ACT.Exp, bias=small[:, NMX + n:NMX + n + 1],
                                         accum_out=small[:, SUM + n:SUM + n + 1]).then_inc(pl_exp[n].sem, 1)
                act.wait_ge(*att.filled(i, ("scale",)))
                nc.scalar.activation(small[:, SE:SE + 1], att.tile(("scale",))[:, 0:1], ACT.Exp,
                                     bias=small[:, BUPN:BUPN + 1], scale=-1.0).then_inc(sc_exp.sem, 1)
                act.wait_ge(*pp_ready(i, 1))
                nc.scalar.activation(pl[1][:], pl[1][:], ACT.Exp, scale=-1.0).then_inc(pp_exp.sem, 1)
                for x in range(3):
                    act.wait_ge(*att.filled(i, ("k", x)))
                    nc.scalar.activation(ks[:].rearrange("p d g v -> p (d g v)"), att.tile(("k", x))[0:64, 0:2 * NG * W],
                                         ACT.Identity, bias=const["bk"][:, 0:1]).then_inc(k_ready.sem, 1)
                    for d in range(2):
                        for h in range(2):
                            item = ("v", x, d, h)
                            act.wait_ge(*att.filled(i, item))
                            nc.scalar.copy(vs[:, d, 3 * h:3 * h + 3, :],
                                           att.tile(item)[0:GP, 0:384].rearrange("p (g c) -> p g c", g=3)).then_inc(v_ready.sem, 1)
                    act.wait_ge(*e_sub(i, x + 1))
                    nc.scalar.activation(pr[:], es[:], ACT.Exp).then_inc(p_exp.sem, 1)
                    act.wait_ge(*p_sum(i, x + 1))
                    nc.scalar.activation(st[:, 2, :], st[:, 1, :], ACT.Ln).then_inc(s_log.sem, 1)
                    act.wait_ge(*d_ready(i, 2 * x + 2))
                    nc.scalar.activation(gw[:], dw[:], ACT.Exp).then_inc(g_exp.sem, 1)
                    for j in range(3):
                        item = ("p", x, 1, j)
                        act.wait_ge(*att.filled(i, item))
                        nc.scalar.copy(pt[:, 1, 4 * j:4 * j + 4, :],
                                       att.tile(item)[0:GP, 0:384].rearrange("p (g c) -> p g c", g=4)).then_inc(pt_ready[1].sem, 1)
                    for d in range(2):
                        for h in range(2):
                            item = ("o", x, d, h)
                            src = att.tile(item)[:, 0:HALF]
                            dst = ow[d][:, h * HALF:(h + 1) * HALF]
                            if d == 1:
                                src = src.rearrange("p (w h) -> p h w", h=H)
                                dst = grid3(ow[1][:])[:, :, h * (W // 2):(h + 1) * (W // 2)]
                            act.wait_ge(*att.filled(i, item))
                            nc.scalar.activation(dst, src, ACT.Identity, bias=const["bv"][:, 0:1]).then_inc(o_ready.sem, 1)
                act.wait_ge(*a_ready(i, 3))
                act.dma_start(out[i], ares[2][:]).then_inc(stored.sem, 16)
            act.wait_ge(*stored(PAIRS - 1, 16))

        @block.vector
        def _(dve):
            def w(pair):
                dve.wait_ge(*pair)

            dve.wait_ge(loaded, 16 * n_const)
            v = nc.vector
            v.tensor_scalar(bnw[:, :, 0], bn[:, :, 4], EPS, None, ALU.add).then_inc(s_bn, 1)
            dve.wait_ge(s_bn, 2)
            v.reciprocal(bnw[:, :, 0], bnw[:, :, 1]).then_inc(s_bn, 1)
            dve.wait_ge(s_bn, 3)
            v.tensor_tensor(bnw[:, :, 2], bnw[:, :, 0], bn[:, :, 1], ALU.mult).then_inc(s_bn, 1)
            dve.wait_ge(s_bn, 4)
            v.tensor_tensor(bnw[:, :, 1], bn[:, :, 0], bn[:, :, 3], ALU.subtract).then_inc(s_bn, 1)
            dve.wait_ge(s_bn, 5)
            v.tensor_tensor(bnw[:, :, 1], bnw[:, :, 1], bnw[:, :, 2], ALU.mult).then_inc(s_bn, 1)
            dve.wait_ge(s_bn, 6)
            v.tensor_tensor(bnw[:, :, 3], bnw[:, :, 1], bn[:, :, 2], ALU.add).then_inc(s_bn, 1)
            v.tensor_scalar(small[:, BUPN:BUPN + 1], const["bup"][:], -1.0, None, ALU.mult).then_inc(s_bn, 1)

            with dve.Fori(0, PAIRS) as i:
                for l in range(2):
                    item = ("offsets", l)
                    w(work.filled(i, item))
                    v.scalar_tensor_tensor(out=coords[:].rearrange("p (b n) -> p b n", b=2),
                                           in0=work.tile(item)[0:96, :, 0:HALF], scalar=boff[:, l:l + 1],
                                           in1=grid[:].rearrange("p (b n) -> p b n", b=2),
                                           op0=ALU.add, op1=ALU.add).then_inc(coords_raw.sem, 1)
                    w(sig_exp(i, l + 1))
                    v.tensor_scalar(coords[64:96, :], coords[64:96, :], 1.0, None, ALU.add).then_inc(sig_add.sem, 1)
                    w(sig_add(i, l + 1))
                    w(coords_raw(i, l + 1))
                    v.reciprocal(coords[64:96, :], coords[64:96, :]).then_inc(coords_ready.sem, 1)
                    for s in range(2):
                        for t in range(2):
                            n = TILE_ROWS[t]
                            k = (l * 2 + s) * 2 + t + 1
                            item = ("m", l, s, t)
                            w(work.filled(i, item))
                            w(hatx_f(i, k))
                            v.tensor_tensor(hatf[1][t][0:n, :].rearrange("p (b n) -> p b n", b=2),
                                            work.tile(item)[0:n, :, 0:HALF],
                                            hatf[1][t][0:n, :].rearrange("p (b n) -> p b n", b=2),
                                            ALU.mult).then_inc(hatx_m.sem, 1)
                    for g, (c, ky, b) in enumerate(groups()):
                        r0, r1 = blocks_of(c, ky, NARROW)[b]
                        n = (r1 - r0) * W
                        m = chunk_rows(c) * W
                        for s in range(2):
                            item = ("hy", l, s, g)
                            w(work.filled(i, item))
                            if g % per_row == 0:
                                w(work.emptied(i, ("hx", l, s, 3 * ky + 2)))
                            if g >= 2:
                                w(prod_used(i, l * (n_groups - 1) + g - 1))
                            v.tensor_tensor(prod[s][g % 2][0:m, :, 0:n],
                                            work.tile(item).rearrange("p b n -> p (b n)").rearrange(
                                                "p (t n) -> p t n", n=SEG)[0:m, 0:3, 0:n],
                                            hxe[s][ky % 2][0:m, :, r0 * W:r1 * W],
                                            ALU.mult).then_inc(prod_ready[s].sem, 1)
                w(y_read(i, 4))
                v.tensor_tensor(rows(xpad[2], 0, H), grid3(xin[:]), grid3(relu1), ALU.add).then_inc(x2_ready.sem, 1)
                w(work.filled(i, ("gate",)))
                v.tensor_scalar(halves(lgt), work.tile(("gate",))[:, :, 0:HALF], const["bm"][:, 0:1], None,
                                ALU.add).then_inc(lgt_ready.sem, 1)
                w(lgt_ready(i, 1))
                v.scalar_tensor_tensor(out=lgd, in0=lgt, scalar=0.0, in1=lgt,
                                       op0=ALU.is_gt, op1=ALU.subtract).then_inc(lgd_ready.sem, 1)
                w(lgd_ready(i, 1))
                v.tensor_tensor(rows(mpad, 0, H), grid3(lgt), grid3(lgd), ALU.add).then_inc(gate_ready.sem, 1)
                w(gate_ready(i, 1))
                v.tensor_tensor(hmax, mpad[:, :, 0:W], mpad[:, :, 1:W + 1], ALU.max).then_inc(hmax_a.sem, 1)
                w(hmax_a(i, 1))
                v.tensor_tensor(hmax, hmax, mpad[:, :, 2:W + 2], ALU.max).then_inc(hmax_ready.sem, 1)
                w(hmax_ready(i, 1))
                v.tensor_tensor(grid3(dil), hmax[:, 0:H, :], hmax[:, 1:H + 1, :], ALU.max).then_inc(dil_a.sem, 1)
                w(dil_a(i, 1))
                v.tensor_tensor(grid3(dil), grid3(dil), hmax[:, 2:H + 2, :], ALU.max).then_inc(dil_ready.sem, 1)
                w(dil_ready(i, 1))
                w(work.filled(i, ("conv1",)))
                for h in range(2):
                    v.scalar_tensor_tensor(out=rows(hpad, h * HR, (h + 1) * HR),
                                           in0=grid3(work.tile(("conv1",))[:, h, 0:HALF]), scalar=0.0,
                                           in1=grid3(dil[:, h * HALF:(h + 1) * HALF]),
                                           op0=ALU.max, op1=ALU.mult).then_inc(h_ready.sem, 1)
                w(work.filled(i, ("conv2",)))
                w(gate_ready(i, 1))
                for h in range(2):
                    v.scalar_tensor_tensor(out=grid3(c2[:, h * HALF:(h + 1) * HALF]),
                                           in0=grid3(work.tile(("conv2",))[:, h, 0:HALF]), scalar=0.0,
                                           in1=rows(mpad, h * HR, (h + 1) * HR),
                                           op0=ALU.max, op1=ALU.mult).then_inc(c2_relu.sem, 1)
                w(c2_relu(i, 2))
                v.tensor_tensor(grid3(c2), grid3(c2), rows(mpad, 0, H), ALU.mult).then_inc(c2_gated.sem, 1)
                w(c2_gated(i, 1))
                v.tensor_tensor(grid3(x3[:]), grid3(c2), rows(xpad[2], 0, H), ALU.add).then_inc(x3_ready.sem, 1)
                w(x3_ready(i, 1))

                v.tensor_reduce(small[:, XM:XM + 1], x3[:], AX, ALU.add).then_inc(xm_sum.sem, 1)
                w(xm_sum(i, 1))
                v.tensor_scalar(small[:, XA:XA + 1], small[:, XM:XM + 1], 1.0 / HW, None, ALU.mult).then_inc(xm_ready.sem, 1)

                def softmax_max(n):
                    w(pl_ready[n](i, 2))
                    v.tensor_reduce(small[:, SUM + n:SUM + n + 1], pl[n][:], AX, ALU.max).then_inc(pl_max[n].sem, 1)
                    w(pl_max[n](i, 1))
                    v.tensor_scalar(small[:, NMX + n:NMX + n + 1], small[:, SUM + n:SUM + n + 1], -1.0, None,
                                    ALU.mult).then_inc(pl_max[n].sem, 1)

                softmax_max(0)
                w(att.filled(i, ("avg",)))
                v.tensor_copy(small[0:2 * CM, AVG:AVG + 1], att.tile(("avg",))[0:2 * CM, 0:1]).then_inc(avg_ready.sem, 1)
                w(att.filled(i, ("theta",)))
                v.tensor_copy(small[:, U:U + 1], att.tile(("theta",))[:, 0:1]).then_inc(u_ready.sem, 1)
                w(u_ready(i, 1))
                v.tensor_scalar(ublk[:], const["oneb"][:], small[:, U:U + 1], None, ALU.mult).then_inc(ublk_ready.sem, 1)
                w(pl_exp[0](i, 1))
                v.tensor_tensor_reduce(out=lgt, in0=x3[:], in1=pl[0][:], scale=1.0, scalar=0.0,
                                       op0=ALU.mult, op1=ALU.add, accum_out=small[:, XS:XS + 1]).then_inc(xs_sum.sem, 1)
                v.reciprocal(small[:, RCP:RCP + 1], small[:, SUM:SUM + 1]).then_inc(pl_rcp[0].sem, 1)
                w(xs_sum(i, 1))
                w(pl_rcp[0](i, 1))
                v.tensor_tensor(small[:, XR:XR + 1], small[:, XS:XS + 1], small[:, RCP:RCP + 1],
                                ALU.mult).then_inc(xs_ready.sem, 1)
                softmax_max(1)
                w(att.filled(i, ("ctx",)))
                v.tensor_copy(small[0:2 * CM, CTX:CTX + 1], att.tile(("ctx",))[0:2 * CM, 0:1]).then_inc(ctx_ready.sem, 1)
                w(pl_exp[1](i, 1))
                v.reciprocal(small[:, RCP + 1:RCP + 2], small[:, SUM + 1:SUM + 2]).then_inc(pl_rcp[1].sem, 1)
                w(pl_rcp[1](i, 1))
                v.tensor_scalar(pl[1][:], pl[1][:], small[:, RCP + 1:RCP + 2], None, ALU.mult).then_inc(pp_ready.sem, 1)
                w(sc_exp(i, 1))
                v.tensor_scalar(small[:, SA:SA + 1], small[:, SE:SE + 1], 1.0, None, ALU.add).then_inc(sc_add.sem, 1)
                w(sc_add(i, 1))
                v.reciprocal(small[:, SR:SR + 1], small[:, SA:SA + 1]).then_inc(sc_ready.sem, 1)
                w(sc_ready(i, 1))
                v.tensor_scalar(xt[0][:], x3[:], small[:, SR:SR + 1], None, ALU.mult).then_inc(xt_ready.sem, 1)
                w(pp_exp(i, 1))
                v.tensor_scalar(pl[1][:], pl[1][:], 1.0, None, ALU.add).then_inc(pp_add.sem, 1)
                w(pp_add(i, 1))
                v.reciprocal(pl[1][:], pl[1][:]).then_inc(pp_rcp.sem, 1)
                w(pp_rcp(i, 1))
                v.tensor_tensor(xt[1][:], x3[:], pl[1][:], ALU.mult).then_inc(xt_ready.sem, 1)

                for x in range(3):
                    for d in range(2):
                        for h in range(2):
                            item = ("q", x, d, h)
                            w(att.filled(i, item))
                            v.tensor_tensor(qs[:, d, 3 * h:3 * h + 3, :],
                                            att.tile(item)[0:64, 0:HALF].rearrange("p (g n) -> p g n", g=3),
                                            const["bq"][:].unsqueeze(1).broadcast_to([64, 3, GP]),
                                            ALU.add).then_inc(q_ready.sem, 1)
                    flat = es[:].rearrange("p s j v -> p (s j) v")
                    probs = pr[:].rearrange("p s j v -> p (s j) v")
                    for s in range(2):
                        item = ("e", x, s)
                        w(att.filled(i, item))
                        v.tensor_tensor(es[:, s].rearrange("p (d g) v -> p d g v", d=2),
                                        att.tile(item)[0:GP, 0:HALF].rearrange("p (d g v) -> p d g v", d=2, g=NG),
                                        const["emask"][:].unsqueeze(2).broadcast_to([GP, 2, NG, W]), ALU.add).then_inc(e_ready.sem, 1)
                    w(e_ready(i, 2 * x + 2))
                    v.tensor_reduce(st[:, 0, :], flat, AX, ALU.max).then_inc(e_max.sem, 1)
                    w(e_max(i, x + 1))
                    v.tensor_tensor(flat, flat, st[:, 0, :].unsqueeze(2).broadcast_to([GP, 4 * NG, W]),
                                    ALU.subtract).then_inc(e_sub.sem, 1)
                    w(p_exp(i, x + 1))
                    v.tensor_reduce(st[:, 1, :], probs, AX, ALU.add).then_inc(p_sum.sem, 1)
                    w(p_sum(i, x + 1))
                    v.reciprocal(st[:, 4, :], st[:, 1, :]).then_inc(s_rcp.sem, 1)
                    w(s_log(i, x + 1))
                    v.tensor_tensor(st[:, 3, :], st[:, 0, :], st[:, 2, :], ALU.add).then_inc(lse_ready.sem, 1)
                    w(s_rcp(i, x + 1))
                    v.tensor_tensor(probs, probs, st[:, 4, :].unsqueeze(2).broadcast_to([GP, 4 * NG, W]),
                                    ALU.mult).then_inc(p_norm.sem, 1)
                    w(att.filled(i, ("lse", x)))
                    v.tensor_copy(lset[:], att.tile(("lse", x))[0:4 * NG, 0:GP]).then_inc(lset_ready.sem, 1)
                    w(p_norm(i, x + 1))
                    v.tensor_tensor(pb[:, 0], pr[:, 0].unsqueeze(2).broadcast_to([GP, 2 * NG, G, W]),
                                    const["blk"][:].unsqueeze(1).broadcast_to([GP, 2 * NG, G, W]),
                                    ALU.mult).then_inc(pb_ready[0].sem, 1)
                    for h in range(2):
                        item = ("d", x, h)
                        w(att.filled(i, item))
                        v.tensor_scalar(dw[:, h * HALF:(h + 1) * HALF], att.tile(item)[:, 0:HALF], -1.0, 80.0,
                                        ALU.mult, ALU.min).then_inc(d_ready.sem, 1)
                    for j in range(3):
                        item = ("p", x, 0, j)
                        w(att.filled(i, item))
                        v.tensor_copy(pt[:, 0, 4 * j:4 * j + 4, :],
                                      att.tile(item)[0:GP, 0:384].rearrange("p (g c) -> p g c", g=4)).then_inc(pt_ready[0].sem, 1)
                    w(g_exp(i, x + 1))
                    v.tensor_scalar(gw[:], gw[:], 1.0, None, ALU.add).then_inc(g_add.sem, 1)
                    w(g_add(i, x + 1))
                    v.reciprocal(gw[:], gw[:]).then_inc(g_ready.sem, 1)
                    w(o_ready(i, 4 * x + 4))
                    v.tensor_tensor(mix[:], ow[0][:], ow[1][:], ALU.subtract).then_inc(m_diff.sem, 1)
                    w(m_diff(i, x + 1))
                    w(g_ready(i, x + 1))
                    v.tensor_tensor(mix[:], mix[:], gw[:], ALU.mult).then_inc(m_mul.sem, 1)
                    w(m_mul(i, x + 1))
                    v.tensor_tensor(mix[:], mix[:], ow[1][:], ALU.add).then_inc(m_add.sem, 1)
                    w(m_add(i, x + 1))
                    if x == 2:
                        w(stored(i, 0))
                    v.scalar_tensor_tensor(out=ares[x][:], in0=mix[:], scalar=const["gamma"][:, 0:1], in1=xt[x][:],
                                           op0=ALU.mult, op1=ALU.add).then_inc(a_ready.sem, 1)
                    if x == 1:
                        w(a_ready(i, 2))
                        v.tensor_tensor(xt[2][:], ares[0][:], ares[1][:], ALU.add).then_inc(xt_ready.sem, 1)

        @block.tensor
        def _(pe):
            mm = nc.tensor.matmul

            def w(pair):
                pe.wait_ge(*pair)

            w((s_border, 6))
            w((loaded, 16 * n_const))

            with pe.Fori(0, PAIRS) as i:
                def conv(item, weights, src, m):
                    w(work.may_fill(i, item))
                    for h in range(2):
                        for k in range(TAPS):
                            r = k // 3 + h * HR
                            last = mm(work.tile(item)[0:m, h, 0:HALF], weights[:, k, :],
                                      src[:, r:r + HR, k % 3:k % 3 + W], start=(k == 0), stop=(k == TAPS - 1))
                    last.then_inc(work.full_sem(item), 1)

                for l in range(2):
                    if l == 0:
                        w(x_padded(i, 1))
                    else:
                        w(y_read(i, 2))
                        w(x1_padded(i, 1))
                    conv(("offsets", l), woff[:, l], xpad[l], 96)
                    for s in range(2):
                        for c in range(CHUNKS):
                            item = ("z", l, s, c)
                            n = chunk_rows(c) * W
                            w(work.may_fill(i, item))
                            for h in range(2):
                                last = mm(work.tile(item)[0:n, h, 0:HALF],
                                          xin[s * C:(s + 1) * C, c * CR * W:c * CR * W + n],
                                          wdcn[s * C:(s + 1) * C, l, h * HALF:(h + 1) * HALF], start=True, stop=True)
                            last.then_inc(work.full_sem(item), 1)
                        if s == 0:
                            w(coords_ready(i, l + 1))
                        for t in range(2):
                            n = TILE_ROWS[t]
                            for kind, name in enumerate(("y", "x", "m")):
                                item = (name, l, s, t)
                                w(work.may_fill(i, item))
                                for h in range(2):
                                    last = mm(work.tile(item)[0:n, h, 0:HALF], selp[:, s, t, kind, 0:n],
                                              coords[:, h * HALF:(h + 1) * HALF], start=True, stop=True)
                                last.then_inc(work.full_sem(item), 1)
                    w(y_read(i, 2 * l))
                    mm(ysum[:, 0, 0:Y_ROWS * W], zero16[:, 0:128], zero16[:, 0:Y_ROWS * W], start=True, stop=True)
                    mm(ysum[:, 1, 0:(H - Y_ROWS) * W], zero16[:, 0:128], zero16[:, 0:(H - Y_ROWS) * W], start=True, stop=True)
                    w(haty_lo(i, l * 4 + 4))
                    w(z_ready(i, (l + 1) * 2 * CHUNKS))
                    steps = groups()
                    for g in range(n_groups + 1):
                        if g < n_groups and g % per_row == 0:
                            for s in range(2):
                                w(hatx_lo(i, (l * 2 + s) * 2 + 2))
                                for k in range(3 * steps[g][1], 3 * steps[g][1] + 3):
                                    item = ("hx", l, s, k)
                                    t = k // T0
                                    n = TILE_ROWS[t]
                                    w(work.may_fill(i, item))
                                    for h in range(2):
                                        for part in range(2):
                                            last = mm(work.tile(item)[0:120, h, 0:HALF], selx[0:n, k, :],
                                                      hatx[s][t][part][0:n, h * HALF:(h + 1) * HALF],
                                                      start=(part == 0), stop=(part == 1))
                                    last.then_inc(work.full_sem(item), 1)
                        if g < n_groups:
                            c, ky, b = steps[g]
                            r0, r1 = blocks_of(c, ky, NARROW)[b]
                            n = (r1 - r0) * W
                            m = chunk_rows(c) * W
                            for s in range(2):
                                item = ("hy", l, s, g)
                                w(work.may_fill(i, item))
                                slot = work.tile(item).rearrange("p b n -> p (b n)")
                                for q in range(3):
                                    k = 3 * ky + q
                                    t = k // T0
                                    first = ((k - t * T0) * H + c * CR) * W
                                    for part in range(2):
                                        last = mm(slot[0:m, q * SEG:q * SEG + n], sele[0:TILE_ROWS[t], first:first + m],
                                                  haty[s][t][part][0:TILE_ROWS[t], r0 * W:r1 * W],
                                                  start=(part == 0), stop=(part == 1), skip_group_check=True)
                                last.then_inc(work.full_sem(item), 1)
                        if g > 0:
                            c, ky, b = steps[g - 1]
                            r0, r1 = blocks_of(c, ky, NARROW)[b]
                            m = chunk_rows(c) * W
                            for s in range(2):
                                w(prod_ready[s](i, l * n_groups + g))
                            for q in range(3):
                                k = 3 * ky + q
                                for bank, c0, a0, a1 in y_pieces(r0, r1):
                                    for s in range(2):
                                        last = mm(ysum[s * C:(s + 1) * C, bank, c0:c0 + (a1 - a0) * W],
                                                  zt[s][0:m, c, k * C:(k + 1) * C],
                                                  prod[s][(g - 1) % 2][0:m, q, (a0 - r0) * W:(a1 - r0) * W],
                                                  start=False, stop=True, skip_group_check=True)
                            last.then_inc((prod_used if g < n_groups else y_summed).sem, 1)

                w(x2_ready(i, 1))
                w(work.may_fill(i, ("gate",)))
                for h in range(2):
                    last = mm(work.tile(("gate",))[:, h, 0:HALF], const["wm"][:],
                              xpad[2][:, 1 + h * HR:1 + (h + 1) * HR, 1:W + 1], start=True, stop=True)
                last.then_inc(work.full_sem(("gate",)), 1)
                conv(("conv1",), const["w1"], xpad[2], 128)
                w(h_ready(i, 2))
                conv(("conv2",), const["w2"], hpad, 128)

                w(x3_ready(i, 1))

                def one(item, lhsT, rhs, m):
                    w(att.may_fill(i, item))
                    mm(att.tile(item)[0:m, 0:rhs.shape[-1]], lhsT, rhs, start=True, stop=True).then_inc(att.full_sem(item), 1)

                for h in range(2):
                    one(("pool_logits", h), const["wqr"][:], x3[:, h * HALF:(h + 1) * HALF], 128)
                w(xm_ready(i, 1))
                one(("avg",), const["wql"][:], small[:, XA:XA + 1], 2 * CM)
                w(avg_ready(i, 1))
                one(("theta",), const["wvl"][:], small[0:2 * CM, AVG:AVG + 1], 128)
                w(ublk_ready(i, 1))
                for h in range(2):
                    one(("pixel_logits", h), ublk[:], x3[:, h * HALF:(h + 1) * HALF], 128)
                w(xs_ready(i, 1))
                one(("ctx",), const["wvr"][:], small[:, XR:XR + 1], 2 * CM)
                w(ctx_ready(i, 1))
                one(("scale",), const["wup"][:], small[0:2 * CM, CTX:CTX + 1], 128)

                for x in range(3):
                    src = xt[x][:]
                    views = (src.rearrange("p (g r n) -> p g r n", r=G, n=W),
                             src.rearrange("p (n g r) -> p g r n", r=G, g=NG))
                    w(xt_ready(i, x + 1))
                    for d, h in dh:
                        item = ("q", x, d, h)
                        w(att.may_fill(i, item))
                        dst = att.tile(item)[0:64, 0:HALF].rearrange("p (g r n) -> p g r n", g=3, r=G)
                        for r in range(G):
                            last = mm(dst[:, :, r, :], const["wq"][:, r, :], views[d][:, 3 * h:3 * h + 3, r, :],
                                      start=True, stop=True, skip_group_check=True)
                        last.then_inc(att.full_sem(item), 1)
                    item = ("k", x)
                    w(att.may_fill(i, item))
                    for d in range(2):
                        for r in range(G):
                            last = mm(att.tile(item)[0:64, d * NG * W:(d + 1) * NG * W].rearrange("p (g n) -> p g n", g=NG),
                                      const["wk"][:, r, :], views[d][:, :, r, :], start=(r == 0), stop=(r == G - 1),
                                      skip_group_check=True)
                    last.then_inc(att.full_sem(item), 1)
                    w(xcol_ready(i, x + 1))
                    for d, h in dh:
                        item = ("v", x, d, h)
                        w(att.may_fill(i, item))
                        for g in range(3):
                            last = mm(att.tile(item)[0:GP, g * 128:(g + 1) * 128], (src, xcol)[d][:, (3 * h + g) * GP:(3 * h + g + 1) * GP], const["wv"][:],
                                      start=True, stop=True, skip_group_check=True)
                        last.then_inc(att.full_sem(item), 1)
                    w(q_ready(i, 4 * x + 4))
                    w(k_ready(i, x + 1))
                    for s in range(2):
                        item = ("e", x, s)
                        w(att.may_fill(i, item))
                        for d in range(2):
                            for g in range(NG):
                                j = d * NG + g
                                last = mm(att.tile(item)[0:GP, j * W:(j + 1) * W], qs[s * 32:(s + 1) * 32, d, g, :],
                                          ks[s * 32:(s + 1) * 32, d, g, :], start=True, stop=True, skip_group_check=True)
                        last.then_inc(att.full_sem(item), 1)
                    item = ("lse", x)
                    w(lse_ready(i, x + 1))
                    w(att.may_fill(i, item))
                    nc.tensor.transpose(att.tile(item)[0:4 * NG, 0:GP], st[:, 3, :], const["ident"][:]).then_inc(att.full_sem(item), 1)
                    w(lset_ready(i, x + 1))
                    for h in range(2):
                        item = ("d", x, h)
                        w(att.may_fill(i, item))
                        gap = att.tile(item)[:, 0:HALF]
                        mm(gap, zero16[:, 0:128], zero16[:, 0:HALF], start=True, stop=True)
                        for g in range(3):
                            mm(gap[:, g * GP:(g + 1) * GP], const["pick"][:, 3 * h + g, :], lset[:],
                               start=False, stop=True, skip_group_check=True)
                        for g in range(NG):
                            last = mm(grid3(gap)[:, :, g * G:(g + 1) * G], const["pick"][:, NG + g, :],
                                      lset[:].rearrange("p (r n) -> p n r", r=G)[:, h * HR:(h + 1) * HR, :],
                                      start=False, stop=True, skip_group_check=True)
                        last.then_inc(att.full_sem(item), 1)
                    for s in range(2):
                        w(pb_ready[s](i, x + 1))
                        for j in range(3):
                            item = ("p", x, s, j)
                            w(att.may_fill(i, item))
                            for q in range(4):
                                last = nc.tensor.transpose(att.tile(item)[0:GP, q * GP:(q + 1) * GP],
                                                           pb[:, s, 4 * j + q].rearrange("p r v -> p (r v)"), const["ident"][:])
                            last.then_inc(att.full_sem(item), 1)
                    w(v_ready(i, 4 * x + 4))
                    for s in range(2):
                        w(pt_ready[s](i, 3 * x + 3))
                    for d, h in dh:
                        item = ("o", x, d, h)
                        w(att.may_fill(i, item))
                        for g in range(3):
                            for s in range(2):
                                j = 3 * h + g
                                last = mm(att.tile(item)[s * C:(s + 1) * C, g * GP:(g + 1) * GP],
                                          vs[:, d, j, s * C:(s + 1) * C], pt[:, s, d * NG + j, :],
                                          start=True, stop=True, skip_group_check=True)
                        last.then_inc(att.full_sem(item), 1)


def diagonal(blocks, rows, cols):
    out = np.zeros((2 * rows,) + blocks.shape[1:-1] + (2 * cols,), np.float32)
    out[:rows, ..., :cols] = blocks
    out[rows:, ..., cols:] = blocks
    return out


def twice(v):
    return np.concatenate([v, v])[:, None]


def offset_layout(w):
    out = np.zeros((2, C, TAPS, 96), np.float32)
    t = w.reshape(27, C, TAPS).transpose(1, 2, 0)
    for s in range(2):
        for block, part in enumerate((t[..., 0:18:2], t[..., 1:18:2], t[..., 18:27])):
            out[s, :, :, 32 * block + 9 * s:32 * block + 9 * s + 9] = part
    return out.reshape(2 * C, TAPS, 96)


def offset_bias(b):
    out = np.zeros(96, np.float32)
    for s in range(2):
        for block, part in enumerate((b[0:18:2], b[1:18:2], b[18:27])):
            out[32 * block + 9 * s:32 * block + 9 * s + 9] = part
    return out


def group_weights(w):
    out = np.zeros((2, C, G, 2, G, CQ), np.float32)
    for s in range(2):
        for r in range(G):
            out[s, :, r, s, r, :] = w.T
    return out.reshape(2 * C, G, 2 * G * CQ)


def shape_constants():
    grid = np.zeros((96, H, W), np.float32)
    selp = np.zeros((96, 2, 2, 3, 120), np.float32)
    sele = np.zeros((120, 120, W), np.float16)
    for q in range(120):
        sele[q, q] = 1.0 / SCALE16
    selx = np.zeros((120, TAPS, 120), np.float16)
    unit = 1.0 / SCALE16
    for k in range(TAPS):
        t, kl = (0, k) if k < T0 else (1, k - T0)
        for s in range(2):
            grid[9 * s + k] = np.arange(H)[:, None] + (k // 3 - 1)
            grid[32 + 9 * s + k] = np.arange(W)[None, :] + (k % 3 - 1)
            for kind in range(3):
                selp[32 * kind + 9 * s + k, s, t, kind, kl * 24:kl * 24 + 24] = 1.0
        for q in range(24):
            selx[kl * 24 + q, k, q::24] = unit
    negq = np.zeros((120, 2), np.float32)
    negq[:, 0] = -(np.arange(120) % 24)
    negq[:, 1] = SCALE16
    emask = np.zeros((G, H, 2, W), np.float32)
    blk = np.zeros((G, W, G, W), np.float32)
    for n in range(24):
        emask[:, n, 1, n] = MASKED
    for r in range(G):
        blk[r, :, r, :] = 1.0
    pick = np.zeros((2, 2, NG, 2, NG, 2, C), np.float32)
    for s in range(2):
        for g in range(NG):
            pick[s, 0, g, 0, g, s, :] = 1.0
            pick[s, 1, g, 1, g, s, :] = -1.0
    oneb = np.zeros((2, C, 2, C), np.float32)
    for s in range(2):
        oneb[s, :, s, :] = 1.0
    return {
        "grid": grid.reshape(96, HW), "negq": negq, "selp": selp,
        "sele": sele.reshape(120, 120 * W), "selx": selx,
        "emask": emask.reshape(GP, 2, W), "blk": blk.reshape(GP, G, W), "ident": np.eye(GP, dtype=np.float32),
        "pick": pick.reshape(4 * NG, 2 * NG, 128), "oneb": oneb.reshape(128, 128),
    }


def kernel(**inputs):
    import concourse.bacc as bacc
    from concourse.bass_utils import run_bass_kernel_spmd

    p = {n: np.asarray(v) for n, v in inputs.items()}


    def norm(l, names):
        return np.stack([np.concatenate([p[f"L{l}_conv_{n}"]] * 2) for n in names], axis=1)

    def spread(v):
        return diagonal(np.broadcast_to(v.reshape(C, 1), (C, C)), C, C)

    bq = np.zeros((2, G, CQ, G, W), np.float32)
    for r in range(G):
        bq[:, r, :, r, :] = p["L3_conv_cr_bq"][None, :, None]
    wd = [p[n].reshape(C, C, TAPS).transpose(1, 2, 0).reshape(C, TAPS * C) for n in ("L0_conv_w_dcn", "L1_conv_w_conv")]
    taps = {n: p[f"L2_conv_{n}"].reshape(C, C, TAPS).transpose(1, 2, 0) for n in ("w1", "w2")}
    arrays = {
        "x": p["x"].reshape(PAIRS, 2 * C, HW),
        "woff": np.stack([offset_layout(p[f"L{l}_conv_w_off"]) for l in range(2)], axis=1),
        "boff": np.stack([offset_bias(p[f"L{l}_conv_b_off"]) for l in range(2)], axis=1),
        "wdcn": np.stack([np.concatenate([w, w]) for w in wd], axis=1),
        "bn": np.stack([norm(0, ("b_dcn", "gamma", "beta", "running_mean", "running_var")),
                        norm(1, ("b_conv", "gamma", "beta", "run_mean", "run_var"))], axis=1),
        "w1": diagonal(taps["w1"], C, C), "w2": diagonal(taps["w2"], C, C),
        "wm": spread(p["L2_conv_w_mask"]), "bm": np.broadcast_to(p["L2_conv_b_mask"].reshape(1, 1), (128, 1)),
        "wqr": spread(p["L3_conv_w_q_right"]),
        "wvr": diagonal(p["L3_conv_w_v_right"].T, C, CM), "wup": diagonal(p["L3_conv_w_up"].T, CM, C),
        "bup": twice(p["L3_conv_b_up"]),
        "wql": diagonal(p["L3_conv_w_q_left"].T, C, CM), "wvl": diagonal(p["L3_conv_w_v_left"], CM, C),
        "wq": group_weights(p["L3_conv_cr_wq"]), "wk": group_weights(p["L3_conv_cr_wk"]),
        "bq": bq.reshape(2 * G * CQ, GP), "bk": np.tile(p["L3_conv_cr_bk"], 2 * G)[:, None],
        "wv": diagonal(p["L3_conv_cr_wv"].T, C, C), "bv": twice(p["L3_conv_cr_bv"]),
        "gamma": np.broadcast_to(p["L3_conv_gamma"].reshape(1, 1), (128, 1)),
        **shape_constants(),
    }
    arrays = {n: np.ascontiguousarray(v) for n, v in arrays.items()}

    nc = bacc.Bacc("TRN2", target_bir_lowering=False, num_devices=1)
    args = {n: nc.dram_tensor(n, v.shape, mybir.dt.from_np(v.dtype), kind="ExternalInput").ap() for n, v in arrays.items()}
    out = nc.dram_tensor("out", (PAIRS, 2 * C, HW), F32, kind="ExternalOutput").ap()
    build(nc, args, out)
    r = run_bass_kernel_spmd(nc, [arrays], core_ids=[0])
    return r.results[0]["out"].reshape(B, C, H, W)
```

```python
from contextlib import ExitStack

import numpy as np

import concourse.bass as bass
from concourse import mybir

ALU = mybir.AluOpType
ACT = mybir.ActivationFunctionType
AX = mybir.AxisListType.X
F32 = mybir.dt.float32
F16 = mybir.dt.float16

B, C, H, W = 8, 64, 24, 24
HW = H * W
PAIRS = B // 2
HP, WP = H + 2, W + 2
HALF = HW // 2
HR = H // 2
TAPS = 9
EPS = 1e-5
T0 = 5
TILE_ROWS = (T0 * H, (TAPS - T0) * H)
CR = 5
CHUNKS = -(-H // CR)
Y_ROWS = 21
SCALE16 = 1024.0
REACH = 2
SEG = 256
BLOCK_ROWS = 9
G = 4
NG = H // G
GP = G * W
CQ = 8
CM = 32
MASKED = -1e30


def chunk_rows(c):
    return min(CR, H - c * CR)


def blocks_of(c, ky, narrow):
    first, last = 0, H - 1
    if narrow:
        shift = ky - 1
        first = max(0, c * CR - REACH - shift)
        last = min(H - 1, c * CR + chunk_rows(c) - 1 + REACH - shift)
    return [(r, min(r + BLOCK_ROWS, last + 1)) for r in range(first, last + 1, BLOCK_ROWS)]


class Signal:

    def __init__(self, nc, ctx, name, per_pair, primed=False):
        self.sem = ctx.enter_context(nc.semaphore(name))
        self.per_pair = per_pair
        self.primed = int(primed)

    def __call__(self, i, k):
        assert 1 - self.primed <= k <= self.per_pair, k
        return self.sem, i * self.per_pair + (k + self.primed)


class Ring:

    def __init__(self, nc, ctx, name, tiles, items):
        n = len(tiles)
        self.tiles = tiles
        self.read = {item: (signal, k) for item, signal, k in items}
        self.place = {item: (u % n, u // n + 1) for u, (item, _, _) in enumerate(items)}
        self.before = {item: items[u - n][0] if u >= n else None for u, (item, _, _) in enumerate(items)}
        self.last = {u % n: item for u, (item, _, _) in enumerate(items)}
        assert len(self.place) == len(items)
        self.full = [Signal(nc, ctx, f"{name}{t}_full", len(range(t, len(items), n))) for t in range(n)]

    def tile(self, item):
        return self.tiles[self.place[item][0]]

    def filled(self, i, item):
        slot, n = self.place[item]
        return self.full[slot](i, n)

    def emptied(self, i, item):
        signal, k = self.read[item]
        return signal(i, k)

    def may_fill(self, i, item):
        if self.before[item] is None:
            return self.read[self.last[self.place[item][0]]][0](i, 0)
        return self.emptied(i, self.before[item])

    def full_sem(self, item):
        return self.full[self.place[item][0]].sem


def groups(narrow):
    return [(ky, c, rows) for ky in range(3) for c in range(CHUNKS) for rows in blocks_of(c, ky, narrow)]


PARTS = [(name,) for name in ("pool", "theta", "pixel", "ctx", "scale")]
PARTS += [(name, x) for x in range(3) for name in ("qkv", "energy", "exp", "log", "lse", "gap", "turn", "out", "mix")]
STEPS_PER_LAYER = 1 + 2 * 3 + 3 * (1 + CHUNKS)
PART_STEP = [1 + k * (2 * STEPS_PER_LAYER - 3) // len(PARTS) for k in range(len(PARTS))]


def parts_at(step, lag):
    return [part for part, at in zip(PARTS, PART_STEP) if at + lag == step]


def build(nc, a, out):
    ctx = ExitStack()
    with ctx:
        def sb(name, shape, dt=F32):
            return ctx.enter_context(nc.sbuf_tensor(name, shape, dt))

        primed = []

        def sig(name, per_pair, reused=False):
            signal = Signal(nc, ctx, name, per_pair, primed=reused)
            if reused:
                primed.append(signal)
            return signal

        work_t = [ctx.enter_context(nc.psum_tensor(f"work{s}_ps", [128, 2, 512], F32)) for s in range(2)]
        att_t = [ctx.enter_context(nc.psum_tensor(f"att{s}_ps", [128, 512], F32)) for s in range(2)]
        ysum = ctx.enter_context(nc.psum_tensor("ysum", [128, 2, 512], F32))

        const = {n: sb(f"{n}_sb", list(v.shape), v.dtype) for n, v in a.items() if n != "x"}
        woff, boff, wdcn, bn = const["woff"], const["boff"], const["wdcn"], const["bn"]
        grid, negq, selp, sele, selx = (const[n] for n in ("grid", "negq", "selp", "sele", "selx"))
        bnw = sb("bnw", [128, 2, 4])
        zero16 = sb("zero16", [128, 512], F16)

        xin = sb("xin", [128, HW])
        xpad = [sb(f"xpad{n}", [128, HP, WP]) for n in range(3)]
        hpad = sb("hpad", [128, HP, WP])
        mpad = sb("mpad", [128, HP, WP])
        coords = sb("coords", [96, HW])
        hatf = [[sb(f"hatf{d}{t}", [120, HW]) for t in range(2)] for d in range(2)]
        haty = [[[sb(f"haty{s}{t}{p}", [120, HW], F16) for p in range(2)] for t in range(2)] for s in range(2)]
        hatx = [[[sb(f"hatx{s}{t}{p}", [120, HW], F16) for p in range(2)] for t in range(2)] for s in range(2)]
        hxe = [[sb(f"hxe{s}{b}", [120, 3, HW]) for b in range(2)] for s in range(2)]
        zt = [sb(f"zt{s}", [120, CHUNKS, TAPS * C]) for s in range(2)]
        prod = [[sb(f"prod{s}{b}", [120, 3, BLOCK_ROWS * W]) for b in range(2)] for s in range(2)]
        shared = sb("shared", [128, HP * W + 3 * HW])
        hmax = shared[:, 0:HP * W].rearrange("p (h w) -> p h w", w=W)
        dil, lgt, lgd = (shared[:, HP * W + n * HW:HP * W + (n + 1) * HW] for n in range(3))
        relu1 = dil
        c2 = lgd
        x3 = sb("x3", [128, HW])
        pl = [sb(f"pl{n}", [128, HW]) for n in range(2)]
        small = sb("small", [128, 24])
        reach = sb("reach", [32, 2, 32])
        wide = sb("wide", [1, 2], mybir.dt.int32)
        ublk = sb("ublk", [128, 128])
        xt = [sb(f"xt{n}", [128, HW]) for n in range(2)]
        xt.append(xt[0])
        xcol = x3[:]
        qs = sb("qs", [64, 2, NG, GP])
        ks = sb("ks", [64, 2, NG, W])
        vs = sb("vs", [GP, 2, NG, 128])
        es = sb("es", [GP, 2, 2 * NG, W])
        pr = sb("pr", [GP, 2, 2 * NG, W])
        st = sb("st", [GP, 5, 4 * NG])
        lset = sb("lset", [4 * NG, GP])
        pb = sb("pb", [GP, 2, 2 * NG, G, W])
        pt = shared[0:GP, 0:4 * NG * GP].rearrange("p (s j n) -> p s j n", s=2, j=2 * NG)
        gap = sb("gap", [128, HW])
        ow = pl
        mix = ow[0]
        ares = [xt[0], xt[1], sb("ares", [128, HW])]
        share = ares[2]

        loaded = ctx.enter_context(nc.semaphore("consts_loaded"))
        s_border = ctx.enter_context(nc.semaphore("borders_set"))
        s_bn = ctx.enter_context(nc.semaphore("bn_step"))
        x_loaded = sig("x_loaded", 16)
        x_padded = sig("x_padded", 1)
        x1_padded = sig("x1_padded", 1)
        coords_raw = sig("coords_raw", 2)
        coords_ready = sig("coords_ready", 2)
        dist_y = sig("dist_y", 8)
        dist_x = sig("dist_x", 8)
        haty_f = sig("haty_f", 8)
        hatx_f = sig("hatx_f", 8)
        haty_hi = sig("haty_hi", 8)
        haty_lo = sig("haty_lo", 8, reused=True)
        hatx_m = sig("hatx_masked", 8)
        hatx_hi = sig("hatx_hi", 8)
        hatx_lo = sig("hatx_lo", 8, reused=True)
        n_groups = len(groups(True))
        n_wide = 2 * len(groups(False))
        per_row = n_groups // 3
        prod_ready = [sig(f"prod{s}_ready", 2 * n_groups, reused=True) for s in range(2)]
        prod_used = sig("prod_used", 2 * (n_groups - 1))
        wide_full = ctx.enter_context(nc.semaphore("wide_spread_full"))
        wide_ready = ctx.enter_context(nc.semaphore("wide_prod_ready"))
        reach_diff = sig("reach_diff", 2)
        reach_rows = sig("reach_rows", 2)
        reach_turned = sig("reach_turned", 2)
        reach_max = sig("reach_max", 2)
        reach_flag = sig("reach_flag", 2)
        mask_exp = sig("mask_exp", 2)
        mask_add = sig("mask_add", 2)
        y_summed = sig("y_summed", 2, reused=True)
        y_read = sig("y_read", 4, reused=True)
        z_ready = sig("z_ready", 4 * CHUNKS)
        hx_ready = sig("hx_ready", 4 * TAPS)
        x2_ready = sig("x2_ready", 1, reused=True)
        lgt_ready = sig("lgt_ready", 1)
        lgd_ready = sig("lgd_ready", 1)
        gate_ready = sig("gate_ready", 1)
        hmax_a = sig("hmax_a", 1)
        hmax_ready = sig("hmax_ready", 1)
        dil_a = sig("dil_a", 1)
        dil_ready = sig("dil_ready", 1)
        h_ready = sig("h_ready", 2, reused=True)
        c2_relu = sig("c2_relu", 2, reused=True)
        c2_gated = sig("c2_gated", 1)
        x3_ready = sig("x3_ready", 1)

        pl_ready = [sig(f"pool_logits{n}", 2) for n in range(2)]
        pl_max = [sig(f"pool_max{n}", 1) for n in range(2)]
        pl_exp = [sig(f"pool_exp{n}", 1) for n in range(2)]
        pl_rcp = [sig(f"pool_rcp{n}", 1) for n in range(2)]
        xs_sum = sig("pooled_sum", 1)
        xs_ready = sig("pooled_ready", 1)
        ctx_ready = sig("ctx_ready", 1)
        sc_exp = sig("scale_exp", 1)
        sc_add = sig("scale_add", 1)
        sc_ready = sig("scale_ready", 1)
        xm_sum = sig("mean_sum", 1)
        xm_ready = sig("mean_ready", 1)
        avg_ready = sig("avg_ready", 1)
        u_ready = sig("theta_ready", 1)
        ublk_ready = sig("theta_spread", 1)
        pp_ready = sig("pixel_softmax", 1)
        pp_step = sig("pixel_gate_step", 2)
        pp_gate = sig("pixel_gate", 1)
        xt_ready = sig("att_input", 3)
        xcol_ready = sig("att_input_by_columns", 3)
        q_ready = sig("q_ready", 12)
        k_ready = sig("k_ready", 3)
        v_ready = sig("v_ready", 12, reused=True)
        e_ready = sig("energy_ready", 6)
        e_max = sig("energy_max", 3)
        e_sub = sig("energy_shifted", 3)
        p_exp = sig("p_exp", 3)
        p_sum = sig("p_sum", 3)
        s_log = sig("sum_log", 3)
        s_rcp = sig("sum_rcp", 3)
        lse_ready = sig("lse_ready", 3)
        lset_ready = sig("lse_rows_ready", 3)
        p_norm = sig("p_normed", 3)
        pb_ready = [sig(f"p{s}_blocks", 3) for s in range(2)]
        pt_ready = [sig(f"p{s}_turned", 9) for s in range(2)]
        d_ready = sig("gap_ready", 6)
        g_step = sig("share_step", 9)
        g_log = sig("share_log", 3)
        g_ready = sig("share_ready", 3)
        o_ready = sig("out_read", 12, reused=True)
        m_diff = sig("mix_diff", 3)
        m_mul = sig("mix_scaled", 3)
        m_add = sig("mix_added", 3)
        a_ready = sig("att_output", 3, reused=True)
        stored = sig("stored", 16, reused=True)

        items = []
        for l in range(2):
            items.append((("offsets", l), coords_raw, l + 1))
            for s in range(2):
                ls = l * 2 + s
                items += [(("z", l, s, c), z_ready, ls * CHUNKS + c + 1) for c in range(CHUNKS)]
                for t in range(2):
                    items += [(("y", l, s, t), dist_y, ls * 2 + t + 1), (("x", l, s, t), dist_x, ls * 2 + t + 1),
                              (("m", l, s, t), hatx_m, ls * 2 + t + 1)]
            for g in range(n_groups):
                if g % per_row == 0:
                    items += [(("hx", l, s, q), hx_ready, ((l * 3 + g // per_row) * 2 + s) * 3 + q % 3 + 1)
                              for s in range(2) for q in range(g // per_row * 3, g // per_row * 3 + 3)]
                items += [(("hy", l, s, g), prod_ready[s], l * n_groups + g + 1) for s in range(2)]
        items += [(("gate",), lgt_ready, 1), (("conv1",), h_ready, 2), (("conv2",), c2_relu, 2)]
        work = Ring(nc, ctx, "work", work_t, items)
        items = [(("pool_logits", h), pl_ready[0], h + 1) for h in range(2)]
        items += [(("avg",), avg_ready, 1), (("theta",), u_ready, 1)]
        items += [(("pixel_logits", h), pl_ready[1], h + 1) for h in range(2)]
        items += [(("ctx",), ctx_ready, 1), (("scale",), sc_exp, 1)]
        dh = [(d, h) for d in range(2) for h in range(2)]
        for x in range(3):
            items += [(("q", x, d, h), q_ready, x * 4 + d * 2 + h + 1) for d, h in dh] + [(("k", x), k_ready, x + 1)]
            items += [(("v", x, d, h), v_ready, x * 4 + d * 2 + h + 1) for d, h in dh]
            items += [(("e", x, s), e_ready, x * 2 + s + 1) for s in range(2)] + [(("lse", x), lset_ready, x + 1)]
            items += [(("d", x, h), d_ready, x * 2 + h + 1) for h in range(2)]
            items += [(("p", x, s, j), pt_ready[s], x * 3 + j + 1) for s in range(2) for j in range(3)]
            items += [(("o", x, d, h), o_ready, x * 4 + d * 2 + h + 1) for d, h in dh]
        att = Ring(nc, ctx, "att", att_t, items)

        n_const = len(const)
        block = ctx.enter_context(nc.Block())

        NMX, SUM, RCP, XS, XR, CTX, SE, SA, SR, XM, XA, AVG, U, BUPN = 0, 2, 4, 6, 7, 8, 9, 10, 11, 12, 13, 14, 15, 16

        def rows(buf, r0, r1):
            return buf[:, r0 + 1:r1 + 1, 1:W + 1]

        def halves(buf):
            return buf.rearrange("p (b n) -> p b n", b=2)

        def grid3(buf):
            return buf.rearrange("p (h w) -> p h w", w=W)

        def y_pieces(r0, r1):
            if r0 < Y_ROWS:
                yield 0, r0 * W, r0, min(r1, Y_ROWS)
            if r1 > Y_ROWS:
                yield 1, (max(r0, Y_ROWS) - Y_ROWS) * W, max(r0, Y_ROWS), r1

        @block.sync
        def _(sp):
            for signal in primed:
                sp.sem_inc(signal.sem, 1)
            for n, t in const.items():
                sp.dma_start(t[:], a[n]).then_inc(loaded, 16)
            sp.dma_start(xin[:], a["x"][0]).then_inc(x_loaded.sem, 16)
            with sp.Fori(0, PAIRS - 1) as n:
                sp.wait_ge(*x2_ready(n, 1))
                sp.dma_start(xin[:], a["x"][n + 1]).then_inc(x_loaded.sem, 16)
                sp.wait_ge(*a_ready(n, 3))
                sp.dma_start(out[n], ares[2][:]).then_inc(stored.sem, 16)
            sp.wait_ge(*a_ready(PAIRS - 1, 3))
            sp.dma_start(out[PAIRS - 1], ares[2][:]).then_inc(stored.sem, 16)
            sp.wait_ge(*stored(PAIRS - 1, 16))

        def run(eng, convolve, attend, lag):
            convolve(0, lambda step: None)
            with eng.Fori(0, PAIRS - 1) as n:
                def between(step):
                    for part in parts_at(step, lag):
                        attend(n, *part)

                convolve(n + 1, between)
            for part in PARTS:
                attend(PAIRS - 1, *part)

        def step_spread(l, s, t):
            return l * STEPS_PER_LAYER + 2 + 3 * s + t

        def step_sum(l, ky, c):
            return l * STEPS_PER_LAYER + 8 + ky * (1 + CHUNKS) + c

        @block.gpsimd
        def _(pool):
            nc.gpsimd.memset(zero16[:], 0.0).then_inc(s_border, 1)
            for buf in (*xpad, hpad):
                nc.gpsimd.memset(buf[:], 0.0).then_inc(s_border, 1)
            nc.gpsimd.memset(mpad[:], MASKED).then_inc(s_border, 1)
            pool.wait_ge(s_border, 6)

            def copy(dst, src):
                nc.gpsimd.nop(nofuse=True)
                return nc.gpsimd.tensor_copy(dst, src)

            def convolve(i, between):
                pool.wait_ge(*x_loaded(i, 16))
                pool.wait_ge(*y_summed(i, 0))
                copy(rows(xpad[0], 0, H), grid3(xin[:])).then_inc(x_padded.sem, 1)
                for l in range(2):
                    if l == 1:
                        pool.wait_ge(*y_read(i, 2))
                        copy(rows(xpad[1], 0, H), grid3(xin[:])).then_inc(x1_padded.sem, 1)
                    between(l * STEPS_PER_LAYER)
                    for s in range(2):
                        between(step_spread(l, s, -1))
                        for t in range(2):
                            n = TILE_ROWS[t]
                            k = (l * 2 + s) * 2 + t + 1
                            hi, lo = haty[s][t]
                            pool.wait_ge(*haty_f(i, k))
                            pool.wait_ge(*y_summed(i, l))
                            copy(hi[0:n, :], hatf[0][t][0:n, :]).then_inc(haty_hi.sem, 1)
                            pool.wait_ge(*haty_hi(i, k))
                            nc.gpsimd.tensor_tensor(lo[0:n, :], hatf[0][t][0:n, :], hi[0:n, :],
                                                    ALU.subtract).then_inc(haty_lo.sem, 1)
                            hi, lo = hatx[s][t]
                            pool.wait_ge(*hatx_m(i, k))
                            copy(hi[0:n, :], hatf[1][t][0:n, :]).then_inc(hatx_hi.sem, 1)
                            pool.wait_ge(*hatx_hi(i, k))
                            nc.gpsimd.tensor_tensor(lo[0:n, :], hatf[1][t][0:n, :], hi[0:n, :],
                                                    ALU.subtract).then_inc(hatx_lo.sem, 1)
                            between(step_spread(l, s, t))
                    for ky in range(3):
                        for c in range(-1, CHUNKS):
                            between(step_sum(l, ky, c))

            def attend(i, part, x=0):
                if part == "qkv":
                    pool.wait_ge(*xt_ready(i, max(2, x + 1)))
                    if x:
                        pool.wait_ge(*v_ready(i, 4 * x))
                    copy(xcol.rearrange("p (w h) -> p h w", h=H), grid3(xt[x][:])).then_inc(xcol_ready.sem, 1)
                if part == "log":
                    pool.wait_ge(*p_norm(i, x + 1))
                    if x:
                        pool.wait_ge(*att.filled(i, ("p", x - 1, 1, 2)))
                    else:
                        pool.wait_ge(*a_ready(i, 0))
                    p_b = pr[:, 1, :, :].unsqueeze(2).broadcast_to([GP, 2 * NG, G, W])
                    k_b = const["blk"][:].unsqueeze(1).broadcast_to([GP, 2 * NG, G, W])
                    nc.gpsimd.tensor_tensor(pb[:, 1], p_b, k_b, ALU.mult).then_inc(pb_ready[1].sem, 1)

            pool.wait_ge(loaded, 16 * n_const)
            run(pool, convolve, attend, 0)

        @block.scalar
        def _(act):
            act.wait_ge(loaded, 16 * n_const)
            act.wait_ge(s_bn, 1)
            nc.scalar.activation(bnw[:, :, 1], bnw[:, :, 0], ACT.Sqrt).then_inc(s_bn, 1)
            act.wait_ge(s_bn, 8)
            nc.scalar.preload_act_table_set("natural_log_exp_and_others")

            def convolve(i, between):
                for l in range(2):
                    act.wait_ge(*coords_raw(i, l + 1))
                    nc.scalar.activation(coords[64:96, :], coords[64:96, :], ACT.Exp, scale=-1.0).then_inc(mask_exp.sem, 1)
                    between(l * STEPS_PER_LAYER)
                    for s in range(2):
                        for c in range(CHUNKS):
                            n = chunk_rows(c) * W
                            item = ("z", l, s, c)
                            act.wait_ge(*work.filled(i, item))
                            act.wait_ge(*y_summed(i, l))
                            nc.scalar.copy(zt[s][0:n, c, :].rearrange("p (b n) -> p b n", b=2),
                                           work.tile(item)[0:n, :, 0:HALF]).then_inc(z_ready.sem, 1)
                        between(step_spread(l, s, -1))
                        for t in range(2):
                            n = TILE_ROWS[t]
                            k = (l * 2 + s) * 2 + t + 1
                            for kind, d, done, d_done in (("y", 0, haty_f, dist_y),
                                                               ("x", 1, hatx_f, dist_x)):
                                item = (kind, l, s, t)
                                act.wait_ge(*work.filled(i, item))
                                act.wait_ge(*(haty_lo if kind == "y" else hatx_lo)(i, max(0, k - 2)))
                                nc.scalar.activation(hatf[d][t][0:n, :].rearrange("p (b n) -> p b n", b=2),
                                                     work.tile(item)[0:n, :, 0:HALF], ACT.Abs,
                                                     bias=negq[0:n, 0:1]).then_inc(d_done.sem, 1)
                                act.wait_ge(*d_done(i, k))
                                nc.scalar.activation(hatf[d][t][0:n, :], hatf[d][t][0:n, :], ACT.Relu,
                                                     bias=negq[0:n, 1:2], scale=-SCALE16).then_inc(done.sem, 1)
                            between(step_spread(l, s, t))
                    for ky in range(3):
                        for s in range(2):
                            for k in range(3 * ky, 3 * ky + 3):
                                item = ("hx", l, s, k)
                                act.wait_ge(*work.filled(i, item))
                                if ky == 2:
                                    act.wait_ge(*prod_ready[s](i, l * n_groups + per_row))
                                else:
                                    act.wait_ge(*prod_ready[s](i, l * n_groups))
                                nc.scalar.copy(halves(hxe[s][ky % 2][:, k % 3, :]),
                                               work.tile(item)[0:120, :, 0:HALF]).then_inc(hx_ready.sem, 1)
                        for c in range(-1, CHUNKS):
                            between(step_sum(l, ky, c))
                    act.wait_ge(*y_summed(i, l + 1))
                    for bank, c0, r0, r1 in y_pieces(0, H):
                        nc.scalar.activation((xin, relu1)[l][:, r0 * W:r1 * W], ysum[:, bank, c0:c0 + (r1 - r0) * W],
                                             ACT.Relu, bias=bnw[:, l, 3:4], scale=bnw[:, l, 2:3]).then_inc(y_read.sem, 1)

            def softmax_exp(i, n, name):
                for h in range(2):
                    item = (name, h)
                    act.wait_ge(*att.filled(i, item))
                    nc.scalar.copy(pl[n][:, h * HALF:(h + 1) * HALF], att.tile(item)[:, 0:HALF]).then_inc(pl_ready[n].sem, 1)
                act.wait_ge(*pl_max[n](i, 1))
                nc.scalar.activation(pl[n][:], pl[n][:], ACT.Exp, bias=small[:, NMX + n:NMX + n + 1],
                                     accum_out=small[:, SUM + n:SUM + n + 1]).then_inc(pl_exp[n].sem, 1)

            def attend(i, part, x=0):
                if part == "pool":
                    softmax_exp(i, 0, "pool_logits")
                if part == "pixel":
                    softmax_exp(i, 1, "pixel_logits")
                if part == "scale":
                    act.wait_ge(*att.filled(i, ("scale",)))
                    nc.scalar.activation(small[:, SE:SE + 1], att.tile(("scale",))[:, 0:1], ACT.Exp,
                                         bias=small[:, BUPN:BUPN + 1], scale=-1.0).then_inc(sc_exp.sem, 1)
                    act.wait_ge(*pp_ready(i, 1))
                    nc.scalar.activation(pl[1][:], pl[1][:], ACT.Exp, scale=-1.0).then_inc(pp_step.sem, 1)
                    act.wait_ge(*pp_step(i, 1))
                    nc.scalar.activation(pl[1][:], pl[1][:], ACT.Ln, bias=1.0).then_inc(pp_step.sem, 1)
                    act.wait_ge(*pp_step(i, 2))
                    nc.scalar.activation(pl[1][:], pl[1][:], ACT.Exp, scale=-1.0).then_inc(pp_gate.sem, 1)
                if part == "qkv":
                    act.wait_ge(*att.filled(i, ("k", x)))
                    nc.scalar.activation(ks[:].rearrange("p d g v -> p (d g v)"), att.tile(("k", x))[0:64, 0:2 * NG * W],
                                         ACT.Identity, bias=const["bk"][:, 0:1]).then_inc(k_ready.sem, 1)
                    for d in range(2):
                        for h in range(2):
                            item = ("v", x, d, h)
                            act.wait_ge(*att.filled(i, item))
                            nc.scalar.copy(vs[:, d, 3 * h:3 * h + 3, :],
                                           att.tile(item)[0:GP, 0:384].rearrange("p (g c) -> p g c", g=3)).then_inc(v_ready.sem, 1)
                if part == "energy":
                    act.wait_ge(*e_sub(i, x + 1))
                    nc.scalar.activation(pr[:], es[:], ACT.Exp).then_inc(p_exp.sem, 1)
                if part == "exp":
                    act.wait_ge(*p_sum(i, x + 1))
                    nc.scalar.activation(st[:, 2, :], st[:, 1, :], ACT.Ln).then_inc(s_log.sem, 1)
                if part == "gap":
                    act.wait_ge(*d_ready(i, 2 * x + 2))
                    if x == 0:
                        act.wait_ge(*stored(i, 0))
                    nc.scalar.activation(share[:], gap[:], ACT.Abs).then_inc(g_step.sem, 1)
                    act.wait_ge(*g_step(i, 3 * x + 1))
                    nc.scalar.activation(share[:], share[:], ACT.Exp, scale=-1.0).then_inc(g_step.sem, 1)
                    act.wait_ge(*g_step(i, 3 * x + 2))
                    nc.scalar.activation(share[:], share[:], ACT.Ln, bias=1.0).then_inc(g_step.sem, 1)
                if part == "turn":
                    for j in range(3):
                        item = ("p", x, 1, j)
                        act.wait_ge(*att.filled(i, item))
                        nc.scalar.copy(pt[:, 1, 4 * j:4 * j + 4, :],
                                       att.tile(item)[0:GP, 0:384].rearrange("p (g c) -> p g c", g=4)).then_inc(pt_ready[1].sem, 1)
                if part == "out":
                    act.wait_ge(*g_log(i, x + 1))
                    nc.scalar.activation(share[:], share[:], ACT.Exp).then_inc(g_ready.sem, 1)
                    for d in range(2):
                        for h in range(2):
                            item = ("o", x, d, h)
                            src = att.tile(item)[:, 0:HALF]
                            dst = ow[d][:, h * HALF:(h + 1) * HALF]
                            if d == 1:
                                src = src.rearrange("p (w h) -> p h w", h=H)
                                dst = grid3(ow[1][:])[:, :, h * (W // 2):(h + 1) * (W // 2)]
                            act.wait_ge(*att.filled(i, item))
                            nc.scalar.activation(dst, src, ACT.Identity, bias=const["bv"][:, 0:1]).then_inc(o_ready.sem, 1)

            run(act, convolve, attend, 0)

        @block.vector
        def _(dve):
            def w(pair):
                dve.wait_ge(*pair)

            dve.wait_ge(loaded, 16 * n_const)
            v = nc.vector
            v.tensor_scalar(bnw[:, :, 0], bn[:, :, 4], EPS, None, ALU.add).then_inc(s_bn, 1)
            dve.wait_ge(s_bn, 2)
            v.reciprocal(bnw[:, :, 0], bnw[:, :, 1]).then_inc(s_bn, 1)
            dve.wait_ge(s_bn, 3)
            v.tensor_tensor(bnw[:, :, 2], bnw[:, :, 0], bn[:, :, 1], ALU.mult).then_inc(s_bn, 1)
            dve.wait_ge(s_bn, 4)
            v.tensor_tensor(bnw[:, :, 1], bn[:, :, 0], bn[:, :, 3], ALU.subtract).then_inc(s_bn, 1)
            dve.wait_ge(s_bn, 5)
            v.tensor_tensor(bnw[:, :, 1], bnw[:, :, 1], bnw[:, :, 2], ALU.mult).then_inc(s_bn, 1)
            dve.wait_ge(s_bn, 6)
            v.tensor_tensor(bnw[:, :, 3], bnw[:, :, 1], bn[:, :, 2], ALU.add).then_inc(s_bn, 1)
            v.tensor_scalar(small[:, BUPN:BUPN + 1], const["bup"][:], -1.0, None, ALU.mult).then_inc(s_bn, 1)

            v.memset(reach[:], 0.0).then_inc(s_bn, 1)
            dve.wait_ge(s_bn, 9)
            wide_runs = dve.alloc_register("wide_runs_dve")
            dve.reg_mov(wide_runs, 0)

            def multiply(i, l, s, g, narrow, item):
                ky, c, (r0, r1) = groups(narrow)[g]
                n = (r1 - r0) * W
                m = chunk_rows(c) * W
                return v.tensor_tensor(prod[s][g % 2][0:m, :, 0:n],
                                       work.tile(item).rearrange("p b n -> p (b n)").rearrange(
                                           "p (t n) -> p t n", n=SEG)[0:m, 0:3, 0:n],
                                       hxe[s][ky % 2][0:m, :, r0 * W:r1 * W], ALU.mult)

            def convolve(i, between):
                for l in range(2):
                    item = ("offsets", l)
                    w(work.filled(i, item))
                    v.scalar_tensor_tensor(out=coords[:].rearrange("p (b n) -> p b n", b=2),
                                           in0=work.tile(item)[0:96, :, 0:HALF], scalar=boff[:, l:l + 1],
                                           in1=grid[:].rearrange("p (b n) -> p b n", b=2),
                                           op0=ALU.add, op1=ALU.add).then_inc(coords_raw.sem, 1)
                    w(coords_raw(i, l + 1))
                    dev = prod[0][0][0:32].rearrange("p q n -> p (q n)")[:, 0:HW]
                    v.tensor_tensor(dev, coords[0:32, :], grid[0:32, :], ALU.subtract).then_inc(reach_diff.sem, 1)
                    w(reach_diff(i, l + 1))
                    v.tensor_reduce(reach[:, 0, 0:1], dev, AX, ALU.max, apply_absolute_value=True).then_inc(reach_rows.sem, 1)
                    w(reach_rows(i, l + 1))
                    v.transpose(reach[:, 1, :], reach[:, 0, :]).then_inc(reach_turned.sem, 1)
                    w(reach_turned(i, l + 1))
                    v.tensor_reduce(reach[0:1, 0, 1:2], reach[0:1, 1, :], AX, ALU.max).then_inc(reach_max.sem, 1)
                    w(reach_max(i, l + 1))
                    v.tensor_scalar(wide[0:1, l:l + 1], reach[0:1, 0, 1:2], REACH - 0.01, None, ALU.is_gt).then_inc(reach_flag.sem, 1)
                    w(mask_exp(i, l + 1))
                    v.tensor_scalar(coords[64:96, :], coords[64:96, :], 1.0, None, ALU.add).then_inc(mask_add.sem, 1)
                    w(mask_add(i, l + 1))
                    v.reciprocal(coords[64:96, :], coords[64:96, :]).then_inc(coords_ready.sem, 1)
                    between(l * STEPS_PER_LAYER)
                    for s in range(2):
                        between(step_spread(l, s, -1))
                        for t in range(2):
                            n = TILE_ROWS[t]
                            k = (l * 2 + s) * 2 + t + 1
                            item = ("m", l, s, t)
                            w(work.filled(i, item))
                            w(hatx_f(i, k))
                            v.tensor_tensor(hatf[1][t][0:n, :].rearrange("p (b n) -> p b n", b=2),
                                            work.tile(item)[0:n, :, 0:HALF],
                                            hatf[1][t][0:n, :].rearrange("p (b n) -> p b n", b=2),
                                            ALU.mult).then_inc(hatx_m.sem, 1)
                            between(step_spread(l, s, t))
                    w(reach_flag(i, l + 1))
                    dve.nop(nofuse=True)
                    is_wide = dve.value_load(wide[0:1, l:l + 1], min_val=0, max_val=1)
                    with dve.If(is_wide != 0):
                        runs = dve.snap(wide_runs)
                        for g, (ky, c, _) in enumerate(groups(False)):
                            row, at = divmod(g, n_wide // 6)
                            for s in range(2):
                                w((wide_full, runs * n_wide + 2 * g + s + 1))
                                if at == 0:
                                    w(work.emptied(i, ("hx", l, s, 3 * ky + 2)))
                                multiply(i, l, s, g, False, ("hy", l, s, 0)).then_inc(wide_ready, 1)
                            if at == 0:
                                between(step_sum(l, ky, -1))
                            if g + 1 == len(groups(False)) or groups(False)[g + 1][1] != c:
                                between(step_sum(l, ky, c))
                            if at == n_wide // 6 - 1:
                                w((wide_ready, runs * n_wide + 2 * g + 2))
                                for s in range(2):
                                    dve.sem_inc(prod_ready[s].sem, per_row)
                        dve.reg_add(wide_runs, wide_runs, 1)
                    with dve.Else():
                        for g, (ky, c, _) in enumerate(groups(True)):
                            if g % per_row == 0:
                                between(step_sum(l, ky, -1))
                            for s in range(2):
                                item = ("hy", l, s, g)
                                w(work.filled(i, item))
                                if g % per_row == 0:
                                    w(work.emptied(i, ("hx", l, s, 3 * ky + 2)))
                                if g >= 2:
                                    w(prod_used(i, l * (n_groups - 1) + g - 1))
                                multiply(i, l, s, g, True, item).then_inc(prod_ready[s].sem, 1)
                            between(step_sum(l, ky, c))
                w(y_read(i, 4))
                v.tensor_tensor(rows(xpad[2], 0, H), grid3(xin[:]), grid3(relu1), ALU.add).then_inc(x2_ready.sem, 1)
                w(work.filled(i, ("gate",)))
                v.tensor_scalar(halves(lgt), work.tile(("gate",))[:, :, 0:HALF], const["bm"][:, 0:1], None,
                                ALU.add).then_inc(lgt_ready.sem, 1)
                w(lgt_ready(i, 1))
                v.scalar_tensor_tensor(out=lgd, in0=lgt, scalar=0.0, in1=lgt,
                                       op0=ALU.is_gt, op1=ALU.subtract).then_inc(lgd_ready.sem, 1)
                w(lgd_ready(i, 1))
                v.tensor_tensor(rows(mpad, 0, H), grid3(lgt), grid3(lgd), ALU.add).then_inc(gate_ready.sem, 1)
                w(gate_ready(i, 1))
                v.tensor_tensor(hmax, mpad[:, :, 0:W], mpad[:, :, 1:W + 1], ALU.max).then_inc(hmax_a.sem, 1)
                w(hmax_a(i, 1))
                v.tensor_tensor(hmax, hmax, mpad[:, :, 2:W + 2], ALU.max).then_inc(hmax_ready.sem, 1)
                w(hmax_ready(i, 1))
                v.tensor_tensor(grid3(dil), hmax[:, 0:H, :], hmax[:, 1:H + 1, :], ALU.max).then_inc(dil_a.sem, 1)
                w(dil_a(i, 1))
                v.tensor_tensor(grid3(dil), grid3(dil), hmax[:, 2:H + 2, :], ALU.max).then_inc(dil_ready.sem, 1)
                w(dil_ready(i, 1))
                w(work.filled(i, ("conv1",)))
                for h in range(2):
                    v.scalar_tensor_tensor(out=rows(hpad, h * HR, (h + 1) * HR),
                                           in0=grid3(work.tile(("conv1",))[:, h, 0:HALF]), scalar=0.0,
                                           in1=grid3(dil[:, h * HALF:(h + 1) * HALF]),
                                           op0=ALU.max, op1=ALU.mult).then_inc(h_ready.sem, 1)
                w(work.filled(i, ("conv2",)))
                w(gate_ready(i, 1))
                for h in range(2):
                    v.scalar_tensor_tensor(out=grid3(c2[:, h * HALF:(h + 1) * HALF]),
                                           in0=grid3(work.tile(("conv2",))[:, h, 0:HALF]), scalar=0.0,
                                           in1=rows(mpad, h * HR, (h + 1) * HR),
                                           op0=ALU.max, op1=ALU.mult).then_inc(c2_relu.sem, 1)
                w(c2_relu(i, 2))
                v.tensor_tensor(grid3(c2), grid3(c2), rows(mpad, 0, H), ALU.mult).then_inc(c2_gated.sem, 1)
                w(c2_gated(i, 1))
                w(v_ready(i, 0))
                v.tensor_tensor(grid3(x3[:]), grid3(c2), rows(xpad[2], 0, H), ALU.add).then_inc(x3_ready.sem, 1)
                w(x3_ready(i, 1))

                v.tensor_reduce(small[:, XM:XM + 1], x3[:], AX, ALU.add).then_inc(xm_sum.sem, 1)
                w(xm_sum(i, 1))
                v.tensor_scalar(small[:, XA:XA + 1], small[:, XM:XM + 1], 1.0 / HW, None, ALU.mult).then_inc(xm_ready.sem, 1)

            def softmax_max(i, n):
                w(pl_ready[n](i, 2))
                v.tensor_reduce(small[:, NMX + n:NMX + n + 1], pl[n][:], AX, ALU.max, negate=True).then_inc(pl_max[n].sem, 1)

            def attend(i, part, x=0):
                if part == "pool":
                    softmax_max(i, 0)
                    w(att.filled(i, ("avg",)))
                    v.tensor_copy(small[0:2 * CM, AVG:AVG + 1], att.tile(("avg",))[0:2 * CM, 0:1]).then_inc(avg_ready.sem, 1)
                if part == "theta":
                    w(att.filled(i, ("theta",)))
                    v.tensor_copy(small[:, U:U + 1], att.tile(("theta",))[:, 0:1]).then_inc(u_ready.sem, 1)
                    w(u_ready(i, 1))
                    v.tensor_scalar(ublk[:], const["oneb"][:], small[:, U:U + 1], None, ALU.mult).then_inc(ublk_ready.sem, 1)
                if part == "pixel":
                    w(pl_exp[0](i, 1))
                    v.tensor_tensor_reduce(out=lgt, in0=x3[:], in1=pl[0][:], scale=1.0, scalar=0.0,
                                           op0=ALU.mult, op1=ALU.add, accum_out=small[:, XS:XS + 1]).then_inc(xs_sum.sem, 1)
                    v.reciprocal(small[:, RCP:RCP + 1], small[:, SUM:SUM + 1]).then_inc(pl_rcp[0].sem, 1)
                    w(xs_sum(i, 1))
                    w(pl_rcp[0](i, 1))
                    v.tensor_tensor(small[:, XR:XR + 1], small[:, XS:XS + 1], small[:, RCP:RCP + 1],
                                    ALU.mult).then_inc(xs_ready.sem, 1)
                    softmax_max(i, 1)
                if part == "ctx":
                    w(att.filled(i, ("ctx",)))
                    v.tensor_copy(small[0:2 * CM, CTX:CTX + 1], att.tile(("ctx",))[0:2 * CM, 0:1]).then_inc(ctx_ready.sem, 1)
                    w(pl_exp[1](i, 1))
                    v.reciprocal(small[:, RCP + 1:RCP + 2], small[:, SUM + 1:SUM + 2]).then_inc(pl_rcp[1].sem, 1)
                    w(pl_rcp[1](i, 1))
                    v.tensor_scalar(pl[1][:], pl[1][:], small[:, RCP + 1:RCP + 2], None, ALU.mult).then_inc(pp_ready.sem, 1)
                if part == "scale":
                    w(sc_exp(i, 1))
                    v.tensor_scalar(small[:, SA:SA + 1], small[:, SE:SE + 1], 1.0, None, ALU.add).then_inc(sc_add.sem, 1)
                    w(sc_add(i, 1))
                    v.reciprocal(small[:, SR:SR + 1], small[:, SA:SA + 1]).then_inc(sc_ready.sem, 1)
                    w(sc_ready(i, 1))
                    v.tensor_scalar(xt[0][:], x3[:], small[:, SR:SR + 1], None, ALU.mult).then_inc(xt_ready.sem, 1)
                    w(pp_gate(i, 1))
                    v.tensor_tensor(xt[1][:], x3[:], pl[1][:], ALU.mult).then_inc(xt_ready.sem, 1)

                if part == "qkv":
                    for d in range(2):
                        for h in range(2):
                            item = ("q", x, d, h)
                            w(att.filled(i, item))
                            v.tensor_tensor(qs[:, d, 3 * h:3 * h + 3, :],
                                            att.tile(item)[0:64, 0:HALF].rearrange("p (g n) -> p g n", g=3),
                                            const["bq"][:].unsqueeze(1).broadcast_to([64, 3, GP]),
                                            ALU.add).then_inc(q_ready.sem, 1)
                flat = es[:].rearrange("p s j v -> p (s j) v")
                probs = pr[:].rearrange("p s j v -> p (s j) v")
                if part == "energy":
                    for s in range(2):
                        item = ("e", x, s)
                        w(att.filled(i, item))
                        v.tensor_tensor(es[:, s].rearrange("p (d g) v -> p d g v", d=2),
                                        att.tile(item)[0:GP, 0:HALF].rearrange("p (d g v) -> p d g v", d=2, g=NG),
                                        const["emask"][:].unsqueeze(2).broadcast_to([GP, 2, NG, W]), ALU.add).then_inc(e_ready.sem, 1)
                    w(e_ready(i, 2 * x + 2))
                    v.tensor_reduce(st[:, 0, :], flat, AX, ALU.max).then_inc(e_max.sem, 1)
                    w(e_max(i, x + 1))
                    v.tensor_tensor(flat, flat, st[:, 0, :].unsqueeze(2).broadcast_to([GP, 4 * NG, W]),
                                    ALU.subtract).then_inc(e_sub.sem, 1)
                if part == "exp":
                    w(p_exp(i, x + 1))
                    v.tensor_reduce(st[:, 1, :], probs, AX, ALU.add).then_inc(p_sum.sem, 1)
                    w(p_sum(i, x + 1))
                    v.reciprocal(st[:, 4, :], st[:, 1, :]).then_inc(s_rcp.sem, 1)
                if part == "log":
                    w(s_log(i, x + 1))
                    v.tensor_tensor(st[:, 3, :], st[:, 0, :], st[:, 2, :], ALU.add).then_inc(lse_ready.sem, 1)
                    w(s_rcp(i, x + 1))
                    v.tensor_tensor(probs, probs, st[:, 4, :].unsqueeze(2).broadcast_to([GP, 4 * NG, W]),
                                    ALU.mult).then_inc(p_norm.sem, 1)
                    w(p_norm(i, x + 1))
                    v.tensor_tensor(pb[:, 0], pr[:, 0].unsqueeze(2).broadcast_to([GP, 2 * NG, G, W]),
                                    const["blk"][:].unsqueeze(1).broadcast_to([GP, 2 * NG, G, W]),
                                    ALU.mult).then_inc(pb_ready[0].sem, 1)
                if part == "lse":
                    w(att.filled(i, ("lse", x)))
                    v.tensor_copy(lset[:], att.tile(("lse", x))[0:4 * NG, 0:GP]).then_inc(lset_ready.sem, 1)
                if part == "gap":
                    for h in range(2):
                        item = ("d", x, h)
                        w(att.filled(i, item))
                        v.tensor_copy(gap[:, h * HALF:(h + 1) * HALF], att.tile(item)[:, 0:HALF]).then_inc(d_ready.sem, 1)
                if part == "turn":
                    for j in range(3):
                        item = ("p", x, 0, j)
                        w(att.filled(i, item))
                        v.tensor_copy(pt[:, 0, 4 * j:4 * j + 4, :],
                                      att.tile(item)[0:GP, 0:384].rearrange("p (g c) -> p g c", g=4)).then_inc(pt_ready[0].sem, 1)
                    w(g_step(i, 3 * x + 3))
                    v.scalar_tensor_tensor(out=share[:], in0=gap[:], scalar=0.0, in1=share[:],
                                           op0=ALU.min, op1=ALU.subtract).then_inc(g_log.sem, 1)
                if part == "mix":
                    w(o_ready(i, 4 * x + 4))
                    v.tensor_tensor(mix[:], ow[0][:], ow[1][:], ALU.subtract).then_inc(m_diff.sem, 1)
                    w(m_diff(i, x + 1))
                    w(g_ready(i, x + 1))
                    v.tensor_tensor(mix[:], mix[:], share[:], ALU.mult).then_inc(m_mul.sem, 1)
                    w(m_mul(i, x + 1))
                    v.tensor_tensor(mix[:], mix[:], ow[1][:], ALU.add).then_inc(m_add.sem, 1)
                    w(m_add(i, x + 1))
                    v.scalar_tensor_tensor(out=ares[x][:], in0=mix[:], scalar=const["gamma"][:, 0:1], in1=xt[x][:],
                                           op0=ALU.mult, op1=ALU.add).then_inc(a_ready.sem, 1)
                    if x == 1:
                        w(a_ready(i, 2))
                        v.tensor_tensor(xt[2][:], ares[0][:], ares[1][:], ALU.add).then_inc(xt_ready.sem, 1)

            run(dve, convolve, attend, 0)

        @block.tensor
        def _(pe):
            mm = nc.tensor.matmul

            def w(pair):
                pe.wait_ge(*pair)

            w((s_border, 6))
            w((loaded, 16 * n_const))

            wide_runs = pe.alloc_register("wide_runs_pe")
            pe.reg_mov(wide_runs, 0)

            def conv(i, item, weights, src, m):
                w(work.may_fill(i, item))
                for h in range(2):
                    for k in range(TAPS):
                        r = k // 3 + h * HR
                        last = mm(work.tile(item)[0:m, h, 0:HALF], weights[:, k, :],
                                  src[:, r:r + HR, k % 3:k % 3 + W], start=(k == 0), stop=(k == TAPS - 1))
                last.then_inc(work.full_sem(item), 1)

            def spread_x(i, l, ky):
                for s in range(2):
                    w(hatx_lo(i, (l * 2 + s) * 2 + 2))
                    for k in range(3 * ky, 3 * ky + 3):
                        item = ("hx", l, s, k)
                        t = k // T0
                        n = TILE_ROWS[t]
                        w(work.may_fill(i, item))
                        for h in range(2):
                            for part in range(2):
                                last = mm(work.tile(item)[0:120, h, 0:HALF], selx[0:n, k, :],
                                          hatx[s][t][part][0:n, h * HALF:(h + 1) * HALF],
                                          start=(part == 0), stop=(part == 1))
                        last.then_inc(work.full_sem(item), 1)

            def spread_y(s, g, narrow, slot):
                ky, c, (r0, r1) = groups(narrow)[g]
                n = (r1 - r0) * W
                m = chunk_rows(c) * W
                slot = slot.rearrange("p b n -> p (b n)")
                for q in range(3):
                    t, kl = divmod(3 * ky + q, T0)
                    first = (kl * H + c * CR) * W
                    for part in range(2):
                        last = mm(slot[0:m, q * SEG:q * SEG + n], sele[0:TILE_ROWS[t], first:first + m],
                                  haty[s][t][part][0:TILE_ROWS[t], r0 * W:r1 * W],
                                  start=(part == 0), stop=(part == 1), skip_group_check=True)
                return last

            def add_up(g, narrow):
                ky, c, (r0, r1) = groups(narrow)[g]
                m = chunk_rows(c) * W
                for q in range(3):
                    k = 3 * ky + q
                    for bank, c0, a0, a1 in y_pieces(r0, r1):
                        for s in range(2):
                            last = mm(ysum[s * C:(s + 1) * C, bank, c0:c0 + (a1 - a0) * W],
                                      zt[s][0:m, c, k * C:(k + 1) * C],
                                      prod[s][g % 2][0:m, q, (a0 - r0) * W:(a1 - r0) * W],
                                      start=False, stop=True, skip_group_check=True)
                return last

            def convolve(i, between):
                for l in range(2):
                    if l == 0:
                        w(x_padded(i, 1))
                    else:
                        w(y_read(i, 2))
                        w(x1_padded(i, 1))
                    conv(i, ("offsets", l), woff[:, l], xpad[l], 96)
                    between(l * STEPS_PER_LAYER)
                    for s in range(2):
                        for c in range(CHUNKS):
                            item = ("z", l, s, c)
                            n = chunk_rows(c) * W
                            w(work.may_fill(i, item))
                            for h in range(2):
                                last = mm(work.tile(item)[0:n, h, 0:HALF],
                                          xin[s * C:(s + 1) * C, c * CR * W:c * CR * W + n],
                                          wdcn[s * C:(s + 1) * C, l, h * HALF:(h + 1) * HALF], start=True, stop=True)
                            last.then_inc(work.full_sem(item), 1)
                        between(step_spread(l, s, -1))
                        if s == 0:
                            w(coords_ready(i, l + 1))
                        for t in range(2):
                            n = TILE_ROWS[t]
                            for kind, name in enumerate(("y", "x", "m")):
                                item = (name, l, s, t)
                                w(work.may_fill(i, item))
                                for h in range(2):
                                    last = mm(work.tile(item)[0:n, h, 0:HALF], selp[:, s, t, kind, 0:n],
                                              coords[:, h * HALF:(h + 1) * HALF], start=True, stop=True)
                                last.then_inc(work.full_sem(item), 1)
                            between(step_spread(l, s, t))
                    w(y_read(i, 2 * l))
                    mm(ysum[:, 0, 0:Y_ROWS * W], zero16[:, 0:128], zero16[:, 0:Y_ROWS * W], start=True, stop=True)
                    mm(ysum[:, 1, 0:(H - Y_ROWS) * W], zero16[:, 0:128], zero16[:, 0:(H - Y_ROWS) * W], start=True, stop=True)
                    w(haty_lo(i, l * 4 + 4))
                    w(z_ready(i, (l + 1) * 2 * CHUNKS))
                    w(reach_flag(i, l + 1))
                    pe.nop(nofuse=True)
                    is_wide = pe.value_load(wide[0:1, l:l + 1], min_val=0, max_val=1)
                    with pe.If(is_wide != 0):
                        runs = pe.snap(wide_runs)
                        steps = groups(False)
                        for g, (ky, c, _) in enumerate(steps):
                            row, at = divmod(g, n_wide // 6)
                            if at == 0:
                                spread_x(i, l, ky)
                                between(step_sum(l, ky, -1))
                                for s in range(2):
                                    w(work.may_fill(i, ("hy", l, s, row * per_row)))
                            else:
                                w((wide_ready, runs * n_wide + 2 * g))
                            for s in range(2):
                                spread_y(s, g, False, work.tile(("hy", l, s, 0))).then_inc(wide_full, 1)
                            w((wide_ready, runs * n_wide + 2 * g + 2))
                            last = add_up(g, False)
                            if g == len(steps) - 1:
                                last.then_inc(y_summed.sem, 1)
                            if at == n_wide // 6 - 1:
                                for full in work.full:
                                    pe.sem_inc(full.sem, per_row)
                            if g + 1 == len(steps) or steps[g + 1][1] != c:
                                between(step_sum(l, ky, c))
                        pe.sem_inc(prod_used.sem, n_groups - 1)
                        pe.reg_add(wide_runs, wide_runs, 1)
                    with pe.Else():
                        steps = groups(True)
                        for g in range(n_groups + 1):
                            if g < n_groups:
                                ky, c, _ = steps[g]
                                if g % per_row == 0:
                                    spread_x(i, l, ky)
                                    between(step_sum(l, ky, -1))
                                for s in range(2):
                                    item = ("hy", l, s, g)
                                    w(work.may_fill(i, item))
                                    spread_y(s, g, True, work.tile(item)).then_inc(work.full_sem(item), 1)
                            if g > 0:
                                for s in range(2):
                                    w(prod_ready[s](i, l * n_groups + g))
                                add_up(g - 1, True).then_inc((prod_used if g < n_groups else y_summed).sem, 1)
                            if g < n_groups:
                                between(step_sum(l, ky, c))

                w(x2_ready(i, 1))
                w(work.may_fill(i, ("gate",)))
                for h in range(2):
                    last = mm(work.tile(("gate",))[:, h, 0:HALF], const["wm"][:],
                              xpad[2][:, 1 + h * HR:1 + (h + 1) * HR, 1:W + 1], start=True, stop=True)
                last.then_inc(work.full_sem(("gate",)), 1)
                conv(i, ("conv1",), const["w1"], xpad[2], 128)
                w(h_ready(i, 2))
                conv(i, ("conv2",), const["w2"], hpad, 128)

            def one(i, item, lhsT, rhs, m):
                w(att.may_fill(i, item))
                mm(att.tile(item)[0:m, 0:rhs.shape[-1]], lhsT, rhs, start=True, stop=True).then_inc(att.full_sem(item), 1)

            def attend(i, part, x=0):
                if part == "pool":
                    w(x3_ready(i, 1))
                    for h in range(2):
                        one(i, ("pool_logits", h), const["wqr"][:], x3[:, h * HALF:(h + 1) * HALF], 128)
                    w(xm_ready(i, 1))
                    one(i, ("avg",), const["wql"][:], small[:, XA:XA + 1], 2 * CM)
                if part == "theta":
                    w(avg_ready(i, 1))
                    one(i, ("theta",), const["wvl"][:], small[0:2 * CM, AVG:AVG + 1], 128)
                if part == "pixel":
                    w(ublk_ready(i, 1))
                    for h in range(2):
                        one(i, ("pixel_logits", h), ublk[:], x3[:, h * HALF:(h + 1) * HALF], 128)
                if part == "ctx":
                    w(xs_ready(i, 1))
                    one(i, ("ctx",), const["wvr"][:], small[:, XR:XR + 1], 2 * CM)
                if part == "scale":
                    w(ctx_ready(i, 1))
                    one(i, ("scale",), const["wup"][:], small[0:2 * CM, CTX:CTX + 1], 128)
                if part == "qkv":
                    src = xt[x][:]
                    views = (src.rearrange("p (g r n) -> p g r n", r=G, n=W),
                             src.rearrange("p (n g r) -> p g r n", r=G, g=NG))
                    w(xt_ready(i, x + 1))
                    for d, h in dh:
                        item = ("q", x, d, h)
                        w(att.may_fill(i, item))
                        dst = att.tile(item)[0:64, 0:HALF].rearrange("p (g r n) -> p g r n", g=3, r=G)
                        for r in range(G):
                            last = mm(dst[:, :, r, :], const["wq"][:, r, :], views[d][:, 3 * h:3 * h + 3, r, :],
                                      start=True, stop=True, skip_group_check=True)
                        last.then_inc(att.full_sem(item), 1)
                    item = ("k", x)
                    w(att.may_fill(i, item))
                    for d in range(2):
                        for r in range(G):
                            last = mm(att.tile(item)[0:64, d * NG * W:(d + 1) * NG * W].rearrange("p (g n) -> p g n", g=NG),
                                      const["wk"][:, r, :], views[d][:, :, r, :], start=(r == 0), stop=(r == G - 1),
                                      skip_group_check=True)
                    last.then_inc(att.full_sem(item), 1)
                    w(xcol_ready(i, x + 1))
                    for d, h in dh:
                        item = ("v", x, d, h)
                        w(att.may_fill(i, item))
                        for g in range(3):
                            last = mm(att.tile(item)[0:GP, g * 128:(g + 1) * 128], (src, xcol)[d][:, (3 * h + g) * GP:(3 * h + g + 1) * GP], const["wv"][:],
                                      start=True, stop=True, skip_group_check=True)
                        last.then_inc(att.full_sem(item), 1)
                if part == "energy":
                    w(q_ready(i, 4 * x + 4))
                    w(k_ready(i, x + 1))
                    for s in range(2):
                        item = ("e", x, s)
                        w(att.may_fill(i, item))
                        for d in range(2):
                            for g in range(NG):
                                j = d * NG + g
                                last = mm(att.tile(item)[0:GP, j * W:(j + 1) * W], qs[s * 32:(s + 1) * 32, d, g, :],
                                          ks[s * 32:(s + 1) * 32, d, g, :], start=True, stop=True, skip_group_check=True)
                        last.then_inc(att.full_sem(item), 1)
                if part == "lse":
                    item = ("lse", x)
                    w(lse_ready(i, x + 1))
                    w(att.may_fill(i, item))
                    nc.tensor.transpose(att.tile(item)[0:4 * NG, 0:GP], st[:, 3, :], const["ident"][:]).then_inc(att.full_sem(item), 1)
                if part == "gap":
                    w(lset_ready(i, x + 1))
                    for h in range(2):
                        item = ("d", x, h)
                        w(att.may_fill(i, item))
                        sums = att.tile(item)[:, 0:HALF]
                        mm(sums, zero16[:, 0:128], zero16[:, 0:HALF], start=True, stop=True)
                        for g in range(3):
                            mm(sums[:, g * GP:(g + 1) * GP], const["pick"][:, 3 * h + g, :], lset[:],
                               start=False, stop=True, skip_group_check=True)
                        for g in range(NG):
                            last = mm(grid3(sums)[:, :, g * G:(g + 1) * G], const["pick"][:, NG + g, :],
                                      lset[:].rearrange("p (r n) -> p n r", r=G)[:, h * HR:(h + 1) * HR, :],
                                      start=False, stop=True, skip_group_check=True)
                        last.then_inc(att.full_sem(item), 1)
                if part == "turn":
                    for s in range(2):
                        w(pb_ready[s](i, x + 1))
                        for j in range(3):
                            item = ("p", x, s, j)
                            w(att.may_fill(i, item))
                            for q in range(4):
                                last = nc.tensor.transpose(att.tile(item)[0:GP, q * GP:(q + 1) * GP],
                                                           pb[:, s, 4 * j + q].rearrange("p r v -> p (r v)"), const["ident"][:])
                            last.then_inc(att.full_sem(item), 1)
                if part == "out":
                    w(v_ready(i, 4 * x + 4))
                    for s in range(2):
                        w(pt_ready[s](i, 3 * x + 3))
                    for d, h in dh:
                        item = ("o", x, d, h)
                        w(att.may_fill(i, item))
                        for g in range(3):
                            for s in range(2):
                                j = 3 * h + g
                                last = mm(att.tile(item)[s * C:(s + 1) * C, g * GP:(g + 1) * GP],
                                          vs[:, d, j, s * C:(s + 1) * C], pt[:, s, d * NG + j, :],
                                          start=True, stop=True, skip_group_check=True)
                        last.then_inc(att.full_sem(item), 1)

            run(pe, convolve, attend, 0)


def diagonal(blocks, rows, cols):
    out = np.zeros((2 * rows,) + blocks.shape[1:-1] + (2 * cols,), np.float32)
    out[:rows, ..., :cols] = blocks
    out[rows:, ..., cols:] = blocks
    return out


def twice(v):
    return np.concatenate([v, v])[:, None]


def offset_layout(w):
    out = np.zeros((2, C, TAPS, 96), np.float32)
    t = w.reshape(27, C, TAPS).transpose(1, 2, 0)
    for s in range(2):
        for block, part in enumerate((t[..., 0:18:2], t[..., 1:18:2], t[..., 18:27])):
            out[s, :, :, 32 * block + 9 * s:32 * block + 9 * s + 9] = part
    return out.reshape(2 * C, TAPS, 96)


def offset_bias(b):
    out = np.zeros(96, np.float32)
    for s in range(2):
        for block, part in enumerate((b[0:18:2], b[1:18:2], b[18:27])):
            out[32 * block + 9 * s:32 * block + 9 * s + 9] = part
    return out


def group_weights(w):
    out = np.zeros((2, C, G, 2, G, CQ), np.float32)
    for s in range(2):
        for r in range(G):
            out[s, :, r, s, r, :] = w.T
    return out.reshape(2 * C, G, 2 * G * CQ)


def shape_constants():
    grid = np.zeros((96, H, W), np.float32)
    selp = np.zeros((96, 2, 2, 3, 120), np.float32)
    sele = np.zeros((120, 120, W), np.float16)
    for q in range(120):
        sele[q, q] = 1.0 / SCALE16
    selx = np.zeros((120, TAPS, 120), np.float16)
    unit = 1.0 / SCALE16
    for k in range(TAPS):
        t, kl = (0, k) if k < T0 else (1, k - T0)
        for s in range(2):
            grid[9 * s + k] = np.arange(H)[:, None] + (k // 3 - 1)
            grid[32 + 9 * s + k] = np.arange(W)[None, :] + (k % 3 - 1)
            for kind in range(3):
                selp[32 * kind + 9 * s + k, s, t, kind, kl * 24:kl * 24 + 24] = 1.0
        for q in range(24):
            selx[kl * 24 + q, k, q::24] = unit
    negq = np.zeros((120, 2), np.float32)
    negq[:, 0] = -(np.arange(120) % 24)
    negq[:, 1] = SCALE16
    emask = np.zeros((G, H, 2, W), np.float32)
    blk = np.zeros((G, W, G, W), np.float32)
    for n in range(24):
        emask[:, n, 1, n] = MASKED
    for r in range(G):
        blk[r, :, r, :] = 1.0
    pick = np.zeros((2, 2, NG, 2, NG, 2, C), np.float32)
    for s in range(2):
        for g in range(NG):
            pick[s, 0, g, 0, g, s, :] = 1.0
            pick[s, 1, g, 1, g, s, :] = -1.0
    oneb = np.zeros((2, C, 2, C), np.float32)
    for s in range(2):
        oneb[s, :, s, :] = 1.0
    return {
        "grid": grid.reshape(96, HW), "negq": negq, "selp": selp,
        "sele": sele.reshape(120, 120 * W), "selx": selx,
        "emask": emask.reshape(GP, 2, W), "blk": blk.reshape(GP, G, W), "ident": np.eye(GP, dtype=np.float32),
        "pick": pick.reshape(4 * NG, 2 * NG, 128), "oneb": oneb.reshape(128, 128),
    }


def kernel(**inputs):
    import concourse.bacc as bacc
    from concourse.bass_utils import run_bass_kernel_spmd

    p = {n: np.asarray(v) for n, v in inputs.items()}


    def norm(l, names):
        return np.stack([np.concatenate([p[f"L{l}_conv_{n}"]] * 2) for n in names], axis=1)

    def spread(v):
        return diagonal(np.broadcast_to(v.reshape(C, 1), (C, C)), C, C)

    bq = np.zeros((2, G, CQ, G, W), np.float32)
    for r in range(G):
        bq[:, r, :, r, :] = p["L3_conv_cr_bq"][None, :, None]
    wd = [p[n].reshape(C, C, TAPS).transpose(1, 2, 0).reshape(C, TAPS * C) for n in ("L0_conv_w_dcn", "L1_conv_w_conv")]
    taps = {n: p[f"L2_conv_{n}"].reshape(C, C, TAPS).transpose(1, 2, 0) for n in ("w1", "w2")}
    arrays = {
        "x": p["x"].reshape(PAIRS, 2 * C, HW),
        "woff": np.stack([offset_layout(p[f"L{l}_conv_w_off"]) for l in range(2)], axis=1),
        "boff": np.stack([offset_bias(p[f"L{l}_conv_b_off"]) for l in range(2)], axis=1),
        "wdcn": np.stack([np.concatenate([w, w]) for w in wd], axis=1),
        "bn": np.stack([norm(0, ("b_dcn", "gamma", "beta", "running_mean", "running_var")),
                        norm(1, ("b_conv", "gamma", "beta", "run_mean", "run_var"))], axis=1),
        "w1": diagonal(taps["w1"], C, C), "w2": diagonal(taps["w2"], C, C),
        "wm": spread(p["L2_conv_w_mask"]), "bm": np.broadcast_to(p["L2_conv_b_mask"].reshape(1, 1), (128, 1)),
        "wqr": spread(p["L3_conv_w_q_right"]),
        "wvr": diagonal(p["L3_conv_w_v_right"].T, C, CM), "wup": diagonal(p["L3_conv_w_up"].T, CM, C),
        "bup": twice(p["L3_conv_b_up"]),
        "wql": diagonal(p["L3_conv_w_q_left"].T, C, CM), "wvl": diagonal(p["L3_conv_w_v_left"], CM, C),
        "wq": group_weights(p["L3_conv_cr_wq"]), "wk": group_weights(p["L3_conv_cr_wk"]),
        "bq": bq.reshape(2 * G * CQ, GP), "bk": np.tile(p["L3_conv_cr_bk"], 2 * G)[:, None],
        "wv": diagonal(p["L3_conv_cr_wv"].T, C, C), "bv": twice(p["L3_conv_cr_bv"]),
        "gamma": np.broadcast_to(p["L3_conv_gamma"].reshape(1, 1), (128, 1)),
        **shape_constants(),
    }
    arrays = {n: np.ascontiguousarray(v) for n, v in arrays.items()}

    nc = bacc.Bacc("TRN2", target_bir_lowering=False, num_devices=1)
    args = {n: nc.dram_tensor(n, v.shape, mybir.dt.from_np(v.dtype), kind="ExternalInput").ap() for n, v in arrays.items()}
    out = nc.dram_tensor("out", (PAIRS, 2 * C, HW), F32, kind="ExternalOutput").ap()
    build(nc, args, out)
    r = run_bass_kernel_spmd(nc, [arrays], core_ids=[0])
    return r.results[0]["out"].reshape(B, C, H, W)
```

```python
from contextlib import ExitStack

import numpy as np

from concourse import mybir

ALU = mybir.AluOpType
ACT = mybir.ActivationFunctionType
AX = mybir.AxisListType.X
F32 = mybir.dt.float32
F16 = mybir.dt.float16

B, C, H, W = 8, 64, 24, 24
HW = H * W
PAIRS = B // 2
HP, WP = H + 2, W + 2
HALF = HW // 2
HR = H // 2
TAPS = 9
EPS = 1e-5
T0 = 5
TILE_ROWS = (T0 * H, (TAPS - T0) * H)
CR = 5
CHUNKS = -(-H // CR)
Y_ROWS = 21
SCALE16 = 1024.0
REACH = (2, 1)
REACH_MARGIN = 0.01
WIDE = H
SEG = 256
BLOCK_ROWS = 9
G = 4
NG = H // G
GP = G * W
CQ = 8
CM = 32
MASKED = -1e30
OFFSET_MAX = 1024.0
LOGIT_MIN = -80.0
LOGIT_MAX = 3e38
MASK_SCALE = 16384.0
FIRST = ("woff", "bn", "boff", "grid", "bup", "selp", "bounds")


def chunk_rows(c):
    return min(CR, H - c * CR)


def blocks_of(c, ky, reach):
    shift = ky - 1
    first = max(0, c * CR - reach - shift)
    last = min(H - 1, c * CR + chunk_rows(c) - 1 + reach - shift)
    return [(r, min(r + BLOCK_ROWS, last + 1)) for r in range(first, last + 1, BLOCK_ROWS)]


def x_after(ky, c=None):
    if ky == 2:
        return []
    taps = [(s, k) for k in range(3 * ky + 3, 3 * ky + 6) for s in range(2)]
    return taps if ky < 0 else taps[2 * c:2 * c + 2]


class Signal:

    def __init__(self, nc, ctx, name, per_pair, primed=False):
        self.sem = ctx.enter_context(nc.semaphore(name))
        self.per_pair = per_pair
        self.primed = int(primed)

    def __call__(self, i, k):
        assert 1 - self.primed <= k <= self.per_pair, k
        return self.sem, i * self.per_pair + (k + self.primed)


class Ring:

    def __init__(self, nc, ctx, name, tiles, items):
        n = len(tiles)
        self.tiles = tiles
        self.read = {item: (signal, k) for item, signal, k in items}
        self.place = {item: (u % n, u // n + 1) for u, (item, _, _) in enumerate(items)}
        self.before = {item: items[u - n][0] if u >= n else None for u, (item, _, _) in enumerate(items)}
        self.last = {u % n: item for u, (item, _, _) in enumerate(items)}
        assert len(self.place) == len(items)
        self.full = [Signal(nc, ctx, f"{name}{t}_full", len(range(t, len(items), n))) for t in range(n)]

    def tile(self, item):
        return self.tiles[self.place[item][0]]

    def filled(self, i, item):
        slot, n = self.place[item]
        return self.full[slot](i, n)

    def emptied(self, i, item):
        signal, k = self.read[item]
        return signal(i, k)

    def may_fill(self, i, item):
        if self.before[item] is None:
            return self.read[self.last[self.place[item][0]]][0](i, 0)
        return self.emptied(i, self.before[item])

    def full_sem(self, item):
        return self.full[self.place[item][0]].sem


def groups(reach):
    return [(ky, c, rows) for ky in range(3) for c in range(CHUNKS) for rows in blocks_of(c, ky, reach)]


PARTS = [(name,) for name in ("pool", "theta", "pixel", "ctx", "scale")]
PARTS += [(name, x) for x in range(3) for name in ("qkv", "energy", "exp", "log", "lse", "gap", "turn", "out", "mix")]
PREPARE = """z00 z01 z02 y00 masks z03 x00 z04 y01 | x01 z10 z11 | m00 z12 m01 | z13 y10 z14 x10
             | y11 reach x11 | m10 m11 |""".split()
STEPS_PER_LAYER = 1 + PREPARE.count("|") + 3 * (1 + CHUNKS)
PART_STEP = [1, 2, 3, 5, 6,
             8, 9, 11, 12, 14, 15, 17, 18, 19,
             20, 22, 24, 25, 27, 28, 30, 31, 33,
             34, 36, 37, 39, 40, 42, 43, 45, 46]


def preparation(between, l, kinds):
    step = l * STEPS_PER_LAYER
    for item in PREPARE:
        if item == "|":
            step += 1
            between(step)
        elif item in kinds:
            yield item, 0, 0
        elif item[0] in kinds and item[1:].isdigit():
            yield item[0], int(item[1]), int(item[2])


def parts_at(step):
    return [part for part, at in zip(PARTS, PART_STEP) if at == step]


def build(nc, a, out):
    ctx = ExitStack()
    with ctx:
        def sb(name, shape, dt=F32):
            return ctx.enter_context(nc.sbuf_tensor(name, shape, dt))

        primed = []

        def sig(name, per_pair, reused=False):
            signal = Signal(nc, ctx, name, per_pair, primed=reused)
            if reused:
                primed.append(signal)
            return signal

        work_t = [ctx.enter_context(nc.psum_tensor(f"work{s}_ps", [128, 2, 512], F32)) for s in range(2)]
        att_t = [ctx.enter_context(nc.psum_tensor(f"att{s}_ps", [128, 512], F32)) for s in range(2)]
        ysum = ctx.enter_context(nc.psum_tensor("ysum", [128, 2, 512], F32))

        const = {n: sb(f"{n}_sb", list(v.shape), v.dtype) for n, v in a.items() if n != "x"}
        woff, boff, wdcn, bn = const["woff"], const["boff"], const["wdcn"], const["bn"]
        grid, unit, selp, sele, selx = (const[n] for n in ("grid", "unit", "selp", "sele", "selx"))
        bnw = sb("bnw", [128, 2, 4])
        zero16 = sb("zero16", [128, 512], F16)

        xin = sb("xin", [128, HW])
        xpad = [sb(f"xpad{n}", [128, HP, WP]) for n in range(3)]
        hpad = sb("hpad", [128, HP, WP])
        mpad = sb("mpad", [128, HP, WP])
        coords = sb("coords", [96, HW])
        off16 = sb("off16", [128, HW], F16)
        mask16 = sb("mask16", [128, HW], F16)
        hatf = [[sb(f"hatf{d}{t}", [120, HW]) for t in range(2)] for d in range(2)]
        haty = [[[sb(f"haty{s}{t}{p}", [120, HW], F16) for p in range(2)] for t in range(2)] for s in range(2)]
        hatx = [[[sb(f"hatx{s}{t}{p}", [120, HW], F16) for p in range(2)] for t in range(2)] for s in range(2)]
        hxe = [[sb(f"hxe{s}{b}", [120, 3, HW]) for b in range(2)] for s in range(2)]
        zt = [sb(f"zt{s}", [120, CHUNKS, TAPS * C]) for s in range(2)]
        prod = [[sb(f"prod{s}{b}", [120, 3, BLOCK_ROWS * W]) for b in range(2)] for s in range(2)]
        shared = sb("shared", [128, HP * W + 3 * HW])
        hmax = shared[:, 0:HP * W].rearrange("p (h w) -> p h w", w=W)
        dil, lgt, lgd = (shared[:, HP * W + n * HW:HP * W + (n + 1) * HW] for n in range(3))
        relu1 = dil
        c2 = lgd
        x3 = sb("x3", [128, HW])
        pl = [sb(f"pl{n}", [128, HW]) for n in range(2)]
        small = sb("small", [128, 24])
        reach = sb("reach", [32, 2, 32])
        wide = sb("wide", [1, 2], mybir.dt.int32)
        ublk = sb("ublk", [128, 128])
        xt = [sb(f"xt{n}", [128, HW]) for n in range(2)]
        xt.append(xt[0])
        xcol = x3[:]
        qs = sb("qs", [128, NG, GP])
        kraw = sb("kraw", [128, NG * W])
        ks = sb("ks", [128, NG, 4, W])
        vs = sb("vs", [GP, 2, NG, 128])
        es = sb("es", [GP, NG, 4, W])
        pr = sb("pr", [GP, NG, 4, W])
        st = sb("st", [GP, 5, 4 * NG])
        lset = sb("lset", [4 * NG, NG, GP])
        pb = sb("pb", [GP, 2, 2 * NG, G, W])
        pt = shared[0:GP, 0:4 * NG * GP].rearrange("p (s j n) -> p s j n", s=2, j=2 * NG)
        gap = sb("gap", [128, HW])
        ow = pl
        mix = ow[0]
        ares = [xt[0], xt[1], sb("ares", [128, HW])]
        share = ares[2]

        first_loaded = ctx.enter_context(nc.semaphore("offset_consts_loaded"))
        loaded = ctx.enter_context(nc.semaphore("consts_loaded"))
        s_border = ctx.enter_context(nc.semaphore("first_border_set"))
        other_borders = ctx.enter_context(nc.semaphore("borders_set"))
        s_bn = ctx.enter_context(nc.semaphore("bn_step"))
        x_loaded = sig("x_loaded", 16)
        x_padded = sig("x_padded", 1)
        x1_padded = sig("x1_padded", 2)
        coords_raw = sig("coords_raw", 2)
        coords_ready = sig("coords_ready", 2)
        dist_y = sig("dist_y", 8)
        dist_x = sig("dist_x", 8)
        haty_f = sig("haty_f", 8)
        hatx_f = sig("hatx_f", 8)
        haty_hi = sig("haty_hi", 8)
        haty_lo = sig("haty_lo", 8, reused=True)
        hatx_m = sig("hatx_masked", 8)
        hatx_hi = sig("hatx_hi", 8)
        hatx_lo = sig("hatx_lo", 8, reused=True)
        n_groups = len(groups(REACH[0]))
        n_wide = 2 * len(groups(WIDE))
        per_row = n_groups // 3
        assert per_row == CHUNKS
        prod_ready = [sig(f"prod{s}_ready", 2 * n_groups, reused=True) for s in range(2)]
        prod_used = sig("prod_used", 2 * (n_groups - 1))
        wide_full = ctx.enter_context(nc.semaphore("wide_spread_full"))
        wide_ready = ctx.enter_context(nc.semaphore("wide_prod_ready"))
        reach_rows = sig("reach_rows", 2)
        reach_turned = sig("reach_turned", 2)
        reach_max = sig("reach_max", 2)
        reach_flag = sig("reach_flag", 2)
        mask_exp = sig("mask_exp", 2)
        mask_add = sig("mask_add", 2)
        mask_rcp = sig("mask_ready", 2)
        mask_hi = sig("mask_hi", 2)
        mask_lo = sig("mask_lo", 2)
        coords_cut = sig("coords_cut", 2)
        offs_hi = sig("offsets_hi", 2)
        first_half = sig("conv_first_half", 4)
        y_summed = sig("y_summed", 2, reused=True)
        y_read = sig("y_read", 4, reused=True)
        z_ready = [sig(f"z{s}_ready", 2 * CHUNKS) for s in range(2)]
        hx_ready = [sig(f"hx{s}_ready", 2 * TAPS) for s in range(2)]
        x2_ready = sig("x2_ready", 1, reused=True)
        lgt_ready = sig("lgt_ready", 1)
        lgd_ready = sig("lgd_ready", 1)
        gate_ready = sig("gate_ready", 1)
        hmax_a = sig("hmax_a", 1)
        hmax_ready = sig("hmax_ready", 1)
        dil_a = sig("dil_a", 1)
        dil_ready = sig("dil_ready", 1)
        h_ready = sig("h_ready", 2, reused=True)
        c2_relu = sig("c2_relu", 2, reused=True)
        c2_gated = sig("c2_gated", 1)
        x3_ready = sig("x3_ready", 1)

        pl_ready = [sig(f"pool_logits{n}", 2) for n in range(2)]
        pl_max = [sig(f"pool_max{n}", 1) for n in range(2)]
        pl_exp = [sig(f"pool_exp{n}", 1) for n in range(2)]
        pl_rcp = [sig(f"pool_rcp{n}", 1) for n in range(2)]
        xs_sum = sig("pooled_sum", 1)
        xs_ready = sig("pooled_ready", 1)
        ctx_ready = sig("ctx_ready", 1)
        sc_exp = sig("scale_exp", 1)
        sc_add = sig("scale_add", 1)
        sc_ready = sig("scale_ready", 1)
        xm_sum = sig("mean_sum", 1)
        xm_ready = sig("mean_ready", 1)
        avg_ready = sig("avg_ready", 1)
        u_ready = sig("theta_ready", 1)
        ublk_ready = sig("theta_spread", 1)
        pp_ready = sig("pixel_softmax", 1)
        pp_step = sig("pixel_gate_step", 2)
        pp_gate = sig("pixel_gate", 1)
        xt_ready = sig("att_input", 3)
        xcol_ready = sig("att_input_by_columns", 3)
        q_ready = sig("q_ready", 6)
        k_raw = sig("k_raw", 3)
        k_ready = sig("k_ready", 3)
        v_ready = sig("v_ready", 12, reused=True)
        e_ready = sig("energy_ready", 6)
        e_max = sig("energy_max", 3)
        e_sub = sig("energy_shifted", 3)
        p_exp = sig("p_exp", 3)
        p_sum = sig("p_sum", 3)
        s_log = sig("sum_log", 3)
        s_rcp = sig("sum_rcp", 3)
        lse_ready = sig("lse_ready", 3)
        lset_ready = sig("lse_rows_ready", 3)
        p_norm = sig("p_normed", 3)
        pb_ready = [sig(f"p{s}_blocks", 3) for s in range(2)]
        pt_ready = [sig(f"p{s}_turned", 9) for s in range(2)]
        d_ready = sig("gap_ready", 6)
        g_step = sig("share_step", 9)
        g_log = sig("share_log", 3)
        g_ready = sig("share_ready", 3)
        o_ready = sig("out_read", 12, reused=True)
        m_diff = sig("mix_diff", 3)
        m_mul = sig("mix_scaled", 3)
        m_add = sig("mix_added", 3)
        a_ready = sig("att_output", 3, reused=True)
        stored = sig("stored", 16, reused=True)

        items = []
        for l in range(2):
            items.append((("offsets", l), coords_raw, l + 1))
            for kind, s, n in preparation(lambda step: None, l, "zyxm"):
                signal, per_image = {"z": (z_ready[s], CHUNKS), "y": (dist_y, 2), "x": (dist_x, 2), "m": (hatx_m, 2)}[kind]
                images = l if kind == "z" else l * 2 + s
                items.append(((kind, l, s, n), signal, images * per_image + n + 1))
            assert len(groups(REACH[l])) == n_groups
            for g in range(n_groups):
                if g == 0:
                    items += [(("hx", l, s, k), hx_ready[s], l * TAPS + k + 1) for s, k in x_after(-1)]
                items += [(("hy", l, s, g), prod_ready[s], l * n_groups + g + 1) for s in range(2)]
                items += [(("hx", l, s, k), hx_ready[s], l * TAPS + k + 1) for s, k in x_after(*divmod(g, per_row))]
        items += [(("gate",), lgt_ready, 1), (("conv1",), h_ready, 2), (("conv2",), c2_relu, 2)]
        work = Ring(nc, ctx, "work", work_t, items)
        items = [(("pool_logits", h), pl_ready[0], h + 1) for h in range(2)]
        items += [(("avg",), avg_ready, 1), (("theta",), u_ready, 1)]
        items += [(("pixel_logits", h), pl_ready[1], h + 1) for h in range(2)]
        items += [(("ctx",), ctx_ready, 1), (("scale",), sc_exp, 1)]
        dh = [(d, h) for d in range(2) for h in range(2)]
        for x in range(3):
            items += [(("q", x, h), q_ready, x * 2 + h + 1) for h in range(2)] + [(("k", x), k_raw, x + 1)]
            items += [(("v", x, d, h), v_ready, x * 4 + d * 2 + h + 1) for d, h in dh]
            items += [(("e", x, h), e_ready, x * 2 + h + 1) for h in range(2)] + [(("lse", x), lset_ready, x + 1)]
            items += [(("d", x, h), d_ready, x * 2 + h + 1) for h in range(2)]
            items += [(("p", x, s, j), pt_ready[s], x * 3 + j + 1) for s in range(2) for j in range(3)]
            items += [(("o", x, d, h), o_ready, x * 4 + d * 2 + h + 1) for d, h in dh]
        att = Ring(nc, ctx, "att", att_t, items)

        n_first, n_const = len(FIRST), len(const) - len(FIRST)
        block = ctx.enter_context(nc.Block())

        NMX, SUM, RCP, XS, XR, CTX, SE, SA, SR, XM, XA, AVG, U, BUPN = 0, 2, 4, 6, 7, 8, 9, 10, 11, 12, 13, 14, 15, 16

        def rows(buf, r0, r1):
            return buf[:, r0 + 1:r1 + 1, 1:W + 1]

        def halves(buf):
            return buf.rearrange("p (b n) -> p b n", b=2)

        def by_image(buf, s):
            return buf[:].rearrange("p g (d s) v -> p (g d) s v", s=2)[:, :, s, :]

        def grid3(buf):
            return buf.rearrange("p (h w) -> p h w", w=W)

        def y_pieces(r0, r1):
            if r0 < Y_ROWS:
                yield 0, r0 * W, r0, min(r1, Y_ROWS)
            if r1 > Y_ROWS:
                yield 1, (max(r0, Y_ROWS) - Y_ROWS) * W, max(r0, Y_ROWS), r1

        @block.sync
        def _(sp):
            for signal in primed:
                sp.sem_inc(signal.sem, 1)
            sp.dma_start(xin[:], a["x"][0]).then_inc(x_loaded.sem, 16)
            for n in FIRST:
                sp.dma_start(const[n][:], a[n]).then_inc(first_loaded, 16)
            for n, t in const.items():
                if n not in FIRST:
                    sp.dma_start(t[:], a[n]).then_inc(loaded, 16)
            with sp.Fori(0, PAIRS - 1) as n:
                sp.wait_ge(*x2_ready(n, 1))
                sp.dma_start(xin[:], a["x"][n + 1]).then_inc(x_loaded.sem, 16)
                sp.wait_ge(*a_ready(n, 3))
                sp.dma_start(out[n], ares[2][:]).then_inc(stored.sem, 16)
            sp.wait_ge(*a_ready(PAIRS - 1, 3))
            sp.dma_start(out[PAIRS - 1], ares[2][:]).then_inc(stored.sem, 16)
            sp.wait_ge(*stored(PAIRS - 1, 16))

        def run(eng, convolve, attend):
            convolve(0, lambda step: None)
            with eng.Fori(0, PAIRS - 1) as n:
                def between(step):
                    for part in parts_at(step):
                        attend(n, *part)

                convolve(n + 1, between)
            for part in PARTS:
                attend(PAIRS - 1, *part)

        def step_sum(l, ky, c):
            return l * STEPS_PER_LAYER + 2 + PREPARE.count("|") + ky * (1 + CHUNKS) + c

        def z_copy(i, eng, copy, l, s, c):
            n = chunk_rows(c) * W
            item = ("z", l, s, c)
            eng.wait_ge(*work.filled(i, item))
            copy(zt[s][0:n, c, :].rearrange("p (b n) -> p b n", b=2),
                 work.tile(item)[0:n, :, 0:HALF]).then_inc(z_ready[s].sem, 1)

        @block.gpsimd
        def _(pool):
            nc.gpsimd.memset(xpad[0][:], 0.0).then_inc(s_border, 1)
            pool.wait_ge(s_border, 1)

            def copy(dst, src):
                nc.gpsimd.nop(nofuse=True)
                return nc.gpsimd.tensor_copy(dst, src)

            def convolve(i, between):
                pool.wait_ge(*x_loaded(i, 16))
                pool.wait_ge(*y_summed(i, 0))
                copy(rows(xpad[0], 0, H), grid3(xin[:])).then_inc(x_padded.sem, 1)
                pool.wait_ge(loaded, 16 * n_const)
                for l in range(2):
                    between(l * STEPS_PER_LAYER)
                    for kind, s, t in preparation(between, l, "ym"):
                        n = TILE_ROWS[t]
                        k = (l * 2 + s) * 2 + t + 1
                        hat, (hi, lo), done, lo_done = (
                            (hatf[0][t], haty[s][t], haty_f, haty_lo) if kind == "y" else
                            (hatf[1][t], hatx[s][t], hatx_m, hatx_lo))
                        pool.wait_ge(*done(i, k))
                        pool.wait_ge(*y_summed(i, l))
                        nc.gpsimd.tensor_tensor(lo[0:n, :], hat[0:n, :], hi[0:n, :], ALU.subtract).then_inc(lo_done.sem, 1)
                    for ky in range(3):
                        for c in range(-1, CHUNKS):
                            between(step_sum(l, ky, c))

            def attend(i, part, x=0):
                if part == "qkv":
                    pool.wait_ge(*xt_ready(i, max(2, x + 1)))
                    if x:
                        pool.wait_ge(*v_ready(i, 4 * x))
                    copy(xcol.rearrange("p (w h) -> p h w", h=H), grid3(xt[x][:])).then_inc(xcol_ready.sem, 1)
                if part == "log":
                    pool.wait_ge(*p_norm(i, x + 1))
                    if x:
                        pool.wait_ge(*att.filled(i, ("p", x - 1, 1, 2)))
                    else:
                        pool.wait_ge(*a_ready(i, 0))
                    p_b = by_image(pr, 1).unsqueeze(2).broadcast_to([GP, 2 * NG, G, W])
                    k_b = const["blk"][:].unsqueeze(1).broadcast_to([GP, 2 * NG, G, W])
                    nc.gpsimd.tensor_tensor(pb[:, 1], p_b, k_b, ALU.mult).then_inc(pb_ready[1].sem, 1)

            run(pool, convolve, attend)

        @block.scalar
        def _(act):
            act.wait_ge(s_bn, 1)
            nc.scalar.activation(bnw[:, :, 1], bnw[:, :, 0], ACT.Sqrt).then_inc(s_bn, 1)
            act.wait_ge(s_bn, 8)
            act.wait_ge(other_borders, 5)
            nc.scalar.preload_act_table_set("natural_log_exp_and_others")
            act.wait_ge(loaded, 16 * n_const)

            def convolve(i, between):
                for l in range(2):
                    act.wait_ge(*y_summed(i, l))
                    between(l * STEPS_PER_LAYER)
                    for kind, s, t in preparation(between, l, "zyx"):
                        if kind == "z":
                            if s == 0:
                                z_copy(i, act, nc.scalar.copy, l, s, t)
                                if t == 1:
                                    act.wait_ge(*coords_cut(i, l + 1))
                                    nc.scalar.activation(coords[64:96, :], coords[64:96, :], ACT.Exp,
                                                         scale=-1.0).then_inc(mask_exp.sem, 1)
                            continue
                        n = TILE_ROWS[t]
                        k = (l * 2 + s) * 2 + t + 1
                        hat, d_done, lo_done = ((hatf[0][t], dist_y, haty_lo), (hatf[1][t], dist_x, hatx_lo))[kind == "x"]
                        hat = hat[0:n, :]
                        item = (kind, l, s, t)
                        act.wait_ge(*work.filled(i, item))
                        act.wait_ge(*lo_done(i, max(0, k - 2)))
                        nc.scalar.activation(halves(hat), work.tile(item)[0:n, :, 0:HALF],
                                             ACT.Abs).then_inc(d_done.sem, 1)
                        act.wait_ge(*d_done(i, k))
                        if kind == "y":
                            nc.scalar.activation(haty[s][t][0][0:n, :], hat, ACT.Relu,
                                                 bias=unit[0:n, 0:1], scale=-SCALE16).then_inc(haty_hi.sem, 1)
                            act.wait_ge(*haty_hi(i, k))
                        nc.scalar.activation(hat, hat, ACT.Relu, bias=unit[0:n, 0:1],
                                             scale=-SCALE16).then_inc((haty_f if kind == "y" else hatx_f).sem, 1)
                    for s, k in x_after(-1):
                        x_copy(i, l, s, k)
                    for ky in range(3):
                        between(step_sum(l, ky, -1))
                        for c in range(CHUNKS):
                            for s, k in x_after(ky, c):
                                x_copy(i, l, s, k)
                            between(step_sum(l, ky, c))
                    act.wait_ge(*y_summed(i, l + 1))
                    if l == 0:
                        for bank, c0, r0, r1 in y_pieces(0, H):
                            nc.scalar.activation(rows(xpad[1], r0, r1), grid3(ysum[:, bank, c0:c0 + (r1 - r0) * W]),
                                                 ACT.Relu, bias=bnw[:, l, 3:4], scale=bnw[:, l, 2:3]).then_inc(x1_padded.sem, 1)
                    for bank, c0, r0, r1 in y_pieces(0, H):
                        nc.scalar.activation((xin, relu1)[l][:, r0 * W:r1 * W], ysum[:, bank, c0:c0 + (r1 - r0) * W],
                                             ACT.Relu, bias=bnw[:, l, 3:4], scale=bnw[:, l, 2:3]).then_inc(y_read.sem, 1)

            def x_copy(i, l, s, k):
                item = ("hx", l, s, k)
                act.wait_ge(*work.filled(i, item))
                act.wait_ge(*prod_ready[s](i, l * n_groups + (per_row if k // 3 == 2 else 0)))
                nc.scalar.copy(halves(hxe[s][k // 3 % 2][:, k % 3, :]),
                               work.tile(item)[0:120, :, 0:HALF]).then_inc(hx_ready[s].sem, 1)

            def softmax_exp(i, n, name):
                for h in range(2):
                    item = (name, h)
                    act.wait_ge(*att.filled(i, item))
                    nc.scalar.copy(pl[n][:, h * HALF:(h + 1) * HALF], att.tile(item)[:, 0:HALF]).then_inc(pl_ready[n].sem, 1)
                act.wait_ge(*pl_max[n](i, 1))
                nc.scalar.activation(pl[n][:], pl[n][:], ACT.Exp, bias=small[:, NMX + n:NMX + n + 1],
                                     accum_out=small[:, SUM + n:SUM + n + 1]).then_inc(pl_exp[n].sem, 1)

            def attend(i, part, x=0):
                if part == "pool":
                    softmax_exp(i, 0, "pool_logits")
                if part == "pixel":
                    softmax_exp(i, 1, "pixel_logits")
                if part == "scale":
                    act.wait_ge(*att.filled(i, ("scale",)))
                    nc.scalar.activation(small[:, SE:SE + 1], att.tile(("scale",))[:, 0:1], ACT.Exp,
                                         bias=small[:, BUPN:BUPN + 1], scale=-1.0).then_inc(sc_exp.sem, 1)
                    act.wait_ge(*pp_ready(i, 1))
                    nc.scalar.activation(pl[1][:], pl[1][:], ACT.Exp, scale=-1.0).then_inc(pp_step.sem, 1)
                    act.wait_ge(*pp_step(i, 1))
                    nc.scalar.activation(pl[1][:], pl[1][:], ACT.Ln, bias=1.0).then_inc(pp_step.sem, 1)
                    act.wait_ge(*pp_step(i, 2))
                    nc.scalar.activation(pl[1][:], pl[1][:], ACT.Exp, scale=-1.0).then_inc(pp_gate.sem, 1)
                if part == "qkv":
                    act.wait_ge(*att.filled(i, ("k", x)))
                    nc.scalar.activation(kraw[:], att.tile(("k", x))[:, 0:NG * W],
                                         ACT.Identity, bias=const["bk"][:, 0:1]).then_inc(k_raw.sem, 1)
                    for d in range(2):
                        for h in range(2):
                            item = ("v", x, d, h)
                            act.wait_ge(*att.filled(i, item))
                            nc.scalar.copy(vs[:, d, 3 * h:3 * h + 3, :],
                                           att.tile(item)[0:GP, 0:384].rearrange("p (g c) -> p g c", g=3)).then_inc(v_ready.sem, 1)
                if part == "energy":
                    act.wait_ge(*e_sub(i, x + 1))
                    nc.scalar.activation(pr[:], es[:], ACT.Exp).then_inc(p_exp.sem, 1)
                if part == "exp":
                    act.wait_ge(*p_sum(i, x + 1))
                    nc.scalar.activation(st[:, 2, :], st[:, 1, :], ACT.Ln).then_inc(s_log.sem, 1)
                if part == "gap":
                    act.wait_ge(*d_ready(i, 2 * x + 2))
                    if x == 0:
                        act.wait_ge(*stored(i, 0))
                    nc.scalar.activation(share[:], gap[:], ACT.Abs).then_inc(g_step.sem, 1)
                    act.wait_ge(*g_step(i, 3 * x + 1))
                    nc.scalar.activation(share[:], share[:], ACT.Exp, scale=-1.0).then_inc(g_step.sem, 1)
                    act.wait_ge(*g_step(i, 3 * x + 2))
                    nc.scalar.activation(share[:], share[:], ACT.Ln, bias=1.0).then_inc(g_step.sem, 1)
                if part == "turn":
                    for j in range(3):
                        item = ("p", x, 1, j)
                        act.wait_ge(*att.filled(i, item))
                        nc.scalar.copy(pt[:, 1, 4 * j:4 * j + 4, :],
                                       att.tile(item)[0:GP, 0:384].rearrange("p (g c) -> p g c", g=4)).then_inc(pt_ready[1].sem, 1)
                if part == "out":
                    act.wait_ge(*g_log(i, x + 1))
                    nc.scalar.activation(share[:], share[:], ACT.Exp).then_inc(g_ready.sem, 1)
                    for d in range(2):
                        for h in range(2):
                            item = ("o", x, d, h)
                            src = att.tile(item)[:, 0:HALF]
                            dst = ow[d][:, h * HALF:(h + 1) * HALF]
                            if d == 1:
                                src = src.rearrange("p (w h) -> p h w", h=H)
                                dst = grid3(ow[1][:])[:, :, h * (W // 2):(h + 1) * (W // 2)]
                            act.wait_ge(*att.filled(i, item))
                            nc.scalar.activation(dst, src, ACT.Identity, bias=const["bv"][:, 0:1]).then_inc(o_ready.sem, 1)

            run(act, convolve, attend)

        @block.vector
        def _(dve):
            def w(pair):
                dve.wait_ge(*pair)

            v = nc.vector
            for buf in (xpad[1], xpad[2], hpad, zero16):
                v.memset(buf[:], 0.0).then_inc(other_borders, 1)
            v.memset(mpad[:], MASKED).then_inc(other_borders, 1)
            dve.wait_ge(first_loaded, 16 * n_first)
            v.tensor_scalar(bnw[:, :, 0], bn[:, :, 4], EPS, None, ALU.add).then_inc(s_bn, 1)
            dve.wait_ge(s_bn, 2)
            v.reciprocal(bnw[:, :, 0], bnw[:, :, 1]).then_inc(s_bn, 1)
            dve.wait_ge(s_bn, 3)
            v.tensor_tensor(bnw[:, :, 2], bnw[:, :, 0], bn[:, :, 1], ALU.mult).then_inc(s_bn, 1)
            dve.wait_ge(s_bn, 4)
            v.tensor_tensor(bnw[:, :, 1], bn[:, :, 0], bn[:, :, 3], ALU.subtract).then_inc(s_bn, 1)
            dve.wait_ge(s_bn, 5)
            v.tensor_tensor(bnw[:, :, 1], bnw[:, :, 1], bnw[:, :, 2], ALU.mult).then_inc(s_bn, 1)
            dve.wait_ge(s_bn, 6)
            v.tensor_tensor(bnw[:, :, 3], bnw[:, :, 1], bn[:, :, 2], ALU.add).then_inc(s_bn, 1)
            v.tensor_scalar(small[:, BUPN:BUPN + 1], const["bup"][:], -1.0, None, ALU.mult).then_inc(s_bn, 1)

            v.memset(reach[:], 0.0).then_inc(s_bn, 1)
            dve.wait_ge(s_bn, 9)
            dve.wait_ge(other_borders, 5)
            wide_runs = dve.alloc_register("wide_runs_dve")
            dve.reg_mov(wide_runs, 0)

            def multiply(s, g, reach, item):
                ky, c, (r0, r1) = groups(reach)[g]
                n = (r1 - r0) * W
                m = chunk_rows(c) * W
                return v.tensor_tensor(prod[s][g % 2][0:m, :, 0:n],
                                       work.tile(item).rearrange("p b n -> p (b n)").rearrange(
                                           "p (t n) -> p t n", n=SEG)[0:m, 0:3, 0:n],
                                       hxe[s][ky % 2][0:m, :, r0 * W:r1 * W], ALU.mult)

            def convolve(i, between):
                for l in range(2):
                    item = ("offsets", l)
                    w(work.filled(i, item))
                    v.scalar_tensor_tensor(out=coords[:].rearrange("p (b n) -> p b n", b=2),
                                           in0=work.tile(item)[0:96, :, 0:HALF], scalar=boff[:, l:l + 1],
                                           in1=grid[:].rearrange("p (b n) -> p b n", b=2),
                                           op0=ALU.add, op1=ALU.add).then_inc(coords_raw.sem, 1)
                    w(coords_raw(i, l + 1))
                    v.tensor_scalar(coords[:], coords[:], const["bounds"][:, 0:1], const["bounds"][:, 1:2],
                                    ALU.max, ALU.min).then_inc(coords_cut.sem, 1)
                    w(coords_cut(i, l + 1))
                    v.tensor_copy(off16[0:64, :], coords[0:64, :]).then_inc(offs_hi.sem, 1)
                    w(offs_hi(i, l + 1))
                    v.tensor_tensor(off16[64:128, :], coords[0:64, :], off16[0:64, :],
                                    ALU.subtract).then_inc(coords_ready.sem, 1)
                    between(l * STEPS_PER_LAYER)
                    for kind, s, t in preparation(between, l, ("z", "m", "masks", "reach")):
                        if kind == "z":
                            if s == 1:
                                w(y_summed(i, l))
                                z_copy(i, dve, v.tensor_copy, l, s, t)
                        if kind == "reach":
                            v.tensor_reduce(reach[:, 0, 0:1], coords[0:32, :], AX, ALU.max, apply_absolute_value=True).then_inc(reach_rows.sem, 1)
                            w(reach_rows(i, l + 1))
                            v.transpose(reach[:, 1, :], reach[:, 0, :]).then_inc(reach_turned.sem, 1)
                            w(reach_turned(i, l + 1))
                            v.tensor_reduce(reach[0:1, 0, 1:2], reach[0:1, 1, :], AX, ALU.max).then_inc(reach_max.sem, 1)
                            w(reach_max(i, l + 1))
                            v.tensor_scalar(wide[0:1, l:l + 1], reach[0:1, 0, 1:2], REACH[l] - REACH_MARGIN, None, ALU.is_gt).then_inc(reach_flag.sem, 1)
                        if kind == "masks":
                            w(mask_exp(i, l + 1))
                            v.tensor_scalar(coords[64:96, :], coords[64:96, :], 1.0, 1.0 / MASK_SCALE,
                                            ALU.add, ALU.mult).then_inc(mask_add.sem, 1)
                            w(mask_add(i, l + 1))
                            v.reciprocal(coords[64:96, :], coords[64:96, :]).then_inc(mask_rcp.sem, 1)
                            w(mask_rcp(i, l + 1))
                            v.tensor_copy(mask16[64:96, :], coords[64:96, :]).then_inc(mask_hi.sem, 1)
                            w(mask_hi(i, l + 1))
                            v.tensor_tensor(mask16[96:128, :], coords[64:96, :], mask16[64:96, :],
                                            ALU.subtract).then_inc(mask_lo.sem, 1)
                        if kind == "m":
                            n = TILE_ROWS[t]
                            k = (l * 2 + s) * 2 + t + 1
                            item = ("m", l, s, t)
                            hat = halves(hatf[1][t][0:n, :])
                            w(work.filled(i, item))
                            w(hatx_f(i, k))
                            v.tensor_tensor(halves(hatx[s][t][0][0:n, :]), work.tile(item)[0:n, :, 0:HALF], hat,
                                            ALU.mult).then_inc(hatx_hi.sem, 1)
                            w(hatx_hi(i, k))
                            v.tensor_tensor(hat, work.tile(item)[0:n, :, 0:HALF], hat, ALU.mult).then_inc(hatx_m.sem, 1)
                    w((loaded, 16 * n_const))
                    w(reach_flag(i, l + 1))
                    dve.nop(nofuse=True)
                    is_wide = dve.value_load(wide[0:1, l:l + 1], min_val=0, max_val=1)
                    with dve.If(is_wide != 0):
                        runs = dve.snap(wide_runs)
                        steps = groups(WIDE)
                        for g, (ky, c, _) in enumerate(steps):
                            if g == 0 or steps[g - 1][0] != ky:
                                between(step_sum(l, ky, -1))
                            for s in range(2):
                                w((wide_full, runs * n_wide + 2 * g + s + 1))
                                w(work.emptied(i, ("hx", l, s, 3 * ky + 2)))
                                multiply(s, g, WIDE, ("hy", l, s, 0)).then_inc(wide_ready, 1)
                            if g + 1 == len(steps) or steps[g + 1][1] != c:
                                w((wide_ready, runs * n_wide + 2 * g + 2))
                                for s in range(2):
                                    dve.sem_inc(prod_ready[s].sem, 1)
                                between(step_sum(l, ky, c))
                        dve.reg_add(wide_runs, wide_runs, 1)
                    with dve.Else():
                        for g, (ky, c, _) in enumerate(groups(REACH[l])):
                            if c == 0:
                                between(step_sum(l, ky, -1))
                            for s in range(2):
                                item = ("hy", l, s, g)
                                w(work.filled(i, item))
                                if c == 0:
                                    w(work.emptied(i, ("hx", l, s, 3 * ky + 2)))
                                if g >= 2:
                                    w(prod_used(i, l * (n_groups - 1) + g - 1))
                                multiply(s, g, REACH[l], item).then_inc(prod_ready[s].sem, 1)
                            between(step_sum(l, ky, c))
                w(y_read(i, 4))
                v.tensor_tensor(rows(xpad[2], 0, H), grid3(xin[:]), grid3(relu1), ALU.add).then_inc(x2_ready.sem, 1)
                w(work.filled(i, ("gate",)))
                v.tensor_scalar(halves(lgt), work.tile(("gate",))[:, :, 0:HALF], const["bm"][:, 0:1], None,
                                ALU.add).then_inc(lgt_ready.sem, 1)
                w(lgt_ready(i, 1))
                v.scalar_tensor_tensor(out=lgd, in0=lgt, scalar=0.0, in1=lgt,
                                       op0=ALU.is_gt, op1=ALU.subtract).then_inc(lgd_ready.sem, 1)
                w(lgd_ready(i, 1))
                v.tensor_tensor(rows(mpad, 0, H), grid3(lgt), grid3(lgd), ALU.add).then_inc(gate_ready.sem, 1)
                w(gate_ready(i, 1))
                v.tensor_tensor(hmax, mpad[:, :, 0:W], mpad[:, :, 1:W + 1], ALU.max).then_inc(hmax_a.sem, 1)
                w(hmax_a(i, 1))
                v.tensor_tensor(hmax, hmax, mpad[:, :, 2:W + 2], ALU.max).then_inc(hmax_ready.sem, 1)
                w(hmax_ready(i, 1))
                v.tensor_tensor(grid3(dil), hmax[:, 0:H, :], hmax[:, 1:H + 1, :], ALU.max).then_inc(dil_a.sem, 1)
                w(dil_a(i, 1))
                v.tensor_tensor(grid3(dil), grid3(dil), hmax[:, 2:H + 2, :], ALU.max).then_inc(dil_ready.sem, 1)
                w(dil_ready(i, 1))
                for h in range(2):
                    w(work.filled(i, ("conv1",)) if h else first_half(i, 3))
                    v.scalar_tensor_tensor(out=rows(hpad, h * HR, (h + 1) * HR),
                                           in0=grid3(work.tile(("conv1",))[:, h, 0:HALF]), scalar=0.0,
                                           in1=grid3(dil[:, h * HALF:(h + 1) * HALF]),
                                           op0=ALU.max, op1=ALU.mult).then_inc(h_ready.sem, 1)
                w(gate_ready(i, 1))
                for h in range(2):
                    w(work.filled(i, ("conv2",)) if h else first_half(i, 4))
                    v.scalar_tensor_tensor(out=grid3(c2[:, h * HALF:(h + 1) * HALF]),
                                           in0=grid3(work.tile(("conv2",))[:, h, 0:HALF]), scalar=0.0,
                                           in1=rows(mpad, h * HR, (h + 1) * HR),
                                           op0=ALU.max, op1=ALU.mult).then_inc(c2_relu.sem, 1)
                w(c2_relu(i, 2))
                v.tensor_tensor(grid3(c2), grid3(c2), rows(mpad, 0, H), ALU.mult).then_inc(c2_gated.sem, 1)
                w(c2_gated(i, 1))
                w(v_ready(i, 0))
                v.tensor_tensor(grid3(x3[:]), grid3(c2), rows(xpad[2], 0, H), ALU.add).then_inc(x3_ready.sem, 1)
                w(x3_ready(i, 1))

                v.tensor_reduce(small[:, XM:XM + 1], x3[:], AX, ALU.add).then_inc(xm_sum.sem, 1)
                w(xm_sum(i, 1))
                v.tensor_scalar(small[:, XA:XA + 1], small[:, XM:XM + 1], 1.0 / HW, None, ALU.mult).then_inc(xm_ready.sem, 1)

            def softmax_max(i, n):
                w(pl_ready[n](i, 2))
                v.tensor_reduce(small[:, NMX + n:NMX + n + 1], pl[n][:], AX, ALU.max, negate=True).then_inc(pl_max[n].sem, 1)

            def attend(i, part, x=0):
                if part == "pool":
                    softmax_max(i, 0)
                    w(att.filled(i, ("avg",)))
                    v.tensor_copy(small[0:2 * CM, AVG:AVG + 1], att.tile(("avg",))[0:2 * CM, 0:1]).then_inc(avg_ready.sem, 1)
                if part == "theta":
                    w(att.filled(i, ("theta",)))
                    v.tensor_copy(small[:, U:U + 1], att.tile(("theta",))[:, 0:1]).then_inc(u_ready.sem, 1)
                    w(u_ready(i, 1))
                    v.tensor_scalar(ublk[:], const["oneb"][:], small[:, U:U + 1], None, ALU.mult).then_inc(ublk_ready.sem, 1)
                if part == "pixel":
                    w(pl_exp[0](i, 1))
                    v.tensor_tensor_reduce(out=lgt, in0=x3[:], in1=pl[0][:], scale=1.0, scalar=0.0,
                                           op0=ALU.mult, op1=ALU.add, accum_out=small[:, XS:XS + 1]).then_inc(xs_sum.sem, 1)
                    v.reciprocal(small[:, RCP:RCP + 1], small[:, SUM:SUM + 1]).then_inc(pl_rcp[0].sem, 1)
                    w(xs_sum(i, 1))
                    w(pl_rcp[0](i, 1))
                    v.tensor_tensor(small[:, XR:XR + 1], small[:, XS:XS + 1], small[:, RCP:RCP + 1],
                                    ALU.mult).then_inc(xs_ready.sem, 1)
                    softmax_max(i, 1)
                if part == "ctx":
                    w(att.filled(i, ("ctx",)))
                    v.tensor_copy(small[0:2 * CM, CTX:CTX + 1], att.tile(("ctx",))[0:2 * CM, 0:1]).then_inc(ctx_ready.sem, 1)
                    w(pl_exp[1](i, 1))
                    v.reciprocal(small[:, RCP + 1:RCP + 2], small[:, SUM + 1:SUM + 2]).then_inc(pl_rcp[1].sem, 1)
                    w(pl_rcp[1](i, 1))
                    v.tensor_scalar(pl[1][:], pl[1][:], small[:, RCP + 1:RCP + 2], None, ALU.mult).then_inc(pp_ready.sem, 1)
                if part == "scale":
                    w(sc_exp(i, 1))
                    v.tensor_scalar(small[:, SA:SA + 1], small[:, SE:SE + 1], 1.0, None, ALU.add).then_inc(sc_add.sem, 1)
                    w(sc_add(i, 1))
                    v.reciprocal(small[:, SR:SR + 1], small[:, SA:SA + 1]).then_inc(sc_ready.sem, 1)
                    w(sc_ready(i, 1))
                    v.tensor_scalar(xt[0][:], x3[:], small[:, SR:SR + 1], None, ALU.mult).then_inc(xt_ready.sem, 1)
                    w(pp_gate(i, 1))
                    v.tensor_tensor(xt[1][:], x3[:], pl[1][:], ALU.mult).then_inc(xt_ready.sem, 1)

                if part == "qkv":
                    for h in range(2):
                        item = ("q", x, h)
                        w(att.filled(i, item))
                        v.tensor_tensor(qs[:, 3 * h:3 * h + 3, :],
                                        att.tile(item)[:, 0:HALF].rearrange("p (g n) -> p g n", g=3),
                                        const["bq"][:].unsqueeze(1).broadcast_to([128, 3, GP]),
                                        ALU.add).then_inc(q_ready.sem, 1)
                    w(k_raw(i, x + 1))
                    v.tensor_tensor(ks[:], kraw[:].rearrange("p (g v) -> p g v", g=NG).unsqueeze(2).broadcast_to([128, NG, 4, W]),
                                    const["kblk"][:].unsqueeze(1).broadcast_to([128, NG, 4, W]),
                                    ALU.mult).then_inc(k_ready.sem, 1)
                flat = es[:].rearrange("p g b v -> p (g b) v")
                probs = pr[:].rearrange("p g b v -> p (g b) v")
                if part == "energy":
                    for h in range(2):
                        item = ("e", x, h)
                        w(att.filled(i, item))
                        v.tensor_tensor(es[:, 3 * h:3 * h + 3].rearrange("p g b v -> p g (b v)"),
                                        att.tile(item)[0:GP, 0:HALF].rearrange("p (g n) -> p g n", g=3),
                                        const["emask"][:].unsqueeze(1).broadcast_to([GP, 3, 4 * W]), ALU.add).then_inc(e_ready.sem, 1)
                    w(e_ready(i, 2 * x + 2))
                    v.tensor_reduce(st[:, 0, :], flat, AX, ALU.max).then_inc(e_max.sem, 1)
                    w(e_max(i, x + 1))
                    v.tensor_tensor(flat, flat, st[:, 0, :].unsqueeze(2).broadcast_to([GP, 4 * NG, W]),
                                    ALU.subtract).then_inc(e_sub.sem, 1)
                if part == "exp":
                    w(p_exp(i, x + 1))
                    v.tensor_reduce(st[:, 1, :], probs, AX, ALU.add).then_inc(p_sum.sem, 1)
                    w(p_sum(i, x + 1))
                    v.reciprocal(st[:, 4, :], st[:, 1, :]).then_inc(s_rcp.sem, 1)
                if part == "log":
                    w(s_log(i, x + 1))
                    v.tensor_tensor(st[:, 3, :], st[:, 0, :], st[:, 2, :], ALU.add).then_inc(lse_ready.sem, 1)
                    w(s_rcp(i, x + 1))
                    v.tensor_tensor(probs, probs, st[:, 4, :].unsqueeze(2).broadcast_to([GP, 4 * NG, W]),
                                    ALU.mult).then_inc(p_norm.sem, 1)
                    w(p_norm(i, x + 1))
                    v.tensor_tensor(pb[:, 0], by_image(pr, 0).unsqueeze(2).broadcast_to([GP, 2 * NG, G, W]),
                                    const["blk"][:].unsqueeze(1).broadcast_to([GP, 2 * NG, G, W]),
                                    ALU.mult).then_inc(pb_ready[0].sem, 1)
                if part == "lse":
                    w(att.filled(i, ("lse", x)))
                    v.tensor_tensor(lset[:], att.tile(("lse", x))[0:4 * NG, 0:GP].unsqueeze(1).broadcast_to([4 * NG, NG, GP]),
                                    const["gblk"][:].unsqueeze(2).broadcast_to([4 * NG, NG, GP]), ALU.mult).then_inc(lset_ready.sem, 1)
                if part == "gap":
                    for h in range(2):
                        item = ("d", x, h)
                        w(att.filled(i, item))
                        v.tensor_copy(gap[:, h * HALF:(h + 1) * HALF], att.tile(item)[:, 0:HALF]).then_inc(d_ready.sem, 1)
                if part == "turn":
                    for j in range(3):
                        item = ("p", x, 0, j)
                        w(att.filled(i, item))
                        v.tensor_copy(pt[:, 0, 4 * j:4 * j + 4, :],
                                      att.tile(item)[0:GP, 0:384].rearrange("p (g c) -> p g c", g=4)).then_inc(pt_ready[0].sem, 1)
                    w(g_step(i, 3 * x + 3))
                    v.scalar_tensor_tensor(out=share[:], in0=gap[:], scalar=0.0, in1=share[:],
                                           op0=ALU.min, op1=ALU.subtract).then_inc(g_log.sem, 1)
                if part == "mix":
                    w(o_ready(i, 4 * x + 4))
                    v.tensor_tensor(mix[:], ow[0][:], ow[1][:], ALU.subtract).then_inc(m_diff.sem, 1)
                    w(m_diff(i, x + 1))
                    w(g_ready(i, x + 1))
                    v.tensor_tensor(mix[:], mix[:], share[:], ALU.mult).then_inc(m_mul.sem, 1)
                    w(m_mul(i, x + 1))
                    v.tensor_tensor(mix[:], mix[:], ow[1][:], ALU.add).then_inc(m_add.sem, 1)
                    w(m_add(i, x + 1))
                    v.scalar_tensor_tensor(out=ares[x][:], in0=mix[:], scalar=const["gamma"][:, 0:1], in1=xt[x][:],
                                           op0=ALU.mult, op1=ALU.add).then_inc(a_ready.sem, 1)
                    if x == 1:
                        w(a_ready(i, 2))
                        v.tensor_tensor(xt[2][:], ares[0][:], ares[1][:], ALU.add).then_inc(xt_ready.sem, 1)

            run(dve, convolve, attend)

        @block.tensor
        def _(pe):
            mm = nc.tensor.matmul

            def w(pair):
                pe.wait_ge(*pair)

            w((other_borders, 5))
            w((first_loaded, 16 * n_first))

            wide_runs = pe.alloc_register("wide_runs_pe")
            pe.reg_mov(wide_runs, 0)

            def conv(i, item, weights, src, m, inputs):
                w(work.may_fill(i, item))
                for h in range(2):
                    w(inputs[h])
                    for k in range(TAPS):
                        r = k // 3 + h * HR
                        last = mm(work.tile(item)[0:m, h, 0:HALF], weights[:, k, :],
                                  src[:, r:r + HR, k % 3:k % 3 + W], start=(k == 0), stop=(k == TAPS - 1))
                    if h == 0:
                        last.then_inc(first_half.sem, 1)
                last.then_inc(work.full_sem(item), 1)

            def spread_x(i, l, s, k):
                item = ("hx", l, s, k)
                t = k // T0
                n = TILE_ROWS[t]
                w(hatx_lo(i, (l * 2 + s) * 2 + t + 1))
                w(work.may_fill(i, item))
                for h in range(2):
                    for part in range(2):
                        last = mm(work.tile(item)[0:120, h, 0:HALF], selx[0:n, k, :],
                                  hatx[s][t][part][0:n, h * HALF:(h + 1) * HALF],
                                  start=(part == 0), stop=(part == 1))
                last.then_inc(work.full_sem(item), 1)

            def spread_y(s, g, reach, slot):
                ky, c, (r0, r1) = groups(reach)[g]
                n = (r1 - r0) * W
                m = chunk_rows(c) * W
                slot = slot.rearrange("p b n -> p (b n)")
                for q in range(3):
                    t, kl = divmod(3 * ky + q, T0)
                    first = (kl * H + c * CR) * W
                    for part in range(2):
                        last = mm(slot[0:m, q * SEG:q * SEG + n], sele[0:TILE_ROWS[t], first:first + m],
                                  haty[s][t][part][0:TILE_ROWS[t], r0 * W:r1 * W],
                                  start=(part == 0), stop=(part == 1), skip_group_check=True)
                return last

            def add_up(g, reach):
                ky, c, (r0, r1) = groups(reach)[g]
                m = chunk_rows(c) * W
                for q in range(3):
                    k = 3 * ky + q
                    for bank, c0, a0, a1 in y_pieces(r0, r1):
                        for s in range(2):
                            last = mm(ysum[s * C:(s + 1) * C, bank, c0:c0 + (a1 - a0) * W],
                                      zt[s][0:m, c, k * C:(k + 1) * C],
                                      prod[s][g % 2][0:m, q, (a0 - r0) * W:(a1 - r0) * W],
                                      start=False, stop=True, skip_group_check=True)
                return last

            def keep_clock(n):
                for _ in range(n):
                    mm(ysum[:, 1, 128:512], zero16[:, 0:128], zero16[:, 0:384], start=True, stop=True)

            def convolve(i, between):
                for l in range(2):
                    conv(i, ("offsets", l), woff[:, l], xpad[l], 96,
                         [x_padded(i, 1)] * 2 if l == 0 else [x1_padded(i, 1), x1_padded(i, 2)])
                    if l == 0:
                        w((loaded, 16 * n_const))
                    between(l * STEPS_PER_LAYER)
                    for kind, s, t in preparation(between, l, "zyxm"):
                        item = (kind, l, s, t)
                        if kind == "z":
                            n = chunk_rows(t) * W
                            weights = wdcn[s * C:(s + 1) * C, l]
                            pixels = xin[s * C:(s + 1) * C, t * CR * W:t * CR * W + n]
                            if l == 1:
                                w(y_read(i, 2))
                            w(work.may_fill(i, item))
                            for h in range(2):
                                last = mm(work.tile(item)[0:n, h, 0:HALF], pixels,
                                          weights[:, h * HALF:(h + 1) * HALF], start=True, stop=True)
                        else:
                            n = TILE_ROWS[t]
                            w((mask_lo if kind == "m" else coords_ready)(i, l + 1))
                            src, first = (mask16, 64) if kind == "m" else (off16, 0)
                            w(work.may_fill(i, item))
                            for h in range(2):
                                last = mm(work.tile(item)[0:n, h, 0:HALF], selp[first:128, s, t, "yxm".index(kind), 0:n],
                                          src[first:128, h * HALF:(h + 1) * HALF], start=True, stop=True)
                        last.then_inc(work.full_sem(item), 1)
                        keep_clock(2)
                    w(y_read(i, 2 * l))
                    mm(ysum[:, 0, 0:Y_ROWS * W], zero16[:, 0:128], zero16[:, 0:Y_ROWS * W], start=True, stop=True)
                    mm(ysum[:, 1, 0:(H - Y_ROWS) * W], zero16[:, 0:128], zero16[:, 0:(H - Y_ROWS) * W], start=True, stop=True)
                    for s, k in x_after(-1):
                        spread_x(i, l, s, k)
                    w(haty_lo(i, l * 4 + 4))
                    for s in range(2):
                        w(z_ready[s](i, (l + 1) * CHUNKS))
                    w(reach_flag(i, l + 1))
                    pe.nop(nofuse=True)
                    is_wide = pe.value_load(wide[0:1, l:l + 1], min_val=0, max_val=1)
                    with pe.If(is_wide != 0):
                        runs = pe.snap(wide_runs)
                        steps = groups(WIDE)
                        for g, (ky, c, _) in enumerate(steps):
                            if g == 0 or steps[g - 1][0] != ky:
                                between(step_sum(l, ky, -1))
                                for s in range(2):
                                    w(work.may_fill(i, ("hy", l, s, ky * per_row)))
                            if g > 0:
                                w((wide_ready, runs * n_wide + 2 * g))
                            else:
                                for s in range(2):
                                    w(work.emptied(i, ("hx", l, s, 2)))
                            for s in range(2):
                                spread_y(s, g, WIDE, work.tile(("hy", l, s, 0))).then_inc(wide_full, 1)
                            w((wide_ready, runs * n_wide + 2 * g + 2))
                            last = add_up(g, WIDE)
                            if g == len(steps) - 1:
                                last.then_inc(y_summed.sem, 1)
                            if g + 1 == len(steps) or steps[g + 1][1] != c:
                                for full in work.full:
                                    pe.sem_inc(full.sem, 1)
                                for s, k in x_after(ky, c):
                                    spread_x(i, l, s, k)
                                for s, k in x_after(ky, c):
                                    w(work.emptied(i, ("hx", l, s, k)))
                                between(step_sum(l, ky, c))
                        pe.sem_inc(prod_used.sem, n_groups - 1)
                        pe.reg_add(wide_runs, wide_runs, 1)
                    with pe.Else():
                        steps = groups(REACH[l])
                        for g in range(n_groups + 1):
                            if g < n_groups:
                                ky, c, _ = steps[g]
                                if c == 0:
                                    between(step_sum(l, ky, -1))
                                for s in range(2):
                                    item = ("hy", l, s, g)
                                    w(work.may_fill(i, item))
                                    spread_y(s, g, REACH[l], work.tile(item)).then_inc(work.full_sem(item), 1)
                            if g > 0:
                                for s in range(2):
                                    w(prod_ready[s](i, l * n_groups + g))
                                add_up(g - 1, REACH[l]).then_inc((prod_used if g < n_groups else y_summed).sem, 1)
                            if g < n_groups:
                                for s, k in x_after(ky, c):
                                    spread_x(i, l, s, k)
                                between(step_sum(l, ky, c))

                w(x2_ready(i, 1))
                w(work.may_fill(i, ("gate",)))
                for h in range(2):
                    last = mm(work.tile(("gate",))[:, h, 0:HALF], const["wm"][:],
                              xpad[2][:, 1 + h * HR:1 + (h + 1) * HR, 1:W + 1], start=True, stop=True)
                last.then_inc(work.full_sem(("gate",)), 1)
                conv(i, ("conv1",), const["w1"], xpad[2], 128, [x2_ready(i, 1)] * 2)
                conv(i, ("conv2",), const["w2"], hpad, 128, [h_ready(i, 2)] * 2)

            def one(i, item, lhsT, rhs, m):
                w(att.may_fill(i, item))
                mm(att.tile(item)[0:m, 0:rhs.shape[-1]], lhsT, rhs, start=True, stop=True).then_inc(att.full_sem(item), 1)

            def attend(i, part, x=0):
                if part == "pool":
                    w(x3_ready(i, 1))
                    for h in range(2):
                        one(i, ("pool_logits", h), const["wqr"][:], x3[:, h * HALF:(h + 1) * HALF], 128)
                    w(xm_ready(i, 1))
                    one(i, ("avg",), const["wql"][:], small[:, XA:XA + 1], 2 * CM)
                if part == "theta":
                    w(avg_ready(i, 1))
                    one(i, ("theta",), const["wvl"][:], small[0:2 * CM, AVG:AVG + 1], 128)
                if part == "pixel":
                    w(ublk_ready(i, 1))
                    for h in range(2):
                        one(i, ("pixel_logits", h), ublk[:], x3[:, h * HALF:(h + 1) * HALF], 128)
                if part == "ctx":
                    w(xs_ready(i, 1))
                    one(i, ("ctx",), const["wvr"][:], small[:, XR:XR + 1], 2 * CM)
                if part == "scale":
                    w(ctx_ready(i, 1))
                    one(i, ("scale",), const["wup"][:], small[0:2 * CM, CTX:CTX + 1], 128)
                if part == "qkv":
                    src = xt[x][:]
                    views = (src.rearrange("p (g r n) -> p g r n", r=G, n=W),
                             src.rearrange("p (n g r) -> p g r n", r=G, g=NG))
                    w(xt_ready(i, x + 1))
                    for h in range(2):
                        item = ("q", x, h)
                        w(att.may_fill(i, item))
                        for r in range(G):
                            for d in range(2):
                                dst = att.tile(item)[64 * d:64 * d + 64, 0:HALF].rearrange("p (g r n) -> p g r n", g=3, r=G)
                                last = mm(dst[:, :, r, :], const["wq"][:, r, :], views[d][:, 3 * h:3 * h + 3, r, :],
                                          start=True, stop=True, skip_group_check=True)
                        last.then_inc(att.full_sem(item), 1)
                    item = ("k", x)
                    w(att.may_fill(i, item))
                    for r in range(G):
                        for d in range(2):
                            last = mm(att.tile(item)[64 * d:64 * d + 64, 0:NG * W].rearrange("p (g n) -> p g n", g=NG),
                                      const["wk"][:, r, :], views[d][:, :, r, :], start=(r == 0), stop=(r == G - 1),
                                      skip_group_check=True)
                    last.then_inc(att.full_sem(item), 1)
                    w(xcol_ready(i, x + 1))
                    for d, h in dh:
                        item = ("v", x, d, h)
                        w(att.may_fill(i, item))
                        for g in range(3):
                            last = mm(att.tile(item)[0:GP, g * 128:(g + 1) * 128], (src, xcol)[d][:, (3 * h + g) * GP:(3 * h + g + 1) * GP], const["wv"][:],
                                      start=True, stop=True, skip_group_check=True)
                        last.then_inc(att.full_sem(item), 1)
                if part == "energy":
                    w(q_ready(i, 2 * x + 2))
                    w(k_ready(i, x + 1))
                    for h in range(2):
                        item = ("e", x, h)
                        w(att.may_fill(i, item))
                        for g in range(3):
                            last = mm(att.tile(item)[0:GP, g * 4 * W:(g + 1) * 4 * W], qs[:, 3 * h + g, :],
                                      ks[:, 3 * h + g].rearrange("p b v -> p (b v)"), start=True, stop=True, skip_group_check=True)
                        last.then_inc(att.full_sem(item), 1)
                if part == "lse":
                    item = ("lse", x)
                    w(lse_ready(i, x + 1))
                    w(att.may_fill(i, item))
                    nc.tensor.transpose(att.tile(item)[0:4 * NG, 0:GP], st[:, 3, :], const["ident"][:]).then_inc(att.full_sem(item), 1)
                if part == "gap":
                    w(lset_ready(i, x + 1))
                    for h in range(2):
                        item = ("d", x, h)
                        w(att.may_fill(i, item))
                        sums = att.tile(item)[:, 0:HALF]
                        mm(sums, const["pick"][:, 0, :], lset[:, 3 * h:3 * h + 3].rearrange("p g n -> p (g n)"),
                           start=True, stop=False)
                        last = mm(sums, const["pick"][:, 1, :],
                                  lset[:].rearrange("p g (r n) -> p n g r", r=G)[:, h * HR:(h + 1) * HR],
                                  start=False, stop=True)
                        last.then_inc(att.full_sem(item), 1)
                if part == "turn":
                    for s in range(2):
                        w(pb_ready[s](i, x + 1))
                        for j in range(3):
                            item = ("p", x, s, j)
                            w(att.may_fill(i, item))
                            for q in range(4):
                                last = nc.tensor.transpose(att.tile(item)[0:GP, q * GP:(q + 1) * GP],
                                                           pb[:, s, 4 * j + q].rearrange("p r v -> p (r v)"), const["ident"][:])
                            last.then_inc(att.full_sem(item), 1)
                if part == "out":
                    w(v_ready(i, 4 * x + 4))
                    for s in range(2):
                        w(pt_ready[s](i, 3 * x + 3))
                    for d, h in dh:
                        item = ("o", x, d, h)
                        w(att.may_fill(i, item))
                        for g in range(3):
                            for s in range(2):
                                j = 3 * h + g
                                last = mm(att.tile(item)[s * C:(s + 1) * C, g * GP:(g + 1) * GP],
                                          vs[:, d, j, s * C:(s + 1) * C], pt[:, s, 2 * j + d, :],
                                          start=True, stop=True, skip_group_check=True)
                        last.then_inc(att.full_sem(item), 1)

            run(pe, convolve, attend)


def diagonal(blocks, rows, cols):
    out = np.zeros((2 * rows,) + blocks.shape[1:-1] + (2 * cols,), np.float32)
    out[:rows, ..., :cols] = blocks
    out[rows:, ..., cols:] = blocks
    return out


def twice(v):
    return np.concatenate([v, v])[:, None]


def offset_layout(w):
    out = np.zeros((2, C, TAPS, 96), np.float32)
    t = w.reshape(27, C, TAPS).transpose(1, 2, 0)
    for s in range(2):
        for block, part in enumerate((t[..., 0:18:2], t[..., 1:18:2], t[..., 18:27])):
            out[s, :, :, 32 * block + 9 * s:32 * block + 9 * s + 9] = part
    return out.reshape(2 * C, TAPS, 96)


def offset_bias(b):
    out = np.zeros(96, np.float32)
    for s in range(2):
        for block, part in enumerate((b[0:18:2], b[1:18:2], b[18:27])):
            out[32 * block + 9 * s:32 * block + 9 * s + 9] = part
    return out


def group_weights(w):
    out = np.zeros((2, C, G, 2, G, CQ), np.float32)
    for s in range(2):
        for r in range(G):
            out[s, :, r, s, r, :] = w.T
    return out.reshape(2 * C, G, 2 * G * CQ)


def shape_constants():
    one, number = 32 + 2 * TAPS, {0: 33 + 2 * TAPS, 1: 34 + 2 * TAPS}
    grid = np.zeros((96, H, W), np.float32)
    grid[one] = 1.0
    grid[number[0]] = np.arange(H)[:, None]
    grid[number[1]] = np.arange(W)[None, :]
    selp = np.zeros((128, 2, 2, 3, 120), np.float16)
    sele = np.zeros((120, 120, W), np.float16)
    for q in range(120):
        sele[q, q] = 1.0 / SCALE16
    selx = np.zeros((120, TAPS, 120), np.float16)
    for k in range(TAPS):
        t, kl = (0, k) if k < T0 else (1, k - T0)
        for s in range(2):
            rows = slice(kl * H, (kl + 1) * H)
            for kind, shift in enumerate((k // 3 - 1, k % 3 - 1)):
                selp[32 * kind + 9 * s + k, s, t, kind, rows] = 1.0
                selp[64 + 32 * kind + 9 * s + k, s, t, kind, rows] = 1.0
                selp[number[kind], s, t, kind, rows] = 1.0
                selp[one, s, t, kind, rows] = shift - np.arange(H)
            selp[64 + 9 * s + k, s, t, 2, rows] = 1.0 / MASK_SCALE
            selp[96 + 9 * s + k, s, t, 2, rows] = 1.0 / MASK_SCALE
        for q in range(24):
            selx[kl * 24 + q, k, q::24] = 1.0 / SCALE16
    bounds = np.empty((96, 2), np.float32)
    bounds[0:64] = -OFFSET_MAX, OFFSET_MAX
    bounds[64:96] = LOGIT_MIN, LOGIT_MAX
    emask = np.zeros((G, H, 2, 2, W), np.float32)
    blk = np.zeros((G, W, G, W), np.float32)
    for n in range(24):
        emask[:, n, 1, :, n] = MASKED
    for r in range(G):
        blk[r, :, r, :] = 1.0
    pick = np.zeros((NG, 2, 2, 2, 2, C), np.float32)
    kblk = np.zeros((2, 2, G * CQ, 2, 2, W), np.float32)
    for s in range(2):
        for d in range(2):
            pick[:, d, s, d, s, :] = 1 - 2 * d
            kblk[d, s, :, d, s, :] = 1.0
    gblk = np.repeat(np.eye(NG, dtype=np.float32), 4, axis=0)
    oneb = np.zeros((2, C, 2, C), np.float32)
    for s in range(2):
        oneb[s, :, s, :] = 1.0
    return {
        "grid": grid.reshape(96, HW), "bounds": bounds, "unit": np.full((120, 1), SCALE16, np.float32), "selp": selp,
        "sele": sele.reshape(120, 120 * W), "selx": selx,
        "emask": emask.reshape(GP, 4 * W), "blk": blk.reshape(GP, G, W), "ident": np.eye(GP, dtype=np.float32),
        "pick": pick.reshape(4 * NG, 2, 128), "kblk": kblk.reshape(128, 4, W), "gblk": gblk, "oneb": oneb.reshape(128, 128),
    }


def kernel(**inputs):
    import concourse.bacc as bacc
    from concourse.bass_utils import run_bass_kernel_spmd

    p = {n: np.asarray(v) for n, v in inputs.items()}

    def norm(l, names):
        return np.stack([np.concatenate([p[f"L{l}_conv_{n}"]] * 2) for n in names], axis=1)

    def spread(v):
        return diagonal(np.broadcast_to(v.reshape(C, 1), (C, C)), C, C)

    bq = np.zeros((2, G, CQ, G, W), np.float32)
    for r in range(G):
        bq[:, r, :, r, :] = p["L3_conv_cr_bq"][None, :, None]
    wd = [p[n].reshape(C, C, TAPS).transpose(1, 2, 0).reshape(C, TAPS * C) for n in ("L0_conv_w_dcn", "L1_conv_w_conv")]
    taps = {n: p[f"L2_conv_{n}"].reshape(C, C, TAPS).transpose(1, 2, 0) for n in ("w1", "w2")}
    arrays = {
        "x": p["x"].reshape(PAIRS, 2 * C, HW),
        "woff": np.stack([offset_layout(p[f"L{l}_conv_w_off"]) for l in range(2)], axis=1),
        "boff": np.stack([offset_bias(p[f"L{l}_conv_b_off"]) for l in range(2)], axis=1),
        "wdcn": np.stack([np.concatenate([w, w]) for w in wd], axis=1),
        "bn": np.stack([norm(0, ("b_dcn", "gamma", "beta", "running_mean", "running_var")),
                        norm(1, ("b_conv", "gamma", "beta", "run_mean", "run_var"))], axis=1),
        "w1": diagonal(taps["w1"], C, C), "w2": diagonal(taps["w2"], C, C),
        "wm": spread(p["L2_conv_w_mask"]), "bm": np.broadcast_to(p["L2_conv_b_mask"].reshape(1, 1), (128, 1)),
        "wqr": spread(p["L3_conv_w_q_right"]),
        "wvr": diagonal(p["L3_conv_w_v_right"].T, C, CM), "wup": diagonal(p["L3_conv_w_up"].T, CM, C),
        "bup": twice(p["L3_conv_b_up"]),
        "wql": diagonal(p["L3_conv_w_q_left"].T, C, CM), "wvl": diagonal(p["L3_conv_w_v_left"], CM, C),
        "wq": group_weights(p["L3_conv_cr_wq"]), "wk": group_weights(p["L3_conv_cr_wk"]),
        "bq": np.tile(bq.reshape(2 * G * CQ, GP), (2, 1)), "bk": np.tile(p["L3_conv_cr_bk"], 4 * G)[:, None],
        "wv": diagonal(p["L3_conv_cr_wv"].T, C, C), "bv": twice(p["L3_conv_cr_bv"]),
        "gamma": np.broadcast_to(p["L3_conv_gamma"].reshape(1, 1), (128, 1)),
        **shape_constants(),
    }
    arrays = {n: np.ascontiguousarray(v) for n, v in arrays.items()}

    nc = bacc.Bacc("TRN2", target_bir_lowering=False, num_devices=1)
    args = {n: nc.dram_tensor(n, v.shape, mybir.dt.from_np(v.dtype), kind="ExternalInput").ap() for n, v in arrays.items()}
    out = nc.dram_tensor("out", (PAIRS, 2 * C, HW), F32, kind="ExternalOutput").ap()
    build(nc, args, out)
    r = run_bass_kernel_spmd(nc, [arrays], core_ids=[0])
    return r.results[0]["out"].reshape(B, C, H, W)
```
